# Optimizing a Trainium2 kernel written in Bass

```python
import numpy as np
import jax
import jax.numpy as jnp

def _softmax(x, axis=-1):
    return jax.nn.softmax(x, axis=axis)

def _gelu(x):
    return jax.nn.gelu(x, approximate=True)

def _silu(x):
    return jax.nn.silu(x)

def _sigmoid(x):
    return jax.nn.sigmoid(x)

def _layernorm(x, axis=-1, eps=1e-05):
    m = jnp.mean(x, axis=axis, keepdims=True)
    v = jnp.var(x, axis=axis, keepdims=True)
    return (x - m) / jnp.sqrt(v + eps)

def _scatter_add(tgt, idx, src, axis=0):
    return tgt.at[idx].add(src)

def _segment_sum(src, seg, n):
    return jax.ops.segment_sum(src, seg, n)
kernel_name = 'mk_flamingo_gated_d2_seqx_r8_f777ac'

def setup_inputs(seed: int=0):
    np.random.seed(seed)
    _w = jnp.asarray

    def _rec_inputs():
        import jax
        import jax.numpy as jnp
        _rk = jax.random.key(seed)
        x = -0.0002928 + 1 * jax.random.normal(jax.random.fold_in(_rk, 1), (32, 128, 128), jnp.float32)
        _lenS = 128 - jax.random.randint(jax.random.fold_in(_rk, 7), (32,), 0, max(1, 128 // 4) + 1, jnp.int32)
        _lenS2 = 120 - jax.random.randint(jax.random.fold_in(_rk, 8), (32,), 0, max(1, 120 // 4) + 1, jnp.int32)
        _ctx_1024P = jax.random.normal(jax.random.fold_in(_rk, 11), (32, 16, 128), jnp.float32)
        _ctx_1024c = jax.random.dirichlet(jax.random.fold_in(_rk, 511), 0.3 * jnp.ones((16,), jnp.float32), (32, 120))
        _ctx_1024t = jnp.einsum('bsk,bkd->bsd', _ctx_1024c, _ctx_1024P)
        _ctx_1024t = _ctx_1024t * jax.lax.rsqrt(jnp.mean(jnp.square(_ctx_1024t)) + 1e-12) * 0.953939
        ctx_1024 = -1.39393e-06 + 0.999914 * (_ctx_1024t + 0.3 * jax.random.normal(jax.random.fold_in(_rk, 611), (32, 120, 128), jnp.float32))
        fside_BxSxS2_0 = jax.random.uniform(jax.random.fold_in(_rk, 12), (32, 128, 120), jnp.float32, 0.0, 1)
        _validS = jnp.arange(128)[None, :] < _lenS[:, None]
        _validS2 = jnp.arange(120)[None, :] < _lenS2[:, None]
        _causal = jnp.tril(jnp.ones((128, 128), dtype=bool))
        mask_BxSxS2_ik1 = jnp.where(jnp.broadcast_to(_validS2[:, None, :], (32, 128, 120)), 1, 0).astype(jnp.int32)
        mask_1x1xSxS2_bk1 = jnp.broadcast_to(_validS2[0:1, None, None, :], (1, 1, 128, 120))
        _g = jax.random.normal(jax.random.fold_in(_rk, 9001), (2, 2), jnp.float32)
        _g = jnp.sign(_g) * jnp.maximum(jnp.abs(_g), 1.0) + (_g == 0) * 1.0
        g_xattn = _g[0]
        g_ffn = _g[1]
        return (x, ctx_1024, fside_BxSxS2_0, mask_BxSxS2_ik1, mask_1x1xSxS2_bk1, g_xattn, g_ffn)
    x, ctx_1024, fside_BxSxS2_0, mask_BxSxS2_ik1, mask_1x1xSxS2_bk1, g_xattn, g_ffn = _rec_inputs()

    def _L0_xattn_setup():
        import jax, jax.numpy as jnp
        import numpy as np
        NUM_HEADS = 16
        HIDDEN = 128
        B, S = (2, 256)

        def _split_heads(x, H):
            b, s, d = x.shape
            return x.reshape(b, s, H, d // H).transpose(0, 2, 1, 3)
        key = jax.random.key(seed)
        ks = jax.random.split(key, 14)
        D = HIDDEN
        scale = 1.0 / np.sqrt(D)
        inp = {'query': jax.random.normal(ks[0], (B, S, D), jnp.float32), 'key_in': jax.random.normal(ks[1], (B, S, D), jnp.float32), 'value': jax.random.normal(ks[2], (B, S, D), jnp.float32), 'group_prob': jax.random.uniform(ks[3], (B, S, S), jnp.float32), 'mask': jax.random.randint(ks[4], (B, S, S), 0, 2, jnp.int32), 'wq_k': jax.random.normal(ks[5], (D, D), jnp.float32) * scale, 'wq_b': jnp.zeros((D,), jnp.float32), 'wk_k': jax.random.normal(ks[6], (D, D), jnp.float32) * scale, 'wk_b': jnp.zeros((D,), jnp.float32), 'wv_k': jax.random.normal(ks[7], (D, D), jnp.float32) * scale, 'wv_b': jnp.zeros((D,), jnp.float32), 'wo_k': jax.random.normal(ks[8], (D, D), jnp.float32) * scale, 'wo_b': jnp.zeros((D,), jnp.float32)}
        return inp
    _L0_xattn_all = _L0_xattn_setup()
    _L0_xattn_in = {k: v for k, v in _L0_xattn_all.items() if k in ('wq_k', 'wq_b', 'wk_k', 'wk_b', 'wv_k', 'wv_b', 'wo_k', 'wo_b')}
    del _L0_xattn_all

    def _L0_ffn_setup():
        import math
        import jax, jax.numpy as jnp
        import numpy as np
        B, S, D, H, E, K = (4, 256, 128, 512, 8, 2)
        CAPACITY_RATIO = 1.05
        key = jax.random.key(seed)
        k0, k1, k2, k3 = jax.random.split(key, 4)
        x = jax.random.normal(k0, (B, S, D), jnp.float32)
        Wg = jax.random.normal(k1, (D, E), jnp.float32) * 0.02
        W1 = jax.random.normal(k2, (E, D, H), jnp.float32) * 0.02
        b1 = jnp.zeros((E, H), jnp.float32)
        W2 = jax.random.normal(k3, (E, H, D), jnp.float32) * 0.02
        b2 = jnp.zeros((E, D), jnp.float32)
        return {'x': x, 'Wg': Wg, 'W1': W1, 'b1': b1, 'W2': W2, 'b2': b2}
    _L0_ffn_all = _L0_ffn_setup()
    _L0_ffn_in = {k: v for k, v in _L0_ffn_all.items() if k in ('Wg', 'W1', 'b1', 'W2', 'b2')}
    del _L0_ffn_all

    def _L1_xattn_setup():
        import jax, jax.numpy as jnp
        import numpy as np
        D_MODEL = 128
        NUM_HEADS = 16
        D_K = D_MODEL // NUM_HEADS
        B, S = (2, 256)
        NEG = -1000000000.0

        def _split_heads(x):
            b, s, _ = x.shape
            return x.reshape(b, s, NUM_HEADS, D_K).transpose(0, 2, 1, 3)
        key = jax.random.key(seed)
        ks = jax.random.split(key, 12)
        sc = 1.0 / np.sqrt(D_MODEL)
        inp = {'q': jax.random.normal(ks[0], (B, S, D_MODEL), jnp.float32), 'k': jax.random.normal(ks[1], (B, S, D_MODEL), jnp.float32), 'v': jax.random.normal(ks[2], (B, S, D_MODEL), jnp.float32), 'mask': jnp.triu(jnp.ones((S, S), bool), k=1)[None, None], 'w_q': jax.random.normal(ks[3], (D_MODEL, D_MODEL), jnp.float32) * sc, 'b_q': jnp.zeros((D_MODEL,), jnp.float32), 'w_k': jax.random.normal(ks[4], (D_MODEL, D_MODEL), jnp.float32) * sc, 'b_k': jnp.zeros((D_MODEL,), jnp.float32), 'w_v': jax.random.normal(ks[5], (D_MODEL, D_MODEL), jnp.float32) * sc, 'b_v': jnp.zeros((D_MODEL,), jnp.float32), 'w_o': jax.random.normal(ks[6], (D_MODEL, D_MODEL), jnp.float32) * sc, 'b_o': jnp.zeros((D_MODEL,), jnp.float32)}
        return inp
    _L1_xattn_all = _L1_xattn_setup()
    _L1_xattn_in = {k: v for k, v in _L1_xattn_all.items() if k in ('w_q', 'b_q', 'w_k', 'b_k', 'w_v', 'b_v', 'w_o', 'b_o')}
    del _L1_xattn_all

    def _L1_ffn_setup():
        import jax, jax.numpy as jnp
        import numpy as np
        TOP_K = 2
        EPS = 1e-09
        key = jax.random.key(seed)
        ks = jax.random.split(key, 6)
        B, T, D, H, E = (4, 256, 128, 256, 8)
        x = jax.random.normal(ks[0], (B, T, D), dtype=jnp.float32)
        Wg = jax.random.normal(ks[1], (E, D), dtype=jnp.float32) * 0.02
        W1 = jax.random.normal(ks[2], (E, 2 * H, D), dtype=jnp.float32) * 0.02
        b1 = jax.random.normal(ks[3], (E, 2 * H), dtype=jnp.float32) * 0.02
        Wo = jax.random.normal(ks[4], (D, H), dtype=jnp.float32) * 0.02
        bo = jax.random.normal(ks[5], (D,), dtype=jnp.float32) * 0.02
        return {'x': x, 'Wg': Wg, 'W1': W1, 'b1': b1, 'Wo': Wo, 'bo': bo}
    _L1_ffn_all = _L1_ffn_setup()
    _L1_ffn_in = {k: v for k, v in _L1_ffn_all.items() if k in ('Wg', 'W1', 'b1', 'Wo', 'bo')}
    del _L1_ffn_all
    return {'x': x, 'ctx_1024': ctx_1024, 'fside_BxSxS2_0': fside_BxSxS2_0, 'mask_BxSxS2_ik1': mask_BxSxS2_ik1, 'mask_1x1xSxS2_bk1': mask_1x1xSxS2_bk1, 'g_xattn': g_xattn, 'g_ffn': g_ffn, 'L0_xattn_wq_k': _L0_xattn_in['wq_k'], 'L0_xattn_wq_b': _L0_xattn_in['wq_b'], 'L0_xattn_wk_k': _L0_xattn_in['wk_k'], 'L0_xattn_wk_b': _L0_xattn_in['wk_b'], 'L0_xattn_wv_k': _L0_xattn_in['wv_k'], 'L0_xattn_wv_b': _L0_xattn_in['wv_b'], 'L0_xattn_wo_k': _L0_xattn_in['wo_k'], 'L0_xattn_wo_b': _L0_xattn_in['wo_b'], 'L0_ffn_Wg': _L0_ffn_in['Wg'], 'L0_ffn_W1': _L0_ffn_in['W1'], 'L0_ffn_b1': _L0_ffn_in['b1'], 'L0_ffn_W2': _L0_ffn_in['W2'], 'L0_ffn_b2': _L0_ffn_in['b2'], 'L1_xattn_w_q': _L1_xattn_in['w_q'], 'L1_xattn_b_q': _L1_xattn_in['b_q'], 'L1_xattn_w_k': _L1_xattn_in['w_k'], 'L1_xattn_b_k': _L1_xattn_in['b_k'], 'L1_xattn_w_v': _L1_xattn_in['w_v'], 'L1_xattn_b_v': _L1_xattn_in['b_v'], 'L1_xattn_w_o': _L1_xattn_in['w_o'], 'L1_xattn_b_o': _L1_xattn_in['b_o'], 'L1_ffn_Wg': _L1_ffn_in['Wg'], 'L1_ffn_W1': _L1_ffn_in['W1'], 'L1_ffn_b1': _L1_ffn_in['b1'], 'L1_ffn_Wo': _L1_ffn_in['Wo'], 'L1_ffn_bo': _L1_ffn_in['bo']}

def reference(x, ctx_1024, fside_BxSxS2_0, mask_BxSxS2_ik1, mask_1x1xSxS2_bk1, g_xattn, g_ffn, L0_xattn_wq_k, L0_xattn_wq_b, L0_xattn_wk_k, L0_xattn_wk_b, L0_xattn_wv_k, L0_xattn_wv_b, L0_xattn_wo_k, L0_xattn_wo_b, L0_ffn_Wg, L0_ffn_W1, L0_ffn_b1, L0_ffn_W2, L0_ffn_b2, L1_xattn_w_q, L1_xattn_b_q, L1_xattn_w_k, L1_xattn_b_k, L1_xattn_w_v, L1_xattn_b_v, L1_xattn_w_o, L1_xattn_b_o, L1_ffn_Wg, L1_ffn_W1, L1_ffn_b1, L1_ffn_Wo, L1_ffn_bo):
    import jax
    import jax.numpy as jnp

    def _L0_xattn_ref(query, key_in, value, group_prob, mask, wq_k, wq_b, wk_k, wk_b, wv_k, wv_b, wo_k, wo_b):
        import jax, jax.numpy as jnp
        import numpy as np
        NUM_HEADS = 16
        HIDDEN = 128
        B, S = (2, 256)

        def _split_heads(x, H):
            b, s, d = x.shape
            return x.reshape(b, s, H, d // H).transpose(0, 2, 1, 3)
        H = NUM_HEADS
        dh = query.shape[-1] // H
        q = _split_heads(query @ wq_k + wq_b, H)
        k = _split_heads(key_in @ wk_k + wk_b, H)
        v = _split_heads(value @ wv_k + wv_b, H)
        logits = jnp.einsum('bhqd,bhkd->bhqk', q, k) / jnp.sqrt(jnp.asarray(dh, q.dtype))
        neg = (1.0 - mask.astype(q.dtype)) * -1000000000.0
        logits = logits + neg[:, None, :, :]
        attn = jax.nn.softmax(logits, axis=-1)
        attn = attn * group_prob[:, None, :, :]
        out = jnp.einsum('bhqk,bhkd->bhqd', attn, v)
        out = out.transpose(0, 2, 1, 3).reshape(query.shape[0], -1, H * dh)
        return out @ wo_k + wo_b

    def _L0_ffn_ref(x, Wg, W1, b1, W2, b2):
        import math
        import jax, jax.numpy as jnp
        import numpy as np
        B, S, D, H, E, K = (4, 256, 128, 512, 8, 2)
        CAPACITY_RATIO = 1.05
        b, s, d = x.shape
        e = Wg.shape[1]
        n = b * s
        cap = int(math.ceil(n * K / e * CAPACITY_RATIO))
        xf = x.reshape(n, d)
        probs = jax.nn.softmax(xf @ Wg, axis=-1)
        topv, topi = jax.lax.top_k(probs, K)
        gates = topv / jnp.sum(topv, axis=-1, keepdims=True)
        eidx = topi.reshape(-1)
        oh = jax.nn.one_hot(eidx, e, dtype=jnp.int32)
        pos = jnp.sum(jnp.cumsum(oh, axis=0) * oh, axis=-1) - 1
        keep = pos < cap
        dest = jnp.where(keep, eidx * cap + pos, e * cap)
        xr = jnp.repeat(xf, K, axis=0)
        buf = jnp.zeros((e * cap + 1, d), x.dtype).at[dest].set(xr)
        expert_in = buf[:e * cap].reshape(e, cap, d)
        h = jax.nn.gelu(jnp.einsum('ecd,edh->ech', expert_in, W1) + b1[:, None, :])
        y = jnp.einsum('ech,ehd->ecd', h, W2) + b2[:, None, :]
        yf = jnp.concatenate([y.reshape(e * cap, d), jnp.zeros((1, d), y.dtype)], axis=0)
        gathered = yf[dest]
        w = (gates.reshape(-1) * keep.astype(gates.dtype))[:, None]
        out = (gathered * w).reshape(n, K, d).sum(axis=1).reshape(b, s, d)
        return out

    def _L1_xattn_ref(q, k, v, mask, w_q, b_q, w_k, b_k, w_v, b_v, w_o, b_o):
        import jax, jax.numpy as jnp
        import numpy as np
        D_MODEL = 128
        NUM_HEADS = 16
        D_K = D_MODEL // NUM_HEADS
        B, S = (2, 256)
        NEG = -1000000000.0

        def _split_heads(x):
            b, s, _ = x.shape
            return x.reshape(b, s, NUM_HEADS, D_K).transpose(0, 2, 1, 3)
        qp = _split_heads(q @ w_q.T + b_q)
        kp = _split_heads(k @ w_k.T + b_k)
        vp = _split_heads(v @ w_v.T + b_v)
        scores = jnp.einsum('bhqd,bhkd->bhqk', qp, kp) / jnp.sqrt(jnp.float32(D_K))
        scores = jnp.where(mask, NEG, scores)
        attn = jax.nn.softmax(scores, axis=-1)
        out = jnp.einsum('bhqk,bhkd->bhqd', attn, vp)
        out = out.transpose(0, 2, 1, 3).reshape(q.shape[0], -1, D_MODEL)
        return out @ w_o.T + b_o

    def _L1_ffn_ref(x, Wg, W1, b1, Wo, bo):
        import jax, jax.numpy as jnp
        import numpy as np
        TOP_K = 2
        EPS = 1e-09
        E = Wg.shape[0]
        gate_logits = jnp.einsum('btd,ed->bte', x, Wg)
        gate_scores = jax.nn.softmax(gate_logits, axis=-1)
        topk_val, topk_idx = jax.lax.top_k(gate_scores, TOP_K)
        topk_val = topk_val / (topk_val.sum(axis=-1, keepdims=True) + EPS)
        comb = (jax.nn.one_hot(topk_idx, E, dtype=x.dtype) * topk_val[..., None]).sum(axis=-2)
        out = jnp.zeros_like(x)
        for e in range(E):
            h = jnp.einsum('btd,hd->bth', x, W1[e]) + b1[e]
            a, b = jnp.split(h, 2, axis=-1)
            g = a * jax.nn.sigmoid(b)
            eo = jnp.einsum('bth,dh->btd', g, Wo) + bo
            out = out + eo * comb[..., e:e + 1]
        return out
    x = x + jnp.tanh(g_xattn[0]) * _L0_xattn_ref(_layernorm(x, axis=-1), ctx_1024, ctx_1024, fside_BxSxS2_0, mask_BxSxS2_ik1, L0_xattn_wq_k, L0_xattn_wq_b, L0_xattn_wk_k, L0_xattn_wk_b, L0_xattn_wv_k, L0_xattn_wv_b, L0_xattn_wo_k, L0_xattn_wo_b)
    x = x + jnp.tanh(g_ffn[0]) * _L0_ffn_ref(_layernorm(x, axis=-1), L0_ffn_Wg, L0_ffn_W1, L0_ffn_b1, L0_ffn_W2, L0_ffn_b2)
    x = x + jnp.tanh(g_xattn[1]) * _L1_xattn_ref(_layernorm(x, axis=-1), ctx_1024, ctx_1024, mask_1x1xSxS2_bk1, L1_xattn_w_q, L1_xattn_b_q, L1_xattn_w_k, L1_xattn_b_k, L1_xattn_w_v, L1_xattn_b_v, L1_xattn_w_o, L1_xattn_b_o)
    x = x + jnp.tanh(g_ffn[1]) * _L1_ffn_ref(_layernorm(x, axis=-1), L1_ffn_Wg, L1_ffn_W1, L1_ffn_b1, L1_ffn_Wo, L1_ffn_bo)
    return x

_drawn_inputs = setup_inputs


def setup_inputs(seed=0):
    import zlib

    import numpy as np

    out = dict(_drawn_inputs(seed))
    spreads = {'g_ffn': (-1.0, 0.6),
     'L0_xattn_wq_b': (0.0, 0.8),
     'L0_xattn_wk_b': (0.0, 0.8),
     'L0_xattn_wv_b': (0.0, 0.1),
     'L0_xattn_wo_b': (0.0, 0.1),
     'L0_ffn_b1': (0.0, 0.8),
     'L0_ffn_b2': (0.0, 0.1),
     'L1_xattn_b_q': (0.0, 0.405),
     'L1_xattn_b_k': (0.0, 0.8),
     'L1_xattn_b_v': (0.0, 0.1),
     'L1_xattn_b_o': (0.0, 0.1)}
    factors = {'L1_ffn_Wg': 4.06,
     'L1_ffn_W1': 3.555,
     'L1_ffn_b1': 8.0,
     'L1_ffn_Wo': 3.488,
     'L1_ffn_bo': 3.912}
    for name, (base, spread) in spreads.items():
        noise = np.random.default_rng([zlib.crc32(name.encode()), seed]).standard_normal(out[name].shape)
        drawn = base * np.exp(spread * noise) if base else spread * noise
        out[name] = jnp.asarray(drawn.astype(out[name].dtype))
    for name, factor in factors.items():
        out[name] = (out[name] * factor).astype(out[name].dtype)
    return out
```

```python
from contextlib import ExitStack

import concourse.bass as bass
from concourse import mybir

B, S, S2, D = 32, 128, 120, 128
H = 16
DH = D // H
E = 8
HID0 = 512
HID1 = 256
TOPK = 2
TOKENS = B * S
CAP = -(-TOKENS * TOPK * 105 // (E * 100))
SLOTS = E * CAP

CB = 4
NCH = B // CB
CT = CB * S
CK = CB * S2
RING = 3
PAIRS = H // 2
HALF = 64
Q_SLOTS = (0, 1, 2, 0, 1, 0)
K_SLOTS = (0, 0, 0, 1, 1, 2)
SLOT_ROWS = 6 * DH
SHIFT_ROW = SLOT_ROWS
SPARE = HALF - SLOT_ROWS
EPS_LN = 1e-5
EPS_GATE = 1e-9
SCALE = 1.0 / float(DH) ** 0.5
NEG_ADD = -998244352.0
NEG_SET = -float(2 ** 100)
SKIP = float(2 ** 20)

ALU = mybir.AluOpType
ACT = mybir.ActivationFunctionType
F32 = mybir.dt.float32
BF16 = mybir.dt.bfloat16
I32 = mybir.dt.int32
U32 = mybir.dt.uint32
U8 = mybir.dt.uint8
AX_X = mybir.AxisListType.X


class Signal:

    def __init__(self, handle):
        self.handle, self.value = handle, 0


class Line:

    def __init__(self):
        self.items = []

    def put(self, emit, after=(), sig=None, by=1):
        self.items.append((emit, tuple(after), sig, by))
        if sig is None:
            return None
        sig.value += by
        return (sig, sig.value)

    def play(self, eng):
        waited = {}
        for emit, after, sig, by in self.items:
            for mark in after:
                if mark is not None and waited.get(id(mark[0]), 0) < mark[1]:
                    eng.wait_ge(mark[0].handle, mark[1])
                    waited[id(mark[0])] = mark[1]
            ins = emit(eng) if emit is not None else None
            if sig is not None:
                ins.then_inc(sig.handle, by)


def flamingo(nc, t, out, scratch):
    top = ExitStack()
    pe, act, dve, pool, sp = Line(), Line(), Line(), Line(), Line()
    signals = {}

    def sig(name):
        if name not in signals:
            signals[name] = Signal(top.enter_context(nc.semaphore(name)))
        return signals[name]

    def sb(stack, name, shape, dt=F32):
        return stack.enter_context(nc.sbuf_tensor(name, shape, dt))

    def load(name, dst, src, after=(), line=None):
        return (line or sp).put(lambda e: e.dma_start(dst, src), after, sig(name), 16)

    def fence():
        marks = [(s, s.value) for s in signals.values() if s.value]
        for line in (pe, act, dve, pool, sp):
            line.put(None, marks)

    x = sb(top, "x_rows", [S, B, D])
    ctxT = sb(top, "ctx_T", [D, B * S2])
    wq = sb(top, "wq", [D, 2, D])
    wk = sb(top, "wk", [D, 2, D])
    wv = sb(top, "wv", [D, 2, D])
    wo = sb(top, "wo", [D, 2, D])
    cols = sb(top, "bias_cols", [D, 4])
    bv = sb(top, "bv_rows", [S, 2, D])
    bo = sb(top, "bo_rows", [S, 2, D])
    tg_x = sb(top, "tanh_g_xattn", [S, 2])
    tg_f = sb(top, "tanh_g_ffn", [S, 2])
    g_in = sb(top, "g_in", [S, 4])
    ident = sb(top, "ident", [128, 128])
    cbf = sb(top, "const_bf16", [128, 3 * 128], BF16)
    ident_b, tri_b, ones_b = cbf[:, 0:128], cbf[:, 128:256], cbf[:, 256:384]
    iota8 = sb(top, "iota8", [128, E])
    wg = sb(top, "wg", [D, 2, E])
    half_c = sb(top, "minus_half", [128, CB])
    xn = sb(top, "xn_rows", [S, 2, CB, D])
    xnT = sb(top, "xn_T", [D, 2, CT])
    stats = sb(top, "ln_stats", [S, CB, 6])
    mv = sb(top, "ln_mean_var", [S, CB, 2])
    rs = sb(top, "ln_rstd", [S, 5, CB])
    slot_w = sb(top, "slot_weight", [S, TOPK, B])
    slot_put = sb(top, "slot_put", [S, TOPK, B], I32)
    slot_get = sb(top, "slot_get", [S, TOPK, B], I32)

    ps = top.enter_context(nc.psum_tensor("psum", [128, 8, 512], F32))
    ps_b = ps.bitcast(BF16) if hasattr(ps, "bitcast") else None

    for name, dst, src in (("ld_w", wq, "wq"), ("ld_w", wk, "wk"), ("ld_w", wv, "wv"), ("ld_w", wo, "wo"),
                           ("ld_w", cols, "cols"), ("ld_w", ident, "ident"), ("ld_w", cbf, "cbf"),
                           ("ld_w", iota8, "iota8"), ("ld_w", wg, "wg")):
        load(name, dst[:], t[src])
    load("ld_w", bv[:], t["bv"].partition_broadcast(S))
    load("ld_w", bo[:], t["bo"].partition_broadcast(S))
    weights_in = load("ld_w", g_in[:], t["g"].partition_broadcast(S))
    x_in, ctx_in = [], []
    for c0, c1 in ((0, 1), (1, NCH)):
        for c in range(c0, c1):
            x_in.append(load(f"ld_x{c0}", x[:, c0 * CB:c1 * CB, :], t["x"][:, c0 * CB:c1 * CB, :]) if c == c0 else x_in[-1])
            ctx_in.append(load(f"ld_c{c0}", ctxT[:, c0 * CK:c1 * CK], t["ctxT"][:, c0 * CK:c1 * CK]) if c == c0 else ctx_in[-1])

    act.put(lambda e: e.activation(tg_x[:, :], g_in[:, 0:2], ACT.Tanh), [weights_in], sig("tanh"))
    tanh_done = act.put(lambda e: e.activation(tg_f[:, :], g_in[:, 2:4], ACT.Tanh), (), sig("tanh"))
    const_done = pool.put(lambda e: e.memset(half_c[:], -0.5), (), sig("const"))
    for l in range(2):
        bo_done = dve.put(lambda e, l=l: e.tensor_scalar(bo[:, l, :], bo[:, l, :], tg_x[:, l:l + 1], None, ALU.mult),
                          [tanh_done], sig("bo"))

    misc = {"n": 0, "free": [None, None]}
    MISC = (6, 7)

    def misc_bank():
        k = misc["n"] % 2
        misc["n"] += 1
        return k, ps[:, MISC[k], :]

    ln = {"n": 0, "rows_free": [None, None], "T_free": [None, None]}

    def layernorm(c, ready):
        k = ln["n"] % 2
        ln["n"] += 1
        for b in range(CB):
            m = dve.put(lambda e, b=b: e.bn_stats(stats[:, b, :], x[:, c * CB + b, :]), [ready, ln.get("agg"), ln.get("norm")], sig("ln_stats"))
        for b in range(CB):
            agg = dve.put(lambda e, b=b: e.bn_aggr(mv[:, b, :], stats[:, b, :]), [m, ln.get("norm")], sig("ln_aggr"))
        ln["agg"] = agg
        ops = [
            lambda e: e.tensor_scalar(rs[:, 0, :], mv[:, :, 1], EPS_LN, None, ALU.add),
            lambda e: e.tensor_tensor(rs[:, 1, :], rs[:, 0, :], half_c[:, :], ALU.pow),
            lambda e: e.tensor_tensor(rs[:, 2, :], rs[:, 1, :], rs[:, 1, :], ALU.mult),
            lambda e: e.tensor_tensor(rs[:, 3, :], rs[:, 2, :], rs[:, 0, :], ALU.mult),
            lambda e: e.tensor_scalar(rs[:, 2, :], rs[:, 3, :], -0.5, 1.5, ALU.mult, ALU.add),
            lambda e: e.tensor_tensor(rs[:, 4, :], rs[:, 1, :], rs[:, 2, :], ALU.mult),
        ]
        r = [agg, ln.get("norm"), const_done]
        for op in ops:
            r = [pool.put(op, r, sig("ln_rstd"))]
        for b in range(CB):
            norm = dve.put(lambda e, b=b: e.tensor_scalar(xn[:, k, b, :], x[:, c * CB + b, :], mv[:, b, 0:1],
                                                          rs[:, 4, b:b + 1], ALU.subtract, ALU.mult),
                           r + [ln["rows_free"][k]], sig("ln_norm"))
        ln["norm"] = norm
        m, bank = misc_bank()
        for b in range(CB):
            tr = pe.put(lambda e, b=b: e.transpose(bank[:, b * S:(b + 1) * S], xn[:, k, b, :], ident[:, :]),
                        [norm, misc["free"][m], weights_in], sig("ln_T"))
        ln["rows_free"][k] = tr
        done = act.put(lambda e: e.copy(xnT[:, k, :], bank), [tr, ln["T_free"][k]], sig("ln_T_out"))
        misc["free"][m] = done
        return k, norm, done

    def attention(l, x_ready, after_chunk):
        mem = ExitStack()
        buf = lambda name, shape, dt=F32: sb(mem, f"{name}{l}", shape, dt)
        v_rows = buf("v_rows", [S2, 2, CB, D])
        full = buf("full", [D, 2, CT])
        parts = buf("parts", [D, 2, 3, CT], BF16)
        qop = buf("q_operand", [128, RING, PAIRS, CT], BF16)
        kop = buf("k_operand", [128, RING, PAIRS, 2, CK], BF16)
        neg = buf("neg_rows", [S, 2, CB, S2], BF16)
        negT = buf("neg_cols", [S2, 2, CB, S], BF16)
        shift = buf("shift", [S, 2, H])
        rest = buf("shift_rest", [S, 2, H])
        sparts = buf("shift_parts", [S, 2, 3, H], BF16)
        spT = buf("shift_parts_T", [3 * H, 2, S], BF16)
        expT = buf("exp_T", [S2, 2, H, S])
        vx = buf("v_spread", [S2, 2, 4 * 128])
        onesx = buf("ones_spread", [S2, 4, 32])
        rden = buf("rden", [D, S])
        oT = buf("o_T", [D, 2, S])
        if l == 0:
            m_in = buf("mask_in", [S, CB, S2], I32)
            mT_in = buf("maskT_in", [S2, CB, S], I32)
            gT = buf("group_T", [S2, 2, CB, S])
            expG = buf("exp_G", [S2, 2, H, S])
        else:
            m_in = buf("mask_in", [S, S2], U8)
            mT_in = buf("maskT_in", [S2, S], U8)
        q_dram, k_dram, s_dram = scratch["q"], scratch["k"], scratch["shift"]
        n = lambda name: name

        z = []
        for r in range(RING):
            line = (dve, pool)[r % 2]
            z.append(line.put(lambda e, r=r: e.memset(kop[:, r].rearrange("p a b c -> p (a b c)").bitcast(U32), 0), (), sig(n(f"zero{r % 2}_"))))
        ones_in = []
        for r in range(RING):
            for i in range(2):
                m = load(n("ones_row"), kop[HALF * i + SHIFT_ROW:HALF * i + SHIFT_ROW + 3, r, :, i, :],
                         t["ones"][0:3], [z[r]])
        ones_in = m
        a = pool.put(lambda e: e.memset(vx[:], 0.0), (), sig(n("spread0")))
        a = pool.put(lambda e: e.memset(onesx[:], 0.0), (), sig(n("spread0")))
        for g in range(4):
            spread = pool.put(lambda e, g=g: e.memset(onesx[:, g, 8 * g:8 * g + 8], 1.0), [a], sig(n("spread1")))

        free = {}
        q_ready, k_ready, v_ready, neg_ready, g_ready = {}, {}, {}, {}, {}

        def masks(c):
            k = c % 2
            if l == 1:
                if c == 0:
                    a = load(n("mask"), m_in[:], t["mask1"])
                    a = load(n("mask"), mT_in[:], t["mask1T"])
                    pool.put(lambda e: e.tensor_scalar(neg[:, 0, 0, :], m_in[:], NEG_SET, None, ALU.mult), [a], sig(n("neg")))
                    neg_ready[0] = pool.put(lambda e: e.tensor_scalar(negT[:, 0, 0, :], mT_in[:], NEG_SET, None, ALU.mult), (), sig(n("neg")))
                neg_ready[c] = neg_ready[0]
                return
            sl = slice(c * CB, (c + 1) * CB)
            a = load(n("mask"), m_in[:], t["mask0"][:, sl, :], [free.get("m_in")])
            a = load(n("mask"), mT_in[:], t["mask0T"][:, sl, :], [free.get("m_in")])
            g_ready[c] = load(n(f"group{k}_"), gT[:, k], t["groupT"][:, sl, :], [free.get(("g", k))])
            pool.put(lambda e: e.tensor_scalar(neg[:, k], m_in[:], -NEG_ADD, NEG_ADD, ALU.mult, ALU.add),
                     [a, free.get(("neg", k))], sig(n("neg")))
            neg_ready[c] = free["m_in"] = pool.put(
                lambda e: e.tensor_scalar(negT[:, k], mT_in[:], -NEG_ADD, NEG_ADD, ALU.mult, ALU.add),
                [free.get(("negT", k))], sig(n("neg")))

        def split(k, width, made, dram, slots, name):
            f, p = full[:, k, 0:width], parts[:, k, :, 0:width]
            a = act.put(lambda e: e.copy(p[:, 0, :], f), [made, free.get(("parts", k))], sig(n("part0")))
            a = pool.put(lambda e: e.tensor_tensor(f, f, p[:, 0, :], ALU.subtract), [a], sig(n("left")))
            a = act.put(lambda e: e.copy(p[:, 1, :], f), [a], sig(n("part1")))
            a = pool.put(lambda e: e.tensor_tensor(p[:, 2, :], f, p[:, 1, :], ALU.subtract), [a], sig(n("left")))
            free[("full", k)] = a
            for slot in slots:
                part = Q_SLOTS[slot] if k == 0 else K_SLOTS[slot]
                w = load(n(f"{name}_out"), dram[:, slot], p[:, part, :], [a])
            free[("parts", k)] = w
            return w

        def project(c, which, src, src_ready, w, bias_col, scale, width):
            m, bank = misc_bank()
            k = which
            mm = pe.put(lambda e: e.matmul(bank[:, 0:width], w[:, l, :], src, start=True, stop=True),
                        [src_ready, misc["free"][m], weights_in], sig(n("project")))
            made = misc["free"][m] = dve.put(
                lambda e: e.tensor_scalar(full[:, k, 0:width], bank[:, 0:width], cols[:, bias_col:bias_col + 1], scale,
                                          ALU.add, ALU.mult), [mm, free.get(("full", k))], sig(n("projected")))
            return mm, made

        def prep_q(c):
            k, norm, done = layernorm(c, x_ready[c])
            mm, made = project(c, 0, xnT[:, k, :], done, wq, 2 * l, SCALE, CT)
            ln["T_free"][k] = mm
            for b in range(CB):
                xb = pool.put(lambda e, b=b: e.tensor_tensor(x[:, c * CB + b, :], x[:, c * CB + b, :], bo[:, l, :], ALU.add),
                              [norm, bo_done], sig(n("x_bias")))
            x_biased[c] = xb
            w = split(0, CT, made, q_dram[c], range(3), "q")
            r = c % RING
            for i in range(2):
                of_head = q_dram[c].rearrange("(t i) s d n -> i (s d) t n", i=2)[i]
                for s0, s1, src0 in ((0, 3, 0), (3, 5, 0), (5, 6, 0)):
                    load(n(f"q_in{r}_"), qop[HALF * i + s0 * DH:HALF * i + s1 * DH, r, :, :],
                         of_head[src0 * DH:(src0 + s1 - s0) * DH], [w, free.get(("qop", r))])
                q_ready[c] = load(n(f"q_in{r}_"), qop[HALF * i + SLOT_ROWS:HALF * (i + 1), r, :, :], t["zeros"])

        def prep_k(c):
            mm, made = project(c, 1, ctxT[:, c * CK:(c + 1) * CK], ctx_in[c], wk, 2 * l + 1, 1.0, CK)
            w = split(1, CK, made, k_dram[c], range(6), "k")
            r = c % RING
            for i in range(2):
                of_head = k_dram[c].rearrange("(t i) s d n -> i (s d) t n", i=2)[i]
                k_ready[c] = load(n(f"k_in{r}_"), kop[HALF * i:HALF * i + SLOT_ROWS, r, :, i, :], of_head,
                                  [w, free.get(("qop", r)), ones_in, z[r]])

        def prep_v(c):
            m, bank = misc_bank()
            for b in range(CB):
                mm = pe.put(lambda e, b=b: e.matmul(bank[0:S2, b * D:(b + 1) * D], ctxT[:, (c * CB + b) * S2:(c * CB + b + 1) * S2],
                                                    wv[:, l, :], start=True, stop=True),
                            [misc["free"][m], ctx_in[c]], sig(n("v_project")))
            v_ready[c] = misc["free"][m] = dve.put(
                lambda e: e.tensor_tensor(v_rows[:, c % 2], bank[0:S2, :].rearrange("p (b d) -> p b d", b=CB),
                                          bv[0:S2, l:l + 1, :].broadcast_to([S2, CB, D]), ALU.add),
                [mm, free.get(("v", c % 2))], sig(n("v_rows")))

        BANK_S, BANK_T, BANK_AV = 0, 1, 5
        live = {}

        def scores(i, r):
            c, b = divmod(i, CB)
            k = 0 if l == 1 else c % 2
            bb = 0 if l == 1 else b
            bank = ps[:, BANK_S, 0:4 * S2].rearrange("p (h k) -> p h k", h=4)
            pe.put(lambda e: e.matmul(bank, ident_b, neg[:, k, bb:bb + 1, :].broadcast_to([S, 4, S2]), start=True, stop=False),
                   [free.get("S"), neg_ready[c], q_ready[c], k_ready[c]])
            for u in range(2):
                pt = 2 * r + u
                mm = pe.put(lambda e, u=u, pt=pt: e.matmul(bank[:, 2 * u:2 * u + 2, :], qop[:, c % RING, pt, b * S:(b + 1) * S],
                                                           kop[:, c % RING, pt, :, b * S2:(b + 1) * S2], start=False, stop=(u == 1)),
                            (), sig(n("score")) if u == 1 else None)
            mx = free["S"] = dve.put(lambda e: e.tensor_reduce(shift[:, i % 2, 4 * r:4 * r + 4], bank, AX_X, ALU.max, negate=True),
                                     [mm, free.get(("shift", i % 2))], sig(n("row_max")))
            free[("neg", c % 2)] = mm
            if r == 3:
                live[("scored", i)] = mm
                k2 = i % 2
                sp_ = sparts[:, k2]
                order = lambda a: a.rearrange("p (t i) -> p i t", i=2)
                by_part = sp_.rearrange("p s h -> p (s h)").rearrange("p (i s t) -> p i s t", i=2, s=3)
                to = lambda j: by_part[:, :, j, :]
                a = pool.put(lambda e: e.tensor_copy(to(0), order(shift[:, k2])), [mx, free.get(("sparts", k2))], sig(n("shift_part")))
                a = pool.put(lambda e: e.tensor_tensor(order(rest[:, k2]), order(shift[:, k2]), to(0), ALU.subtract), [a], sig(n("shift_part")))
                a = pool.put(lambda e: e.tensor_copy(to(1), order(rest[:, k2])), [a], sig(n("shift_part")))
                a = pool.put(lambda e: e.tensor_tensor(to(2), order(rest[:, k2]), to(1), ALU.subtract), [a], sig(n("shift_part")))
                free[("shift", k2)] = live[("sparts", i)] = a

        def shift_rows(i):
            c, b = divmod(i, CB)
            k2 = i % 2
            m, bank = misc_bank()
            bank_b = bank[0:3 * H, 0:S // 2].bitcast(BF16)
            tr = free[("sparts", k2)] = pe.put(lambda e: e.transpose(bank_b, sparts[:, k2].rearrange("p s h -> p (s h)"), ident_b),
                                               [live[("sparts", i)], misc["free"][m]], sig(n("shift_T")))
            cp = misc["free"][m] = act.put(lambda e: e.copy(spT[:, k2, :], bank_b), [tr, free.get(("spT", k2))], sig(n("shift_T_out")))
            w = free[("spT", k2)] = load(n(f"shift_out{k2}_"), s_dram[i], spT[:, k2, :], [cp])
            for par in range(2):
                src = s_dram[i][par * 3 * PAIRS:(par + 1) * 3 * PAIRS, :].rearrange("(s t) q -> s t q", s=3)
                live[("shift", i)] = load(n(f"shift_in{i % 4}_"), qop[HALF * par + SHIFT_ROW:HALF * par + SHIFT_ROW + 3, c % RING, :, b * S:(b + 1) * S],
                                          src, [w, live[("scored", i)]])

        def weights(i, p):
            c, b = divmod(i, CB)
            k = 0 if l == 1 else c % 2
            bb = 0 if l == 1 else b
            for half in range(2):
                bank = ps[0:S2, BANK_T + 2 * p + half, :]
                pe.put(lambda e, bank=bank: e.matmul(bank.rearrange("p (h q) -> p h q", h=4), ident_b[0:S2, 0:S2],
                                                     negT[:, k, bb:bb + 1, :].broadcast_to([S2, 4, S]), start=True, stop=False),
                       [free.get(("T", p)), live[("shift", i)]])
                for u in range(4):
                    h = 8 * p + 4 * half + u
                    mm = pe.put(lambda e, bank=bank, u=u, h=h: e.matmul(
                        bank[:, u * S:(u + 1) * S], kop[:, c % RING, h // 2, h % 2, b * S2:(b + 1) * S2],
                        qop[:, c % RING, h // 2, b * S:(b + 1) * S], start=False, stop=(u == 3)),
                        (), sig(n("logit_T")) if half == 1 and u == 3 else None)
            free[("negT", c % 2)] = mm
            free[("qop", c % RING)] = mm
            k2 = i % 2
            src = ps[0:S2, BANK_T + 2 * p:BANK_T + 2 * p + 2, :].rearrange("p a (h q) -> p (a h) q", h=4)
            ex = free[("T", p)] = act.put(lambda e: e.activation(expT[:, k2, 8 * p:8 * p + 8, :], src, ACT.Exp),
                                          [mm, free.get(("expT", k2))], sig(n("exp")))
            live[("exp", i, p)] = ex

        def gate(i, p):
            if l == 1:
                return
            c, b = divmod(i, CB)
            k2 = i % 2
            for line, name, h0, h1 in ((dve, "gate_v", 8 * p, 8 * p + 6), (pool, "gate_p", 8 * p + 6, 8 * p + 8)):
                live[(name, i, p)] = line.put(lambda e, h0=h0, h1=h1: e.tensor_tensor(
                    expG[:, k2, h0:h1, :], expT[:, k2, h0:h1, :], gT[:, c % 2, b:b + 1, :].broadcast_to([S2, h1 - h0, S]), ALU.mult),
                    [live[("exp", i, p)], g_ready[c], free.get(("expG", k2))], sig(n(name)))
            if b == CB - 1 and p == 1:
                free[("g", c % 2)] = live[("gate_v", i, 1)]
                free[("g2", c % 2)] = live[("gate_p", i, 1)]

        def spread_v(i):
            c, b = divmod(i, CB)
            dst = vx[:, i % 2, :]
            dst = bass.AP(dst.tensor, dst.offset, [list(dst.ap[0]), [128, 4], [40, 4], [1, DH]])
            a = pool.put(lambda e: e.tensor_copy(dst, v_rows[:, c % 2, b, :].rearrange("p (j g d) -> p j g d", j=4, g=4)),
                         [v_ready[c], spread, free.get(("vx", i % 2))], sig(n("spread_v")))
            live[("vx", i)] = a
            free[("v", c % 2)] = a

        def out_part(i, g_lo, g_hi, den):
            k2 = i % 2
            src = expT if den or l == 1 else expG
            for g in range(g_lo, g_hi):
                for j in range(4):
                    h = 4 * j + g
                    lhs = onesx[:, g, :] if den else vx[:, k2, h * 32:(h + 1) * 32]
                    dst = ps[32 * j:32 * j + 32, BANK_AV, (S if den else 0):(2 * S if den else S)]
                    after = [live[("exp", i, 0)], live[("exp", i, 1)], live[("vx", i)], free.get("AV")]
                    if not den and l == 0:
                        after += [live[(nm, i, p)] for nm in ("gate_v", "gate_p") for p in range(2)]
                    mm = pe.put(lambda e, lhs=lhs, dst=dst, h=h, g=g: e.matmul(dst, lhs, src[:, k2, h, :],
                                                                         start=(g == 0 and not den), stop=(g == 3),
                                                                         skip_group_check=True),
                                after, sig(n("av")) if (g == 3 and j == 3) else None)
            if den:
                free[("expT", k2)] = mm
                live[("den", i)] = mm
            else:
                free[("vx", k2)] = mm
                free[("expG", k2)] = mm

        def normalise(i):
            a = dve.put(lambda e: e.reciprocal(rden[:], ps[:, BANK_AV, S:2 * S]), [live[("den", i)], free.get("rden")], sig(n("rden")))
            live[("oT", i)] = free["AV"] = free["rden"] = dve.put(
                lambda e: e.tensor_tensor(oT[:, i % 2, :], ps[:, BANK_AV, 0:S], rden[:], ALU.mult),
                [a, free.get(("oT", i % 2))], sig(n("o_T")))

        def out_project(i):
            c, b = divmod(i, CB)
            m, bank = misc_bank()
            mm = free[("oT", i % 2)] = pe.put(lambda e: e.matmul(bank[:, 0:D], oT[:, i % 2, :], wo[:, l, :], start=True, stop=True),
                                              [live[("oT", i)], misc["free"][m]], sig(n("out_project")))
            misc["free"][m] = dve.put(lambda e: e.scalar_tensor_tensor(x[:, i, :], bank[:, 0:D], tg_x[:, l:l + 1], x[:, i, :],
                                                                       ALU.mult, ALU.add),
                                      [mm, x_biased[c]], sig(n("x_new")))
            if b == CB - 1:
                x_done[c] = misc["free"][m]

        x_biased, x_done = {}, {}
        masks(0)
        prep_k(0)
        prep_q(0)
        prep_v(0)
        LAG_T, LAG_AV = 3, 4
        for i in range(B + LAG_AV + 1 + 2 * CB):
            if 0 <= i - LAG_AV - 1 < B:
                normalise(i - LAG_AV - 1)
            for r in range(4):
                if i < B:
                    scores(i, r)
                if r % 2 == 0 and 0 <= i - LAG_T < B:
                    weights(i - LAG_T, r // 2)
                if r == 0 and 0 <= i - LAG_AV - 1 < B:
                    out_project(i - LAG_AV - 1)
                if r == 1 and 0 <= i - 1 < B:
                    shift_rows(i - 1)
                if r == 1 and 0 <= i - LAG_AV < B:
                    out_part(i - LAG_AV, 0, 4, False)
                if r == 1 and 0 <= i - LAG_T < B:
                    spread_v(i - LAG_T)
                    gate(i - LAG_T, 0)
                if r == 3 and 0 <= i - LAG_AV < B:
                    out_part(i - LAG_AV, 0, 4, True)
                if r == 3 and 0 <= i - LAG_T < B:
                    gate(i - LAG_T, 1)
                if r == 3:
                    c, b = divmod(i, CB)
                    if c + 1 < NCH:
                        if b == 0:
                            prep_k(c + 1)
                        if b == 1:
                            prep_q(c + 1)
                        if b == 2:
                            if l == 0 and ("g2", (c + 1) % 2) in free:
                                sp.put(None, [free[("g2", (c + 1) % 2)]])
                            masks(c + 1)
                        if b == 3:
                            prep_v(c + 1)
            j = i - LAG_AV - 2
            if j >= 0 and j % CB == CB - 1 and j // CB < NCH:
                after_chunk(j // CB, x_done[j // CB])
        fence()
        mem.close()
        return x_done

    rt = ExitStack()
    lg = sb(rt, "r_logits", [S, CB, E])
    mx8 = sb(rt, "r_top", [S, CB, E])
    ix8 = sb(rt, "r_index", [S, CB, E], U32)
    ixf = sb(rt, "r_index_f", [S, TOPK, CB])
    oh = sb(rt, "r_onehot", [S, TOPK, CB, E])
    oh_b = sb(rt, "r_onehot_sum", [S, CB, E], BF16)
    run_b = sb(rt, "r_running", [S, E], BF16)
    run_f = sb(rt, "r_running_f", [S, E])
    tot_f = sb(rt, "r_chunk_total", [S, E])
    prod = sb(rt, "r_prod", [S, TOPK, CB, E])
    pos = sb(rt, "r_pos", [S, TOPK, CB])
    keep = sb(rt, "r_keep", [S, TOPK, CB])
    dest = sb(rt, "r_dest", [S, TOPK, CB])
    tmp = sb(rt, "r_tmp", [S, TOPK, CB])
    gate_e = sb(rt, "r_gate", [S, 3, CB])
    zero_rows = sb(rt, "zero_rows", [128, 1024])
    zeroed = pool.put(lambda e: e.memset(zero_rows[:], 0.0), (), sig("zero_rows"))
    run0 = dve.put(lambda e: e.memset(run_b[:], 0.0), (), sig("r_run"))
    run0 = dve.put(lambda e: e.memset(run_f[:], 0.0), (), sig("r_run"))
    flat = scratch["xe"].rearrange("n d -> (n d)")
    size = 128 * 1024
    at = 0
    while at < SLOTS * D:
        k = min(size, SLOTS * D - at) // 128
        zero_in = load("zero_slots", flat[at:at + k * 128].rearrange("(p n) -> p n", p=128), zero_rows[:, 0:k], [zeroed])
        at += k * 128
    R = {}

    def choose(l, c, lnT_done, k):
        m, bank = misc_bank()
        for b in range(CB):
            mm = pe.put(lambda e, b=b: e.matmul(bank[:, b * E:(b + 1) * E], xnT[:, k, b * S:(b + 1) * S], wg[:, l, :], start=True, stop=True),
                        [lnT_done, misc["free"][m]], sig("r_mm"))
        a = misc["free"][m] = dve.put(lambda e: e.tensor_copy(lg[:], bank[:, 0:CB * E].rearrange("p (b e) -> p b e", b=CB)), [mm], sig("r_v"))
        for b in range(CB):
            a2 = dve.put(lambda e, b=b: e.max(mx8[:, b, :], lg[:, b, :]), [a, R.get("gate")], sig("r_v"))
        for b in range(CB):
            a = dve.put(lambda e, b=b: e.max_index(ix8[:, b, :], mx8[:, b, :], lg[:, b, :]), [a2], sig("r_v"))
        a = dve.put(lambda e: e.tensor_copy(ixf[:], ix8[:, :, 0:TOPK].rearrange("p b k -> p k b")), [a], sig("r_v"))
        for j in range(TOPK):
            a = dve.put(lambda e, j=j: e.tensor_tensor(oh[:, j], iota8[:].rearrange("p (o e) -> p o e", o=1).broadcast_to([S, CB, E]),
                                                       ixf[:, j, :].rearrange("p (b o) -> p b o", o=1).broadcast_to([S, CB, E]), ALU.is_equal),
                        [a, weights_in], sig("r_v"))
        return mm, a2, a

    def route(c, x_done):
        k, norm, lnT = layernorm(c, x_done)
        mm, top, hot = choose(0, c, lnT, k)
        ln["T_free"][k] = mm
        V = lambda fn, after: dve.put(fn, after, sig("r_v"))
        a = V(lambda e: e.tensor_tensor(gate_e[:, 0, :], mx8[:, :, 1], mx8[:, :, 0], ALU.subtract), [top])
        a = act.put(lambda e: e.activation(gate_e[:, 1, :], gate_e[:, 0, :], ACT.Exp), [a], sig("r_exp"))
        a = V(lambda e: e.tensor_scalar(gate_e[:, 2, :], gate_e[:, 1, :], 1.0, None, ALU.add), [a])
        a = V(lambda e: e.reciprocal(gate_e[:, 0, :], gate_e[:, 2, :]), [a])
        a = V(lambda e: e.tensor_tensor(gate_e[:, 1, :], gate_e[:, 1, :], gate_e[:, 0, :], ALU.mult), [a])
        R["gate"] = a
        a = V(lambda e: e.tensor_tensor(oh_b[:], oh[:, 0], oh[:, 1], ALU.add), [hot])
        m, bank = misc_bank()
        for b in range(CB):
            srcs = [(tri_b, oh_b[:, b, :])] + [(ones_b, oh_b[:, j, :]) for j in range(b)] + [(ones_b, run_b[:, :])]
            for s_, (lhs, rhs) in enumerate(srcs):
                mm = pe.put(lambda e, lhs=lhs, rhs=rhs, b=b, s_=s_, n_=len(srcs): e.matmul(
                    bank[:, b * E:(b + 1) * E], lhs, rhs, start=(s_ == 0), stop=(s_ == n_ - 1)),
                    [a, run0, misc["free"][m]] + ([R["run"]] if "run" in R else []), sig("r_mm"))
        for j in range(TOPK):
            a = V(lambda e, j=j: e.tensor_tensor(prod[:, j], oh[:, j], bank[:, 0:CB * E].rearrange("p (b e) -> p b e", b=CB), ALU.mult), [mm, a])
        misc["free"][m] = a
        t1 = V(lambda e: e.tensor_reduce(tot_f[:], oh_b[:].rearrange("p b e -> p e b"), AX_X, ALU.add), [run0])
        t1 = V(lambda e: e.tensor_tensor(run_f[:], run_f[:], tot_f[:], ALU.add), [t1])
        R["run"] = V(lambda e: e.tensor_copy(run_b[:], run_f[:]), [t1, mm])
        a = V(lambda e: e.tensor_reduce(pos[:], prod[:], AX_X, ALU.add), [a])
        V(lambda e: e.tensor_scalar(keep[:], pos[:], float(CAP), None, ALU.is_lt), [a])
        a = V(lambda e: e.scalar_tensor_tensor(dest[:], ixf[:], float(CAP), pos[:], ALU.mult, ALU.add), [a])
        sl = slice(c * CB, (c + 1) * CB)
        V(lambda e: e.tensor_scalar(slot_get[:, :, sl], dest[:], float(SLOTS - 1), None, ALU.min), [a])
        a = V(lambda e: e.tensor_scalar(tmp[:], keep[:], -SKIP, SKIP, ALU.mult, ALU.add), [a])
        put = V(lambda e: e.tensor_tensor(slot_put[:, :, sl], dest[:], tmp[:], ALU.add), [a])
        a = V(lambda e: e.tensor_scalar(tmp[:], keep[:], tg_f[:, 0:1], None, ALU.mult), [put])
        for j in range(TOPK):
            R["w"] = V(lambda e, j=j: e.tensor_tensor(slot_w[:, j, sl], gate_e[:, j, :], tmp[:, j, :], ALU.mult), [a])
        R["gate"] = R["w"]
        for b in range(CB):
            for j in range(TOPK):
                sc = pool.put(lambda e, b=b, j=j: e.indirect_dma_start(
                    scratch["xe"][:, :], bass.IndirectOffsetOnAxis(slot_put[:, j, c * CB + b:c * CB + b + 1], 0),
                    xn[:, k, b, :], None, bounds_check=SLOTS - 1, oob_is_err=False),
                    [put, zero_in], sig(f"scatter{c % 2}"), 16)
        R[("scatter", c)] = sc
        R["all"] = R.get("all", []) + [sc]
        scattered[k] = sc
        ln["rows_free"][k] = sc

    scattered = {}

    def attention_plain(l, ready):
        return attention(l, ready, lambda c, m: None)

    x_done = attention(0, x_in, route)

    mem = ExitStack()
    w1 = sb(mem, "w1", [D, E, HID0])
    w2 = sb(mem, "w2", [128, E, HID0 // 128, D])
    b1 = sb(mem, "b1_cols", [128, E, HID0 // 128])
    b2 = sb(mem, "b2_rows", [128, E, D])
    NC0 = HID0 // 128
    GW = 3 * 128
    groups = [(a, min(GW, CAP - a)) for a in range(0, CAP, GW)]
    xe = sb(mem, "xe_rows", [128, 3, 3, D])
    xeT = sb(mem, "xe_T", [D, 2, GW])
    hT = sb(mem, "h_T", [128, 2, NC0, GW])
    yb = sb(mem, "y_rows", [128, 3, 3, D])
    w_in = [None] * E
    consts = load("ld_w2", b1[:], t["b1"])
    consts = load("ld_w2", b2[:], t["b2"].partition_broadcast(128))
    for e_ in range(E):
        if e_ in (0, 1):
            hi = 1 if e_ == 0 else E
            load(f"ld_e{e_}", w1[:, e_:hi], t["w1"][:, e_:hi])
            load(f"ld_e{e_}", w2[:, e_:hi], t["w2"][:, e_:hi])
        w_in[e_] = (sig(f"ld_e{min(e_, 1)}"), 32)
    jobs = [(e_, a, w) for e_ in range(E) for a, w in groups]
    F = {}
    H_BANKS, T_BANKS, Y_BANKS = (0, 1, 2, 3), (4, 5), (6, 7)

    def fetch(n):
        e_, a, w = jobs[n]
        base = e_ * CAP + a
        full_, part_ = divmod(w, 128)
        after = [F.get(("xe", n % 3))] + R["all"]
        if full_:
            F[("in", n)] = load(f"xe_in{n % 3}", xe[:, n % 3, 0:full_, :], scratch["xe"][base:base + full_ * 128, :].rearrange("(s p) d -> p s d", p=128), after)
        if part_:
            F[("in", n)] = load(f"xe_in{n % 3}", xe[0:part_, n % 3, full_, :], scratch["xe"][base + full_ * 128:base + w, :], after)

    def turn(n):
        e_, a, w = jobs[n]
        bank = ps[:, T_BANKS[n % 2], :]
        for s_ in range(-(-w // 128)):
            r_ = min(128, w - 128 * s_)
            mm = pe.put(lambda e, s_=s_, r_=r_: e.transpose(bank[:, s_ * 128:s_ * 128 + r_], xe[0:r_, n % 3, s_, :], ident[0:r_, 0:r_]),
                        [F[("in", n)], F.get(("Tbank", n % 2))], sig("e_T"))
        F[("xe", n % 3)] = mm
        F[("xeT", n)] = F[("Tbank", n % 2)] = dve.put(lambda e: e.tensor_copy(xeT[:, n % 2, 0:w], bank[:, 0:w]),
                                                      [mm, F.get(("xeTfree", n % 2))], sig("e_T_out"))

    def up(n):
        e_, a, w = jobs[n]
        for q in range(NC0):
            bank = ps[:, H_BANKS[q], 0:w]
            mm = pe.put(lambda e, q=q, bank=bank: e.matmul(bank, w1[:, e_, q * 128:(q + 1) * 128], xeT[:, n % 2, 0:w], start=True, stop=True),
                        [F[("xeT", n)], w_in[e_], F.get(("H", q))], sig("e_up"))
            F[("H", q)] = F[("h", n)] = act.put(lambda e, q=q, bank=bank: e.activation(hT[:, n % 2, q, 0:w], bank, ACT.Gelu_apprx_tanh, bias=b1[:, e_, q:q + 1]),
                                  [mm, consts, F.get(("hfree", n % 2))], sig("e_gelu"))
        F[("xeTfree", n % 2)] = mm

    def down(n):
        e_, a, w = jobs[n]
        bank = ps[:, Y_BANKS[n % 2], :]
        for s_ in range(-(-w // 128)):
            r_ = min(128, w - 128 * s_)
            for q in range(NC0):
                mm = pe.put(lambda e, s_=s_, r_=r_, q=q: e.matmul(bank[0:r_, s_ * D:(s_ + 1) * D], hT[:, n % 2, q, s_ * 128:s_ * 128 + r_], w2[:, e_, q, :],
                                                                  start=(q == 0), stop=(q == NC0 - 1)),
                            [F[("h", n)], F.get(("Y", n % 2))], sig("e_down") if q == NC0 - 1 else None)
        F[("hfree", n % 2)] = mm
        base = e_ * CAP + a
        full_, part_ = divmod(w, 128)
        marks = []
        y3 = bank[:, 0:3 * D].rearrange("p (s d) -> p s d", s=3)
        if full_:
            a1 = dve.put(lambda e: e.tensor_tensor(yb[:, n % 3, 0:full_, :], y3[:, 0:full_, :], b2[:, e_:e_ + 1, :].broadcast_to([128, full_, D]), ALU.add),
                         [mm, F.get(("y", n % 3))], sig("e_y"))
        if part_:
            a1 = dve.put(lambda e: e.tensor_tensor(yb[0:part_, n % 3, full_, :], y3[0:part_, full_, :], b2[0:part_, e_, :], ALU.add),
                         [mm, F.get(("y", n % 3))], sig("e_y"))
        F[("Y", n % 2)] = a1
        if full_:
            F[("y", n % 3)] = load(f"y_out{n % 3}", scratch["y"][base:base + full_ * 128, :].rearrange("(s p) d -> p s d", p=128), yb[:, n % 3, 0:full_, :], [a1])
        if part_:
            F[("y", n % 3)] = load(f"y_out{n % 3}", scratch["y"][base + full_ * 128:base + w, :], yb[0:part_, n % 3, full_, :], [a1])
        F[("ydone", n % 3)] = F[("y", n % 3)]

    NJ = len(jobs)
    fetch(0)
    fetch(1)
    turn(0)
    for n in range(NJ):
        if n + 2 < NJ:
            fetch(n + 2)
        if n + 1 < NJ:
            turn(n + 1)
        up(n)
        if n >= 1:
            down(n - 1)
    down(NJ - 1)
    ys = [F[("ydone", k)] for k in range(3)]
    got = sb(mem, "got_rows", [128, 4, TOPK, D])
    x2 = []
    for i in range(B):
        for j in range(TOPK):
            g_ = pool.put(lambda e, i=i, j=j: e.indirect_dma_start(got[:, i % 4, j, :], None, scratch["y"][:, :],
                                                                   bass.IndirectOffsetOnAxis(slot_get[:, j, i:i + 1], 0),
                                                                   bounds_check=SLOTS - 1, oob_is_err=True),
                          ys + [F.get(("got", i % 4)), R["w"]], sig(f"gather{i % 4}"), 16)
        a = dve.put(lambda e, i=i: e.scalar_tensor_tensor(x[:, i, :], got[:, i % 4, 0, :], slot_w[:, 0, i:i + 1], x[:, i, :], ALU.mult, ALU.add), [g_], sig("combine"))
        F[("got", i % 4)] = dve.put(lambda e, i=i: e.scalar_tensor_tensor(x[:, i, :], got[:, i % 4, 1, :], slot_w[:, 1, i:i + 1], x[:, i, :], ALU.mult, ALU.add), [a], sig("combine"))
        if i % CB == CB - 1:
            x2.append(F[("got", i % 4)])
    fence()
    mem.close()

    x_done = attention_plain(1, x2)

    mem = ExitStack()
    v1 = sb(mem, "w1_T", [D, E, 2 * HID1])
    vo = sb(mem, "wo_T", [128, 2, D])
    vb = sb(mem, "b1_cols1", [128, E, 4])
    vbo = sb(mem, "bo_rows1", [S, D])
    sel = sb(mem, "expert_rows", [3 * E, E, 128], BF16)
    comb = sb(mem, "comb", [S, CB, E])
    cw = sb(mem, "comb_work", [S, 6, CB, E])
    csum = sb(mem, "comb_sum", [S, 4, CB])
    cparts = sb(mem, "comb_parts", [S, CB, 3, E], BF16)
    cT = sb(mem, "comb_T", [3 * E, 2, CT], BF16)
    cb_sb = sb(mem, "comb_rows", [128, 3, CT])
    sg = sb(mem, "sigmoid", [128, 3, CT])
    ga = sb(mem, "gated", [128, 3, CT])
    gw = sb(mem, "weighted", [128, 3, CT])
    acc = sb(mem, "gated_sum", [128, 2, 2, CT])
    vin = load("ld_f1", v1[:, 0:4], t["f1_w1"][:, 0:4])
    for dst, src in ((v1[:, 4:8], t["f1_w1"][:, 4:8]), (vo[:], t["f1_wo"]), (vb[:], t["f1_b1"]), (vbo[:], t["f1_bo"].partition_broadcast(S)), (sel[:], t["sel"])):
        vin = load("ld_f1", dst, src)
    tb = dve.put(lambda e: e.tensor_scalar(vbo[:], vbo[:], tg_f[:, 1:2], None, ALU.mult), [vin], sig("f_bo"))
    G = {}
    A_BANKS, B_BANKS, C_BANKS = (0, 1), (2, 3), (4, 5)
    outs = []
    units = [0]

    def feed(c):
        k, norm, lnT = layernorm(c, x_done[c])
        ln["rows_free"][k] = (sig("ln_T"), sig("ln_T").value)
        mm, top, hot = choose(1, c, lnT, k)
        V = lambda fn, after: dve.put(fn, after, sig("c_v"))
        a = V(lambda e: e.tensor_tensor(cw[:, 0], lg[:], mx8[:, :, 0:1].broadcast_to([S, CB, E]), ALU.subtract), [top, hot])
        a = V(lambda e: e.tensor_tensor(csum[:, 0, :], mx8[:, :, 1], mx8[:, :, 0], ALU.subtract), [a])
        act.put(lambda e: e.activation(cw[:, 1], cw[:, 0], ACT.Exp), [a], sig("c_exp"))
        ex = act.put(lambda e: e.activation(csum[:, 1, :], csum[:, 0, :], ACT.Exp), [a], sig("c_exp"))
        a = V(lambda e: e.tensor_reduce(csum[:, 2, :], cw[:, 1], AX_X, ALU.add), [ex])
        a = V(lambda e: e.scalar_tensor_tensor(csum[:, 2, :], csum[:, 2, :], EPS_GATE, csum[:, 1, :], ALU.mult, ALU.add), [a])
        a = V(lambda e: e.tensor_scalar(csum[:, 2, :], csum[:, 2, :], 1.0, None, ALU.add), [a])
        a = V(lambda e: e.reciprocal(csum[:, 3, :], csum[:, 2, :]), [a])
        G["x_free"] = R["gate"] = a
        a = V(lambda e: e.tensor_tensor(cw[:, 2], oh[:, 1], csum[:, 1, :].rearrange("p (b o) -> p b o", o=1).broadcast_to([S, CB, E]), ALU.mult), [a])
        a = V(lambda e: e.tensor_tensor(cw[:, 3], cw[:, 2], oh[:, 0], ALU.add), [a])
        a = V(lambda e: e.tensor_tensor(comb[:], cw[:, 3], csum[:, 3, :].rearrange("p (b o) -> p b o", o=1).broadcast_to([S, CB, E]), ALU.mult), [a])
        cs = V(lambda e: e.tensor_reduce(csum[:, 0, :], comb[:], AX_X, ALU.add), [a])
        a = V(lambda e: e.tensor_copy(cparts[:, :, 0, :], comb[:]), [a, G.get("cT_mm")])
        a = V(lambda e: e.tensor_tensor(cw[:, 4], comb[:], cparts[:, :, 0, :], ALU.subtract), [a])
        a = V(lambda e: e.tensor_copy(cparts[:, :, 1, :], cw[:, 4]), [a])
        a = V(lambda e: e.tensor_tensor(cparts[:, :, 2, :], cw[:, 4], cparts[:, :, 1, :], ALU.subtract), [a])
        for b in range(CB):
            xb = V(lambda e, b=b: e.scalar_tensor_tensor(x[:, c * CB + b, :], vbo[:], csum[:, 0, b:b + 1], x[:, c * CB + b, :], ALU.mult, ALU.add), [cs, norm, tb])
        m, bank = misc_bank()
        bank_b = bank[0:3 * E, 0:CT // 2].bitcast(BF16)
        for b in range(CB):
            tr = pe.put(lambda e, b=b: e.transpose(bank_b[:, b * S:(b + 1) * S], cparts[:, b].rearrange("p s e -> p (s e)"), ident_b),
                        [a, misc["free"][m]], sig("c_T"))
        G["cT_mm"] = tr
        ct = misc["free"][m] = act.put(lambda e: e.copy(cT[:, c % 2, :], bank_b), [tr, G.get(("cT", c % 2))], sig("c_T_out"))
        for e_ in range(E):
            u3 = (c * E + e_) % 3
            cbank = ps[:, C_BANKS[e_ % 2], :]
            mm = pe.put(lambda e, e_=e_, cbank=cbank: e.matmul(cbank, sel[:, e_, :], cT[:, c % 2, :], start=True, stop=True),
                        [ct, vin, G.get(("C", e_ % 2))], sig("f_comb"))
            cbm = G[("C", e_ % 2)] = act.put(lambda e, u3=u3, cbank=cbank: e.copy(cb_sb[:, u3, :], cbank), [mm, G.get(("cb", u3))], sig("f_comb_out"))
            for hc in range(2):
                s3, s2_ = units[0] % 3, units[0] % 2
                units[0] += 1
                abank, bbank = ps[:, A_BANKS[s2_], :], ps[:, B_BANKS[s2_], :]
                mb = pe.put(lambda e, e_=e_, hc=hc, bbank=bbank: e.matmul(bbank, v1[:, e_, HID1 + hc * 128:HID1 + (hc + 1) * 128], xnT[:, k, :], start=True, stop=True),
                            [lnT, vin, G.get(("B", s2_))], sig("f_up"))
                G[("B", s2_)] = sgm = act.put(lambda e, e_=e_, hc=hc, bbank=bbank, s3=s3: e.activation(sg[:, s3, :], bbank, ACT.Sigmoid, bias=vb[:, e_, 2 + hc:3 + hc]),
                                              [mb, G.get(("sg", s3))], sig("f_sig"))
                ma = pe.put(lambda e, e_=e_, hc=hc, abank=abank: e.matmul(abank, v1[:, e_, hc * 128:(hc + 1) * 128], xnT[:, k, :], start=True, stop=True),
                            [G.get(("A", s2_))], sig("f_up"))
                gm = G[("A", s2_)] = G[("sg", s3)] = dve.put(
                    lambda e, e_=e_, hc=hc, abank=abank, s3=s3: e.scalar_tensor_tensor(ga[:, s3, :], abank, vb[:, e_, hc:hc + 1], sg[:, s3, :], ALU.add, ALU.mult),
                    [ma, sgm, G.get(("ga", s3))], sig("f_gated"))
                if e_ == 0:
                    G[("ga", s3)] = G[("acc", hc)] = dve.put(lambda e, u3=u3, s3=s3, hc=hc: e.tensor_tensor(acc[:, c % 2, hc, :], ga[:, s3, :], cb_sb[:, u3, :], ALU.mult),
                                                             [gm, cbm, G.get(("accfree", c % 2))], sig("f_weighted"))
                    wm = G[("ga", s3)]
                else:
                    wm = G[("ga", s3)] = dve.put(lambda e, u3=u3, s3=s3: e.tensor_tensor(gw[:, s3, :], ga[:, s3, :], cb_sb[:, u3, :], ALU.mult),
                                                 [gm, cbm, G.get(("gw", s3))], sig("f_weighted"))
                    G[("gw", s3)] = G[("acc", hc)] = pool.put(lambda e, s3=s3, hc=hc: e.tensor_tensor(acc[:, c % 2, hc, :], acc[:, c % 2, hc, :], gw[:, s3, :], ALU.add),
                                                              [wm, G[("acc", hc)]], sig("f_sum"))
                G[("cb", u3)] = wm
        G[("cT", c % 2)] = mm
        ln["T_free"][k] = ma
        m, bank = misc_bank()
        for b in range(CB):
            for hc in range(2):
                mo = pe.put(lambda e, b=b, hc=hc: e.matmul(bank[:, b * D:(b + 1) * D], acc[:, c % 2, hc, b * S:(b + 1) * S], vo[:, hc, :], start=(hc == 0), stop=(hc == 1)),
                            [G[("acc", 0)], G[("acc", 1)], misc["free"][m]], sig("f_out"))
        G[("accfree", c % 2)] = mo
        xs = x[:, c * CB:(c + 1) * CB, :]
        fin = misc["free"][m] = dve.put(lambda e, xs=xs, bank=bank: e.scalar_tensor_tensor(xs, bank.rearrange("p (b d) -> p b d", b=CB), tg_f[:, 1:2], xs, ALU.mult, ALU.add),
                                        [mo, xb], sig("f_x"))
        outs.append(load("out", out[:, c * CB:(c + 1) * CB, :], xs, [fin]))

    for c in range(NCH):
        feed(c)
    sp.put(None, [outs[-1]])
    fence()

    with nc.Block() as block:
        block.tensor(pe.play)
        block.scalar(act.play)
        block.vector(dve.play)
        block.gpsimd(pool.play)
        block.sync(sp.play)
    mem.close()
    rt.close()
    top.close()


def kernel(**inputs):
    import numpy as np
    import concourse.bacc as bacc
    from concourse import mybir as mb
    from concourse.bass_utils import run_bass_kernel_spmd

    a = {k: np.asarray(v) for k, v in inputs.items()}
    c = np.ascontiguousarray
    bf = mb.dt.np(mb.dt.bfloat16) if hasattr(mb.dt, "np") else None
    import ml_dtypes
    bf = ml_dtypes.bfloat16
    f = np.float32
    eye = np.eye(128)
    sel = np.zeros((3, E, E, 128))
    for e in range(E):
        sel[:, e, e, :] = 1.0
    arrays = {
        "x": c(a["x"].transpose(1, 0, 2)),
        "ctxT": c(a["ctx_1024"].reshape(B * S2, D).T),
        "groupT": c(a["fside_BxSxS2_0"].transpose(2, 0, 1)),
        "mask0": c(a["mask_BxSxS2_ik1"].transpose(1, 0, 2)),
        "mask0T": c(a["mask_BxSxS2_ik1"].transpose(2, 0, 1)),
        "mask1": c(a["mask_1x1xSxS2_bk1"][0, 0]),
        "mask1T": c(a["mask_1x1xSxS2_bk1"][0, 0].T),
        "wq": c(np.stack([a["L0_xattn_wq_k"], a["L1_xattn_w_q"].T], 1)),
        "wk": c(np.stack([a["L0_xattn_wk_k"], a["L1_xattn_w_k"].T], 1)),
        "wv": c(np.stack([a["L0_xattn_wv_k"], a["L1_xattn_w_v"].T], 1)),
        "wo": c(np.stack([a["L0_xattn_wo_k"], a["L1_xattn_w_o"].T], 1)),
        "cols": c(np.stack([a["L0_xattn_wq_b"], a["L0_xattn_wk_b"], a["L1_xattn_b_q"], a["L1_xattn_b_k"]], 1)),
        "bv": c(np.stack([a["L0_xattn_wv_b"], a["L1_xattn_b_v"]])),
        "bo": c(np.stack([a["L0_xattn_wo_b"], a["L1_xattn_b_o"]])),
        "g": c(np.concatenate([a["g_xattn"], a["g_ffn"]])),
        "wg": c(np.stack([a["L0_ffn_Wg"], a["L1_ffn_Wg"].T], 1)),
        "w1": c(a["L0_ffn_W1"].transpose(1, 0, 2)),
        "b1": c(a["L0_ffn_b1"].reshape(E, HID0 // 128, 128).transpose(2, 0, 1)),
        "w2": c(a["L0_ffn_W2"].reshape(E, HID0 // 128, 128, D).transpose(2, 0, 1, 3)),
        "b2": c(a["L0_ffn_b2"]),
        "f1_w1": c(a["L1_ffn_W1"].transpose(2, 0, 1)),
        "f1_b1": c(a["L1_ffn_b1"].reshape(E, 4, 128).transpose(2, 0, 1)),
        "f1_wo": c(a["L1_ffn_Wo"].T.reshape(2, 128, D).transpose(1, 0, 2)),
        "f1_bo": c(a["L1_ffn_bo"]),
        "ident": eye.astype(f),
        "cbf": c(np.concatenate([eye, np.triu(np.ones((128, 128)), 1), np.ones((128, 128))], 1)).astype(bf),
        "iota8": c(np.tile(np.arange(E), (128, 1))).astype(f),
        "ones": np.ones((3, PAIRS, CK)).astype(bf),
        "zeros": np.zeros((SPARE, PAIRS, CT)).astype(bf),
        "sel": sel.reshape(3 * E, E, 128).astype(bf),
    }
    nc = bacc.Bacc("TRN2", target_bir_lowering=False, num_devices=1)
    t = {k: nc.dram_tensor(f"in_{k}", v.shape, mb.dt.from_np(v.dtype), kind="ExternalInput").ap() for k, v in arrays.items()}
    out = nc.dram_tensor("out_x", (S, B, D), F32, kind="ExternalOutput").ap()
    scratch = {
        "q": nc.dram_tensor("scratch_q", (NCH, H, 3, DH, CT), BF16, kind="Internal").ap(),
        "k": nc.dram_tensor("scratch_k", (NCH, H, 6, DH, CK), BF16, kind="Internal").ap(),
        "shift": nc.dram_tensor("scratch_shift", (B, 3 * H, S), BF16, kind="Internal").ap(),
        "xe": nc.dram_tensor("scratch_xe", (SLOTS, D), F32, kind="Internal").ap(),
        "y": nc.dram_tensor("scratch_y", (SLOTS, D), F32, kind="Internal").ap(),
    }
    flamingo(nc, t, out, scratch)
    r = run_bass_kernel_spmd(nc, [{f"in_{k}": v for k, v in arrays.items()}], core_ids=[0])
    return c(r.results[0]["out_x"].transpose(1, 0, 2))
```

```python
from contextlib import ExitStack

import concourse.bass as bass
from concourse import mybir

B, S, S2, D = 32, 128, 120, 128
H = 16
DH = D // H
E = 8
HID0 = 512
HID1 = 256
TOPK = 2
TOKENS = B * S
CAP = -(-TOKENS * TOPK * 105 // (E * 100))
SLOTS = E * CAP

CB = 4
NCH = B // CB
CT = CB * S
CK = CB * S2
RING = 3
PAIRS = H // 2
HALF = 64
Q_SLOTS = (0, 1, 2, 0, 1, 0)
K_SLOTS = (0, 0, 0, 1, 1, 2)
SLOT_ROWS = 6 * DH
SHIFT_ROW = SLOT_ROWS
SPARE = HALF - SLOT_ROWS
EPS_LN = 1e-5
EPS_GATE = 1e-9
SCALE = 1.0 / float(DH) ** 0.5
NEG_ADD = -998244352.0
NEG_SET = -float(2 ** 100)
SKIP = float(2 ** 20)

ALU = mybir.AluOpType
ACT = mybir.ActivationFunctionType
F32 = mybir.dt.float32
F32R = mybir.dt.float32r
BF16 = mybir.dt.bfloat16
I32 = mybir.dt.int32
U32 = mybir.dt.uint32
U8 = mybir.dt.uint8
AX_X = mybir.AxisListType.X


class Signal:

    def __init__(self, handle):
        self.handle, self.value = handle, 0


class Line:

    def __init__(self):
        self.items = []

    def put(self, emit, after=(), sig=None, by=1):
        self.items.append((emit, tuple(after), sig, by))
        if sig is None:
            return None
        sig.value += by
        return (sig, sig.value)

    def play(self, eng):
        waited = {}
        for emit, after, sig, by in self.items:
            for mark in after:
                if mark is not None and waited.get(id(mark[0]), 0) < mark[1]:
                    eng.wait_ge(mark[0].handle, mark[1])
                    waited[id(mark[0])] = mark[1]
            ins = emit(eng) if emit is not None else None
            if sig is not None:
                ins.then_inc(sig.handle, by)


def flamingo(nc, t, out, scratch):
    top = ExitStack()
    pe, act, dve, pool, sp = Line(), Line(), Line(), Line(), Line()
    signals = {}

    def sig(name):
        if name not in signals:
            signals[name] = Signal(top.enter_context(nc.semaphore(name)))
        return signals[name]

    def sb(stack, name, shape, dt=F32):
        return stack.enter_context(nc.sbuf_tensor(name, shape, dt))

    def load(name, dst, src, after=(), line=None):
        return (line or sp).put(lambda e: e.dma_start(dst, src), after, sig(name), 16)

    def fence():
        marks = [(s, s.value) for s in signals.values() if s.value]
        for line in (pe, act, dve, pool, sp):
            line.put(None, marks)

    x = sb(top, "x_rows", [S, B, D])
    ctxT = sb(top, "ctx_T", [D, B * S2])
    wq = sb(top, "wq", [D, 2, D])
    wk = sb(top, "wk", [D, 2, D])
    wv = sb(top, "wv", [D, 2, D])
    wo = sb(top, "wo", [D, 2, D])
    cols = sb(top, "bias_cols", [D, 4])
    bv = sb(top, "bv_rows", [S, 2, D])
    bo = sb(top, "bo_rows", [S, 2, D])
    tg_x = sb(top, "tanh_g_xattn", [S, 2])
    tg_f = sb(top, "tanh_g_ffn", [S, 2])
    g_in = sb(top, "g_in", [S, 4])
    ident = sb(top, "ident", [128, 128])
    cbf = sb(top, "const_bf16", [128, 3 * 128], BF16)
    ident_b, tri_b, ones_b = cbf[:, 0:128], cbf[:, 128:256], cbf[:, 256:384]
    iota8 = sb(top, "iota8", [128, E])
    wg = sb(top, "wg", [D, 2, E])
    half_c = sb(top, "minus_half", [128, CB])
    xn = sb(top, "xn_rows", [S, 3, CB, D])
    xnT = sb(top, "xn_T", [D, 2, CT])
    stats = sb(top, "ln_stats", [S, 2, CB, 6])
    mv = sb(top, "ln_mean_var", [S, 2, CB, 2])
    rs = sb(top, "ln_rstd", [S, 2, 6, CB])
    slot_w = sb(top, "slot_weight", [S, TOPK, B])
    slot_put = sb(top, "slot_put", [S, TOPK, B], I32)
    slot_get = sb(top, "slot_get", [S, TOPK, B], I32)

    ps = top.enter_context(nc.psum_tensor("psum", [128, 8, 512], F32))
    ps_b = ps.bitcast(BF16) if hasattr(ps, "bitcast") else None

    for name, dst, src in (("ld_w", wq, "wq"), ("ld_w", wk, "wk"), ("ld_w", wv, "wv"), ("ld_w", wo, "wo"),
                           ("ld_w", cols, "cols"), ("ld_w", ident, "ident"), ("ld_w", cbf, "cbf"),
                           ("ld_w", iota8, "iota8"), ("ld_w", wg, "wg")):
        load(name, dst[:], t[src])
    load("ld_w", bv[:], t["bv"].partition_broadcast(S))
    load("ld_w", bo[:], t["bo"].partition_broadcast(S))
    weights_in = load("ld_w", g_in[:], t["g"].partition_broadcast(S))
    x_in, ctx_in = [], []
    for c0, c1 in ((0, 1), (1, NCH)):
        for c in range(c0, c1):
            x_in.append(load(f"ld_x{c0}", x[:, c0 * CB:c1 * CB, :], t["x"][:, c0 * CB:c1 * CB, :]) if c == c0 else x_in[-1])
            ctx_in.append(load(f"ld_c{c0}", ctxT[:, c0 * CK:c1 * CK], t["ctxT"][:, c0 * CK:c1 * CK]) if c == c0 else ctx_in[-1])

    act.put(lambda e: e.activation(tg_x[:, :], g_in[:, 0:2], ACT.Tanh), [weights_in], sig("tanh"))
    tanh_done = act.put(lambda e: e.activation(tg_f[:, :], g_in[:, 2:4], ACT.Tanh), (), sig("tanh"))
    const_done = pool.put(lambda e: e.memset(half_c[:], -0.5), (), sig("const"))
    for j in (0, 2):
        cols_done = dve.put(lambda e, j=j: e.tensor_scalar(cols[:, j:j + 1], cols[:, j:j + 1], SCALE, None, ALU.mult),
                            [weights_in], sig("cols"))
    for l in range(2):
        bo_done = dve.put(lambda e, l=l: e.tensor_scalar(bo[:, l, :], bo[:, l, :], tg_x[:, l:l + 1], None, ALU.mult),
                          [tanh_done], sig("bo"))

    misc = {"n": 0, "free": [None, None]}
    MISC = (6, 7)

    def misc_bank():
        k = misc["n"] % 2
        misc["n"] += 1
        return k, ps[:, MISC[k], :]

    ln = {}

    def layernorm(who, slot, c, ready):
        st, m_v, r_s = stats[:, who], mv[:, who], rs[:, who]
        for b in range(CB):
            m = dve.put(lambda e, b=b: e.bn_stats(st[:, b, :], x[:, c * CB + b, :]), [ready, ln.get(("agg", who))], sig("ln_stats"))
        for b in range(CB):
            agg = dve.put(lambda e, b=b: e.bn_aggr(m_v[:, b, :], st[:, b, :]), [m, ln.get(("shift", who))], sig("ln_aggr"))
        ln[("agg", who)] = agg
        yield
        ops = [
            lambda e: e.tensor_scalar(r_s[:, 0, :], m_v[:, :, 1], EPS_LN, None, ALU.add),
            lambda e: e.tensor_tensor(r_s[:, 1, :], r_s[:, 0, :], half_c[:, :], ALU.pow),
            lambda e: e.tensor_tensor(r_s[:, 2, :], r_s[:, 1, :], r_s[:, 1, :], ALU.mult),
            lambda e: e.tensor_tensor(r_s[:, 3, :], r_s[:, 2, :], r_s[:, 0, :], ALU.mult),
            lambda e: e.tensor_scalar(r_s[:, 2, :], r_s[:, 3, :], -0.5, 1.5, ALU.mult, ALU.add),
            lambda e: e.tensor_tensor(r_s[:, 4, :], r_s[:, 1, :], r_s[:, 2, :], ALU.mult),
            lambda e: e.tensor_tensor(r_s[:, 5, :], r_s[:, 4, :], m_v[:, :, 0], ALU.mult),
            lambda e: e.tensor_scalar(r_s[:, 5, :], r_s[:, 5, :], -1.0, None, ALU.mult),
        ]
        r = [agg, ln.get(("norm", who)), const_done]
        for op in ops:
            r = [pool.put(op, r, sig("ln_rstd"))]
        ln[("shift", who)] = r[0]
        yield
        for b in range(CB):
            norm = act.put(lambda e, b=b: e.activation(xn[:, slot, b, :], x[:, c * CB + b, :], ACT.Identity,
                                                       bias=r_s[:, 5, b:b + 1], scale=r_s[:, 4, b:b + 1]),
                           r + [ln.get(("rows_free", slot))], sig("ln_norm"))
        ln[("norm", who)] = norm
        yield
        m, bank = misc_bank()
        for b in range(CB):
            tr = pe.put(lambda e, b=b: e.transpose(bank[:, b * S:(b + 1) * S], xn[:, slot, b, :], ident[:, :]),
                        [norm, misc["free"][m], weights_in], sig("ln_T"))
        ln[("rows_free", slot)] = tr
        ln[("T", who)] = misc["free"][m] = act.put(lambda e: e.copy(xnT[:, who, :], bank), [tr, ln.get(("T_free", who))], sig("ln_T_out"))
        yield

    def finish(task):
        for _ in task:
            pass

    def attention(l, bring, after_chunk):
        mem = ExitStack()
        buf = lambda name, shape, dt=F32: sb(mem, f"{name}{l}", shape, dt)
        v_rows = buf("v_rows", [S2, 2, CB, D])
        full = buf("full", [D, 2, CT])
        parts = buf("parts", [D, 2, 3, CT], BF16)
        qop = buf("q_operand", [128, RING, PAIRS, CT], BF16)
        kop = buf("k_operand", [128, RING, PAIRS, 2, CK], BF16)
        neg = buf("neg_rows", [S, 2, CB, S2], BF16)
        negT = buf("neg_cols", [S2, 2, CB, S], BF16)
        shift = buf("shift", [S, 2, H])
        rest = buf("shift_rest", [S, 2, H])
        sparts = buf("shift_parts", [S, 2, 3, H], BF16)
        spT = buf("shift_parts_T", [3 * H, 2, S], BF16)
        expT = buf("exp_T", [S2, 2, H, S])
        vx = buf("v_spread", [S2, 2, 4 * 128])
        onesx = buf("ones_spread", [S2, 4, 32])
        rden = buf("rden", [D, S])
        oT = buf("o_T", [D, 2, S])
        if l == 0:
            m_in = buf("mask_in", [S, CB, S2], I32)
            mT_in = buf("maskT_in", [S2, CB, S], I32)
            gT = buf("group_T", [S2, 2, CB, S])
            expG = buf("exp_G", [S2, 2, H, S])
        else:
            m_in = buf("mask_in", [S, S2], U8)
            mT_in = buf("maskT_in", [S2, S], U8)
        q_dram, k_dram, s_dram = scratch["q"], scratch["k"], scratch["shift"]
        n = lambda name: name

        z = []
        for r in range(RING):
            line = (dve, pool)[r % 2]
            z.append(line.put(lambda e, r=r: e.memset(kop[:, r].rearrange("p a b c -> p (a b c)").bitcast(U32), 0), (), sig(n(f"zero{r % 2}_"))))
        ones_in = []
        for r in range(RING):
            for i in range(2):
                m = load(n("ones_row"), kop[HALF * i + SHIFT_ROW:HALF * i + SHIFT_ROW + 3, r, :, i, :],
                         t["ones"][0:3], [z[r]])
        ones_in = m
        a = pool.put(lambda e: e.memset(vx[:], 0.0), (), sig(n("spread0")))
        a = pool.put(lambda e: e.memset(onesx[:], 0.0), (), sig(n("spread0")))
        for g in range(4):
            spread = pool.put(lambda e, g=g: e.memset(onesx[:, g, 8 * g:8 * g + 8], 1.0), [a], sig(n("spread1")))

        free = {}
        q_ready, k_ready, v_ready, neg_ready, g_ready = {}, {}, {}, {}, {}

        def masks(c):
            k = c % 2
            if l == 1:
                if c == 0:
                    a = load(n("mask"), m_in[:], t["mask1"])
                    a = load(n("mask"), mT_in[:], t["mask1T"])
                    pool.put(lambda e: e.tensor_scalar(neg[:, 0, 0, :], m_in[:], NEG_SET, None, ALU.mult), [a], sig(n("neg")))
                    neg_ready[0] = pool.put(lambda e: e.tensor_scalar(negT[:, 0, 0, :], mT_in[:], NEG_SET, None, ALU.mult), (), sig(n("neg")))
                neg_ready[c] = neg_ready[0]
                return
            sl = slice(c * CB, (c + 1) * CB)
            a = load(n("mask"), m_in[:], t["mask0"][:, sl, :], [free.get("m_in")])
            a = load(n("mask"), mT_in[:], t["mask0T"][:, sl, :], [free.get("m_in")])
            g_ready[c] = load(n(f"group{k}_"), gT[:, k], t["groupT"][:, sl, :], [free.get(("g", k))])
            pool.put(lambda e: e.tensor_scalar(neg[:, k], m_in[:], -NEG_ADD, NEG_ADD, ALU.mult, ALU.add),
                     [a, free.get(("neg", k))], sig(n("neg")))
            neg_ready[c] = free["m_in"] = pool.put(
                lambda e: e.tensor_scalar(negT[:, k], mT_in[:], -NEG_ADD, NEG_ADD, ALU.mult, ALU.add),
                [free.get(("negT", k))], sig(n("neg")))

        def split(k, width, made, dram, slots, name):
            f, p = full[:, k, 0:width], parts[:, k, :, 0:width]
            a = act.put(lambda e: e.copy(p[:, 0, :], f), [made, free.get(("parts", k))], sig(n("part0")))
            yield
            a = pool.put(lambda e: e.tensor_tensor(f, f, p[:, 0, :], ALU.subtract), [a], sig(n("left")))
            yield
            a = act.put(lambda e: e.copy(p[:, 1, :], f), [a], sig(n("part1")))
            yield
            a = pool.put(lambda e: e.tensor_tensor(p[:, 2, :], f, p[:, 1, :], ALU.subtract), [a], sig(n("left")))
            free[("full", k)] = a
            yield
            for slot in slots:
                part = Q_SLOTS[slot] if k == 0 else K_SLOTS[slot]
                w = load(n(f"{name}_out"), dram[:, slot], p[:, part, :], [a])
            free[("parts", k)] = live[("split", k)] = w

        def project(c, which, src, src_ready, w, bias_col, scale, width):
            m, bank = misc_bank()
            k = which
            mm = pe.put(lambda e: e.matmul(bank[:, 0:width], w[:, l, :], src, start=True, stop=True),
                        [src_ready, misc["free"][m], weights_in], sig(n("project")))
            made = misc["free"][m] = act.put(
                lambda e: e.activation(full[:, k, 0:width], bank[:, 0:width], ACT.Identity,
                                       bias=cols[:, bias_col:bias_col + 1], scale=scale), [mm, free.get(("full", k)), cols_done], sig(n("projected")))
            return mm, made

        def prep_q(c):
            yield from bring(c)
            yield from layernorm(0, 0, c, x_ready[c])
            mm, made = project(c, 0, xnT[:, 0, :], ln[("T", 0)], wq, 2 * l, SCALE, CT)
            ln[("T_free", 0)] = mm
            for b in range(CB):
                xb = pool.put(lambda e, b=b: e.tensor_tensor(x[:, c * CB + b, :], x[:, c * CB + b, :], bo[:, l, :], ALU.add),
                              [ln[("norm", 0)], bo_done], sig(n("x_bias")))
            x_biased[c] = xb
            yield
            yield from split(0, CT, made, q_dram[c], range(3), "q")
            w = live[("split", 0)]
            r = c % RING
            for i in range(2):
                of_head = q_dram[c].rearrange("(t i) s d n -> i (s d) t n", i=2)[i]
                for s0, s1, src0 in ((0, 3, 0), (3, 5, 0), (5, 6, 0)):
                    load(n(f"q_in{r}_"), qop[HALF * i + s0 * DH:HALF * i + s1 * DH, r, :, :],
                         of_head[src0 * DH:(src0 + s1 - s0) * DH], [w, free.get(("qop", r))])
                q_ready[c] = load(n(f"q_in{r}_"), qop[HALF * i + SLOT_ROWS:HALF * (i + 1), r, :, :], t["zeros"])

        def prep_k(c):
            mm, made = project(c, 1, ctxT[:, c * CK:(c + 1) * CK], ctx_in[c], wk, 2 * l + 1, 1.0, CK)
            yield
            yield from split(1, CK, made, k_dram[c], range(6), "k")
            w = live[("split", 1)]
            r = c % RING
            for i in range(2):
                of_head = k_dram[c].rearrange("(t i) s d n -> i (s d) t n", i=2)[i]
                k_ready[c] = load(n(f"k_in{r}_"), kop[HALF * i:HALF * i + SLOT_ROWS, r, :, i, :], of_head,
                                  [w, free.get(("qop", r)), ones_in, z[r]])

        def prep_v(c):
            m, bank = misc_bank()
            for b in range(CB):
                mm = pe.put(lambda e, b=b: e.matmul(bank[0:S2, b * D:(b + 1) * D], ctxT[:, (c * CB + b) * S2:(c * CB + b + 1) * S2],
                                                    wv[:, l, :], start=True, stop=True),
                            [misc["free"][m], ctx_in[c]], sig(n("v_project")))
            v_ready[c] = misc["free"][m] = dve.put(
                lambda e: e.tensor_tensor(v_rows[:, c % 2], bank[0:S2, :].rearrange("p (b d) -> p b d", b=CB),
                                          bv[0:S2, l:l + 1, :].broadcast_to([S2, CB, D]), ALU.add),
                [mm, free.get(("v", c % 2))], sig(n("v_rows")))

        BANK_S, BANK_T, BANK_AV = 0, 1, 5
        live = {}

        def scores(i, r):
            c, b = divmod(i, CB)
            k = 0 if l == 1 else c % 2
            bb = 0 if l == 1 else b
            bank = ps[:, BANK_S, 0:4 * S2].rearrange("p (h k) -> p h k", h=4)
            pe.put(lambda e: e.matmul(bank, ident_b, neg[:, k, bb:bb + 1, :].broadcast_to([S, 4, S2]), start=True, stop=False),
                   [free.get("S"), neg_ready[c], q_ready[c], k_ready[c]])
            for u in range(2):
                pt = 2 * r + u
                mm = pe.put(lambda e, u=u, pt=pt: e.matmul(bank[:, 2 * u:2 * u + 2, :], qop[:, c % RING, pt, b * S:(b + 1) * S],
                                                           kop[:, c % RING, pt, :, b * S2:(b + 1) * S2], start=False, stop=(u == 1)),
                            (), sig(n("score")) if u == 1 else None)
            mx = free["S"] = dve.put(lambda e: e.tensor_reduce(shift[:, i % 2, 4 * r:4 * r + 4], bank, AX_X, ALU.max, negate=True),
                                     [mm, free.get(("shift", i % 2))], sig(n("row_max")))
            free[("neg", c % 2)] = mm
            if r == 3:
                live[("scored", i)] = mm
                k2 = i % 2
                sp_ = sparts[:, k2]
                order = lambda a: a.rearrange("p (t i) -> p i t", i=2)
                by_part = sp_.rearrange("p s h -> p (s h)").rearrange("p (i s t) -> p i s t", i=2, s=3)
                to = lambda j: by_part[:, :, j, :]
                a = pool.put(lambda e: e.tensor_scalar(to(0), order(shift[:, k2]), 1.0, None, ALU.mult), [mx, free.get(("sparts", k2))], sig(n("shift_part")))
                a = pool.put(lambda e: e.tensor_tensor(order(rest[:, k2]), order(shift[:, k2]), to(0), ALU.subtract), [a], sig(n("shift_part")))
                a = pool.put(lambda e: e.tensor_scalar(to(1), order(rest[:, k2]), 1.0, None, ALU.mult), [a], sig(n("shift_part")))
                a = pool.put(lambda e: e.tensor_tensor(to(2), order(rest[:, k2]), to(1), ALU.subtract), [a], sig(n("shift_part")))
                free[("shift", k2)] = live[("sparts", i)] = a

        def shift_rows(i):
            c, b = divmod(i, CB)
            k2 = i % 2
            m, bank = misc_bank()
            bank_b = bank[0:3 * H, 0:S // 2].bitcast(BF16)
            tr = free[("sparts", k2)] = pe.put(lambda e: e.transpose(bank_b, sparts[:, k2].rearrange("p s h -> p (s h)"), ident_b),
                                               [live[("sparts", i)], misc["free"][m]], sig(n("shift_T")))
            cp = misc["free"][m] = act.put(lambda e: e.copy(spT[:, k2, :], bank_b), [tr, free.get(("spT", k2))], sig(n("shift_T_out")))
            w = free[("spT", k2)] = load(n(f"shift_out{k2}_"), s_dram[i], spT[:, k2, :], [cp])
            for par in range(2):
                src = s_dram[i][par * 3 * PAIRS:(par + 1) * 3 * PAIRS, :].rearrange("(s t) q -> s t q", s=3)
                live[("shift", i)] = load(n(f"shift_in{i % 4}_"), qop[HALF * par + SHIFT_ROW:HALF * par + SHIFT_ROW + 3, c % RING, :, b * S:(b + 1) * S],
                                          src, [w, live[("scored", i)]])

        def weights(i, p):
            c, b = divmod(i, CB)
            k = 0 if l == 1 else c % 2
            bb = 0 if l == 1 else b
            for half in range(2):
                bank = ps[0:S2, BANK_T + 2 * p + half, :]
                pe.put(lambda e, bank=bank: e.matmul(bank.rearrange("p (h q) -> p h q", h=4), ident_b[0:S2, 0:S2],
                                                     negT[:, k, bb:bb + 1, :].broadcast_to([S2, 4, S]), start=True, stop=False),
                       [free.get(("T", p)), live[("shift", i)]])
                for u in range(4):
                    h = 8 * p + 4 * half + u
                    mm = pe.put(lambda e, bank=bank, u=u, h=h: e.matmul(
                        bank[:, u * S:(u + 1) * S], kop[:, c % RING, h // 2, h % 2, b * S2:(b + 1) * S2],
                        qop[:, c % RING, h // 2, b * S:(b + 1) * S], start=False, stop=(u == 3)),
                        (), sig(n("logit_T")) if half == 1 and u == 3 else None)
            free[("negT", c % 2)] = mm
            free[("qop", c % RING)] = mm
            k2 = i % 2
            src = ps[0:S2, BANK_T + 2 * p:BANK_T + 2 * p + 2, :].rearrange("p a (h q) -> p (a h) q", h=4)
            ex = free[("T", p)] = act.put(lambda e: e.activation(expT[:, k2, 8 * p:8 * p + 8, :], src, ACT.Exp),
                                          [mm, free.get(("expT", k2))], sig(n("exp")))
            live[("exp", i, p)] = ex

        def gate(i, p):
            if l == 1:
                return
            c, b = divmod(i, CB)
            k2 = i % 2
            for line, name, h0, h1 in ((dve, "gate_v", 8 * p, 8 * p + 6), (pool, "gate_p", 8 * p + 6, 8 * p + 8)):
                live[(name, i, p)] = line.put(lambda e, h0=h0, h1=h1: e.tensor_tensor(
                    expG[:, k2, h0:h1, :], expT[:, k2, h0:h1, :], gT[:, c % 2, b:b + 1, :].broadcast_to([S2, h1 - h0, S]), ALU.mult),
                    [live[("exp", i, p)], g_ready[c], free.get(("expG", k2))], sig(n(name)))
            if b == CB - 1 and p == 1:
                free[("g", c % 2)] = live[("gate_v", i, 1)]
                free[("g2", c % 2)] = live[("gate_p", i, 1)]

        def spread_v(i):
            c, b = divmod(i, CB)
            dst = vx[:, i % 2, :]
            dst = bass.AP(dst.tensor, dst.offset, [list(dst.ap[0]), [128, 4], [40, 4], [1, DH]])
            a = pool.put(lambda e: e.tensor_scalar(dst, v_rows[:, c % 2, b, :].rearrange("p (j g d) -> p j g d", j=4, g=4), 1.0, None, ALU.mult),
                         [v_ready[c], spread, free.get(("vx", i % 2))], sig(n("spread_v")))
            live[("vx", i)] = a
            free[("v", c % 2)] = a

        def out_part(i, g_lo, g_hi, den):
            k2 = i % 2
            src = expT if den or l == 1 else expG
            for g in range(g_lo, g_hi):
                for j in range(4):
                    h = 4 * j + g
                    lhs = onesx[:, g, :] if den else vx[:, k2, h * 32:(h + 1) * 32]
                    dst = ps[32 * j:32 * j + 32, BANK_AV, (S if den else 0):(2 * S if den else S)]
                    after = [live[("exp", i, 0)], live[("exp", i, 1)], live[("vx", i)], free.get("AV")]
                    if not den and l == 0:
                        after += [live[(nm, i, p)] for nm in ("gate_v", "gate_p") for p in range(2)]
                    mm = pe.put(lambda e, lhs=lhs, dst=dst, h=h, g=g: e.matmul(dst, lhs, src[:, k2, h, :],
                                                                         start=(g == 0 and not den), stop=(g == 3),
                                                                         skip_group_check=True),
                                after, sig(n("av")) if (g == 3 and j == 3) else None)
            if den:
                free[("expT", k2)] = mm
                live[("den", i)] = mm
            else:
                free[("vx", k2)] = mm
                free[("expG", k2)] = mm

        def normalise(i):
            a = dve.put(lambda e: e.reciprocal(rden[:], ps[:, BANK_AV, S:2 * S]), [live[("den", i)], free.get("rden")], sig(n("rden")))
            live[("oT", i)] = free["AV"] = free["rden"] = dve.put(
                lambda e: e.tensor_tensor(oT[:, i % 2, :], ps[:, BANK_AV, 0:S], rden[:], ALU.mult),
                [a, free.get(("oT", i % 2))], sig(n("o_T")))

        def out_project(i):
            c, b = divmod(i, CB)
            m, bank = misc_bank()
            mm = free[("oT", i % 2)] = pe.put(lambda e: e.matmul(bank[:, 0:D], oT[:, i % 2, :], wo[:, l, :], start=True, stop=True),
                                              [live[("oT", i)], misc["free"][m]], sig(n("out_project")))
            misc["free"][m] = dve.put(lambda e: e.scalar_tensor_tensor(x[:, i, :], bank[:, 0:D], tg_x[:, l:l + 1], x[:, i, :],
                                                                       ALU.mult, ALU.add),
                                      [mm, x_biased[c]], sig(n("x_new")))
            if b == CB - 1:
                x_done[c] = misc["free"][m]

        x_biased, x_done = {}, {}
        for task in (prep_k(0), prep_q(0)):
            finish(task)
        masks(0)
        prep_v(0)
        LAG_T, LAG_AV = 3, 4
        preps, after = [], []

        def step():
            for task in list(preps):
                if next(task, "end") == "end":
                    preps.remove(task)
            if after and next(after[0], "end") == "end":
                after.pop(0)

        for i in range(B + LAG_AV + 1):
            c, b = divmod(i, CB)
            if b == 0:
                for task in preps:
                    finish(task)
                preps = [prep_k(c + 1), prep_q(c + 1)] if c + 1 < NCH else []
            if 0 <= i - LAG_AV - 1 < B:
                normalise(i - LAG_AV - 1)
            for r in range(4):
                if i < B:
                    scores(i, r)
                if r % 2 == 0 and 0 <= i - LAG_T < B:
                    weights(i - LAG_T, r // 2)
                if r == 0 and 0 <= i - LAG_AV - 1 < B:
                    out_project(i - LAG_AV - 1)
                if r == 1 and 0 <= i - 1 < B:
                    shift_rows(i - 1)
                if r == 1 and 0 <= i - LAG_AV < B:
                    out_part(i - LAG_AV, 0, 4, False)
                if r == 1 and 0 <= i - LAG_T < B:
                    spread_v(i - LAG_T)
                    gate(i - LAG_T, 0)
                if r == 3 and 0 <= i - LAG_AV < B:
                    out_part(i - LAG_AV, 0, 4, True)
                if r == 3 and 0 <= i - LAG_T < B:
                    gate(i - LAG_T, 1)
                if r == 3 and c + 1 < NCH:
                    if b == 2:
                        if l == 0 and ("g2", (c + 1) % 2) in free:
                            sp.put(None, [free[("g2", (c + 1) % 2)]])
                        masks(c + 1)
                    if b == 3:
                        prep_v(c + 1)
                step()
            j = i - LAG_AV - 1
            if j >= 0 and j % CB == CB - 1:
                after.append(after_chunk(j // CB, x_done[j // CB]))
        for task in after:
            finish(task)
        fence()
        mem.close()
        return x_done

    rt = ExitStack()
    lg = sb(rt, "r_logits", [S, CB, E])
    mx8 = sb(rt, "r_top", [S, CB, E])
    ix8 = sb(rt, "r_index", [S, CB, E], U32)
    ixf = sb(rt, "r_index_f", [S, TOPK, CB])
    oh = sb(rt, "r_onehot", [S, TOPK, CB, E])
    oh_b = sb(rt, "r_onehot_sum", [S, CB, E], BF16)
    run_b = sb(rt, "r_running", [S, E], BF16)
    run_f = sb(rt, "r_running_f", [S, E])
    tot_f = sb(rt, "r_chunk_total", [S, E])
    prod = sb(rt, "r_prod", [S, TOPK, CB, E])
    pos = sb(rt, "r_pos", [S, TOPK, CB])
    keep = sb(rt, "r_keep", [S, TOPK, CB])
    dest = sb(rt, "r_dest", [S, TOPK, CB])
    tmp = sb(rt, "r_tmp", [S, TOPK, CB])
    gate_e = sb(rt, "r_gate", [S, 3, CB])
    run0 = dve.put(lambda e: e.memset(run_b[:], 0.0), (), sig("r_run"))
    run0 = dve.put(lambda e: e.memset(run_f[:], 0.0), (), sig("r_run"))
    R = {}

    def zero_slots():
        flat = scratch["xe"].rearrange("n d -> (n d)")
        for at in range(0, SLOTS * D, 128 * 1024):
            k = min(1024, (SLOTS * D - at) // 128)
            R["zero"] = load("zero_slots", flat[at:at + k * 128].rearrange("(p n) -> p n", p=128), t["zero_rows"][:, 0:k])


    def choose(l):
        m, bank = misc_bank()
        for b in range(CB):
            mm = pe.put(lambda e, b=b: e.matmul(bank[:, b * E:(b + 1) * E], xnT[:, 1, b * S:(b + 1) * S], wg[:, l, :], start=True, stop=True),
                        [ln[("T", 1)], misc["free"][m]], sig("r_mm"))
        ln[("T_free", 1)] = mm
        a = misc["free"][m] = dve.put(lambda e: e.tensor_copy(lg[:], bank[:, 0:CB * E].rearrange("p (b e) -> p b e", b=CB)), [mm, R.get("lg")], sig("r_v"))
        yield
        for b in range(CB):
            a2 = dve.put(lambda e, b=b: e.max(mx8[:, b, :], lg[:, b, :]), [a, R.get("gate")], sig("r_v"))
        R["top"] = a2
        for b in range(CB):
            a = dve.put(lambda e, b=b: e.max_index(ix8[:, b, :], mx8[:, b, :], lg[:, b, :]), [a2], sig("r_v"))
        yield
        a = dve.put(lambda e: e.tensor_copy(ixf[:], ix8[:, :, 0:TOPK].rearrange("p b k -> p k b")), [a], sig("r_v"))
        for j in range(TOPK):
            R["hot"] = dve.put(lambda e, j=j: e.tensor_tensor(oh[:, j], iota8[:].rearrange("p (o e) -> p o e", o=1).broadcast_to([S, CB, E]),
                                                              ixf[:, j, :].rearrange("p (b o) -> p b o", o=1).broadcast_to([S, CB, E]), ALU.is_equal),
                               [a, weights_in], sig("r_v"))

    def route(c, x_done):
        slot = 1 + c % 2
        yield from layernorm(1, slot, c, x_done)
        yield from choose(0)
        V = lambda fn, after: dve.put(fn, after, sig("r_v"))
        a = V(lambda e: e.tensor_tensor(gate_e[:, 0, :], mx8[:, :, 1], mx8[:, :, 0], ALU.subtract), [R["top"]])
        ex = act.put(lambda e: e.activation(gate_e[:, 1, :], gate_e[:, 0, :], ACT.Exp), [a], sig("r_exp"))
        hot = V(lambda e: e.tensor_tensor(oh_b[:], oh[:, 0], oh[:, 1], ALU.add), [R["hot"]])
        yield
        m, bank = misc_bank()
        for b in range(CB):
            srcs = [(tri_b, oh_b[:, b, :])] + [(ones_b, oh_b[:, j, :]) for j in range(b)] + [(ones_b, run_b[:, :])]
            for s_, (lhs, rhs) in enumerate(srcs):
                mm = pe.put(lambda e, lhs=lhs, rhs=rhs, b=b, s_=s_, n_=len(srcs): e.matmul(
                    bank[:, b * E:(b + 1) * E], lhs, rhs, start=(s_ == 0), stop=(s_ == n_ - 1)),
                    [hot, run0, misc["free"][m]] + ([R["run"]] if "run" in R else []), sig("r_mm"))
        for j in range(TOPK):
            a = V(lambda e, j=j: e.tensor_tensor(prod[:, j], oh[:, j], bank[:, 0:CB * E].rearrange("p (b e) -> p b e", b=CB), ALU.mult), [mm, hot])
        misc["free"][m] = a
        yield
        a = V(lambda e: e.tensor_reduce(pos[:], prod[:], AX_X, ALU.add), [a])
        t1 = V(lambda e: e.tensor_reduce(tot_f[:], oh_b[:].rearrange("p b e -> p e b"), AX_X, ALU.add), [run0])
        g = V(lambda e: e.tensor_scalar(gate_e[:, 2, :], gate_e[:, 1, :], 1.0, None, ALU.add), [ex])
        V(lambda e: e.tensor_scalar(keep[:], pos[:], float(CAP), None, ALU.is_lt), [a])
        a = V(lambda e: e.scalar_tensor_tensor(dest[:], ixf[:], float(CAP), pos[:], ALU.mult, ALU.add), [a])
        t1 = V(lambda e: e.tensor_tensor(run_f[:], run_f[:], tot_f[:], ALU.add), [t1])
        g = V(lambda e: e.reciprocal(gate_e[:, 0, :], gate_e[:, 2, :]), [g])
        yield
        sl = slice(c * CB, (c + 1) * CB)
        V(lambda e: e.tensor_scalar(slot_get[:, :, sl], dest[:], float(SLOTS - 1), None, ALU.min), [a])
        a = V(lambda e: e.tensor_scalar(tmp[:], keep[:], -SKIP, SKIP, ALU.mult, ALU.add), [a])
        R["run"] = V(lambda e: e.tensor_copy(run_b[:], run_f[:]), [t1, mm])
        g = V(lambda e: e.tensor_tensor(gate_e[:, 1, :], gate_e[:, 1, :], gate_e[:, 0, :], ALU.mult), [g])
        put = V(lambda e: e.tensor_tensor(slot_put[:, :, sl], dest[:], tmp[:], ALU.add), [a])
        a = V(lambda e: e.tensor_scalar(tmp[:], keep[:], tg_f[:, 0:1], None, ALU.mult), [put])
        for j in range(TOPK):
            R["w"] = V(lambda e, j=j: e.tensor_tensor(slot_w[:, j, sl], gate_e[:, j, :], tmp[:, j, :], ALU.mult), [a, g])
        R["gate"] = R["lg"] = R["w"]
        yield
        for b in range(CB):
            for j in range(TOPK):
                sc = pool.put(lambda e, b=b, j=j: e.indirect_dma_start(
                    scratch["xe"][:, :], bass.IndirectOffsetOnAxis(slot_put[:, j, c * CB + b:c * CB + b + 1], 0),
                    xn[:, slot, b, :], None, bounds_check=SLOTS - 1, oob_is_err=False),
                    [put, R["zero"]], sig(f"scatter{c % 2}"), 16)
            yield
        R["all"] = R.get("all", []) + [sc]
        ln[("rows_free", slot)] = sc

    x_ready = {}

    def bring_x(c):
        x_ready[c] = x_in[c]
        if c == 1:
            zero_slots()
        return
        yield

    x_done = attention(0, bring_x, route)

    mem = ExitStack()
    w1 = sb(mem, "w1_raw", [D, E, HID0])
    w1h = sb(mem, "w1_high", [D, E, HID0], F32R)
    w1l = sb(mem, "w1_low", [D, E, HID0], F32R)
    w2 = sb(mem, "w2", [128, E, HID0 // 128, D])
    b1 = sb(mem, "b1_cols", [128, E, HID0 // 128])
    b2 = sb(mem, "b2_rows", [128, E, D])
    NC0 = HID0 // 128
    GW = 3 * 128
    groups = [(a, min(GW, CAP - a)) for a in range(0, CAP, GW)]
    xe = sb(mem, "xe_rows", [128, 3, 3, D])
    xeh = sb(mem, "xe_T_high", [D, 2, GW], F32R)
    xel = sb(mem, "xe_T_low", [D, 2, GW], F32R)
    hT = sb(mem, "h_T", [128, 2, NC0, GW])
    yb = sb(mem, "y_rows", [128, 3, 3, D])
    w_in = [None] * E
    consts = load("ld_w2", b1[:], t["b1"])
    consts = load("ld_w2", b2[:], t["b2"].partition_broadcast(128))
    for e_ in range(E):
        if e_ in (0, 1):
            hi = 1 if e_ == 0 else E
            load(f"ld_e{e_}", w1[:, e_:hi], t["w1"][:, e_:hi])
            load(f"ld_e{e_}", w2[:, e_:hi], t["w2"][:, e_:hi])
        w_in[e_] = (sig(f"ld_e{min(e_, 1)}"), 32)
    jobs = [(e_, a, w) for e_ in range(E) for a, w in groups]
    F = {}
    H_BANKS, T_BANKS, Y_BANKS = (0, 1, 2, 3), (4, 5), (6, 7)

    def fetch(n):
        e_, a, w = jobs[n]
        base = e_ * CAP + a
        full_, part_ = divmod(w, 128)
        after = [F.get(("xe", n % 3))] + R["all"]
        if full_:
            F[("in", n)] = load(f"xe_in{n % 3}", xe[:, n % 3, 0:full_, :], scratch["xe"][base:base + full_ * 128, :].rearrange("(s p) d -> p s d", p=128), after)
        if part_:
            F[("in", n)] = load(f"xe_in{n % 3}", xe[0:part_, n % 3, full_, :], scratch["xe"][base + full_ * 128:base + w, :], after)

    def turn(n):
        e_, a, w = jobs[n]
        bank = ps[:, T_BANKS[n % 2], :]
        for s_ in range(-(-w // 128)):
            r_ = min(128, w - 128 * s_)
            mm = pe.put(lambda e, s_=s_, r_=r_: e.transpose(bank[:, s_ * 128:s_ * 128 + r_], xe[0:r_, n % 3, s_, :], ident[0:r_, 0:r_]),
                        [F[("in", n)], F.get(("Tbank", n % 2))], sig("e_T"))
        F[("xe", n % 3)] = mm
        hi = act.put(lambda e: e.copy(xeh[:, n % 2, 0:w], bank[:, 0:w]), [mm, F.get(("xeTfree", n % 2))], sig("e_T_high"))
        F[("xeT", n)] = F[("Tbank", n % 2)] = dve.put(lambda e: e.tensor_tensor(xel[:, n % 2, 0:w], bank[:, 0:w], xeh[:, n % 2, 0:w].bitcast(F32), ALU.subtract),
                                                      [hi], sig("e_T_low"))

    def split_w1(e_):
        a = dve.put(lambda e: e.tensor_copy(w1h[:, e_], w1[:, e_]), [w_in[e_]], sig("e_wh"))
        F[("w1", e_)] = dve.put(lambda e: e.tensor_tensor(w1l[:, e_], w1[:, e_], w1h[:, e_].bitcast(F32), ALU.subtract), [a], sig("e_wl"))

    def up(n):
        e_, a, w = jobs[n]
        xh0, xl0 = xeh[:, n % 2, 0:w], xel[:, n % 2, 0:w]
        for q in range(NC0):
            bank = ps[:, H_BANKS[q], 0:w]
            wc = slice(q * 128, (q + 1) * 128)
            pe.put(lambda e, wc=wc, bank=bank: e.matmul(bank, w1h[:, e_, wc], xh0, start=True, stop=False),
                   [F[("xeT", n)], F[("w1", e_)], F.get(("H", q))])
            pe.put(lambda e, wc=wc, bank=bank: e.matmul(bank, w1h[:, e_, wc], xl0, start=False, stop=False))
            mm = pe.put(lambda e, wc=wc, bank=bank: e.matmul(bank, w1l[:, e_, wc], xh0, start=False, stop=True), (), sig("e_up"))
            F[("H", q)] = F[("h", n)] = act.put(lambda e, q=q, bank=bank: e.activation(hT[:, n % 2, q, 0:w], bank, ACT.Gelu_apprx_tanh, bias=b1[:, e_, q:q + 1]),
                                  [mm, consts, F.get(("hfree", n % 2))], sig("e_gelu"))
        F[("xeTfree", n % 2)] = mm

    def down(n):
        e_, a, w = jobs[n]
        bank = ps[:, Y_BANKS[n % 2], :]
        for s_ in range(-(-w // 128)):
            r_ = min(128, w - 128 * s_)
            for q in range(NC0):
                mm = pe.put(lambda e, s_=s_, r_=r_, q=q: e.matmul(bank[0:r_, s_ * D:(s_ + 1) * D], hT[:, n % 2, q, s_ * 128:s_ * 128 + r_], w2[:, e_, q, :],
                                                                  start=(q == 0), stop=(q == NC0 - 1)),
                            [F[("h", n)], F.get(("Y", n % 2))], sig("e_down") if q == NC0 - 1 else None)
        F[("hfree", n % 2)] = mm
        base = e_ * CAP + a
        full_, part_ = divmod(w, 128)
        marks = []
        y3 = bank[:, 0:3 * D].rearrange("p (s d) -> p s d", s=3)
        if full_:
            a1 = dve.put(lambda e: e.tensor_tensor(yb[:, n % 3, 0:full_, :], y3[:, 0:full_, :], b2[:, e_:e_ + 1, :].broadcast_to([128, full_, D]), ALU.add),
                         [mm, F.get(("y", n % 3))], sig("e_y"))
        if part_:
            a1 = dve.put(lambda e: e.tensor_tensor(yb[0:part_, n % 3, full_, :], y3[0:part_, full_, :], b2[0:part_, e_, :], ALU.add),
                         [mm, F.get(("y", n % 3))], sig("e_y"))
        F[("Y", n % 2)] = a1
        if full_:
            F[("y", n % 3)] = load(f"y_out{n % 3}", scratch["y"][base:base + full_ * 128, :].rearrange("(s p) d -> p s d", p=128), yb[:, n % 3, 0:full_, :], [a1])
        if part_:
            F[("y", n % 3)] = load(f"y_out{n % 3}", scratch["y"][base + full_ * 128:base + w, :], yb[0:part_, n % 3, full_, :], [a1])
        F[("ydone", n % 3)] = F[("y", n % 3)]

    NJ = len(jobs)
    split_w1(0)
    fetch(0)
    fetch(1)
    turn(0)
    for n in range(NJ):
        if n % len(groups) == 0 and n // len(groups) + 1 < E:
            split_w1(n // len(groups) + 1)
        if n + 2 < NJ:
            fetch(n + 2)
        if n + 1 < NJ:
            turn(n + 1)
        up(n)
        if n >= 1:
            down(n - 1)
    down(NJ - 1)
    ys = [F[("ydone", k)] for k in range(3)]
    fence()
    mem.close()
    feed_mem = ExitStack()
    got = sb(feed_mem, "got_rows", [128, 4, TOPK, D])
    xh = sb(feed_mem, "xn_T_high", [D, NCH, CT], F32R)
    xl = sb(feed_mem, "xn_T_low", [D, NCH, CT], F32R)
    vbo = sb(feed_mem, "bo_rows1", [S, D])
    comb = sb(feed_mem, "comb", [S, CB, E])
    cw = sb(feed_mem, "comb_work", [S, 5, CB, E])
    csum = sb(feed_mem, "comb_sum", [S, 4, CB])
    cparts = sb(feed_mem, "comb_parts", [S, CB, 3, E], BF16)
    cT = sb(feed_mem, "comb_T", [3 * E, NCH, CT], BF16)
    vbo_in = load("ld_bo1", vbo[:], t["f1_bo"].partition_broadcast(S))
    tb = dve.put(lambda e: e.tensor_scalar(vbo[:], vbo[:], tg_f[:, 1:2], None, ALU.mult), [vbo_in], sig("f_bo"))

    def bring_y(c):
        for i in range(c * CB, (c + 1) * CB):
            for j in range(TOPK):
                g_ = pool.put(lambda e, i=i, j=j: e.indirect_dma_start(got[:, i % 4, j, :], None, scratch["y"][:, :],
                                                                       bass.IndirectOffsetOnAxis(slot_get[:, j, i:i + 1], 0),
                                                                       bounds_check=SLOTS - 1, oob_is_err=True),
                              ys + [F.get(("got", i % 4)), R["w"]], sig(f"gather{i % 4}"), 16)
            F[("g", i)] = g_
            if i > c * CB:
                add_y(i - 1)
            yield
        add_y(c * CB + CB - 1)
        x_ready[c] = F[("got", (CB - 1) % 4)]
        yield

    def add_y(i):
        a = dve.put(lambda e: e.scalar_tensor_tensor(x[:, i, :], got[:, i % 4, 0, :], slot_w[:, 0, i:i + 1], x[:, i, :], ALU.mult, ALU.add), [F[("g", i)]], sig("combine"))
        F[("got", i % 4)] = dve.put(lambda e: e.scalar_tensor_tensor(x[:, i, :], got[:, i % 4, 1, :], slot_w[:, 1, i:i + 1], x[:, i, :], ALU.mult, ALU.add), [a], sig("combine"))

    G = {}

    def weigh(c, x_done):
        yield from layernorm(1, 1 + c % 2, c, x_done)
        hi = act.put(lambda e: e.copy(xh[:, c, :], xnT[:, 1, :]), [ln[("T", 1)]], sig("f_xh"))
        yield from choose(1)
        V = lambda fn, after: dve.put(fn, after, sig("c_v"))
        a = G[("x", c)] = V(lambda e: e.tensor_tensor(xl[:, c, :], xnT[:, 1, :], xh[:, c, :].bitcast(F32), ALU.subtract), [hi])
        ln[("T_free", 1)] = a
        V(lambda e: e.tensor_tensor(cw[:, 0], lg[:], mx8[:, :, 0:1].broadcast_to([S, CB, E]), ALU.subtract), [R["top"], R["hot"]])
        a = R["lg"] = R["gate"] = V(lambda e: e.tensor_tensor(csum[:, 0, :], mx8[:, :, 1], mx8[:, :, 0], ALU.subtract), [G.get("x_b")])
        yield
        act.put(lambda e: e.activation(cw[:, 1], cw[:, 0], ACT.Exp), [a], sig("c_exp"))
        ex = act.put(lambda e: e.activation(csum[:, 1, :], csum[:, 0, :], ACT.Exp), [a], sig("c_exp"))
        yield
        a = V(lambda e: e.tensor_reduce(csum[:, 2, :], cw[:, 1], AX_X, ALU.add), [ex])
        a = V(lambda e: e.scalar_tensor_tensor(csum[:, 2, :], csum[:, 2, :], EPS_GATE, csum[:, 1, :], ALU.mult, ALU.add), [a])
        a = V(lambda e: e.tensor_scalar(csum[:, 2, :], csum[:, 2, :], 1.0, None, ALU.add), [a])
        a = V(lambda e: e.reciprocal(csum[:, 3, :], csum[:, 2, :]), [a])
        a = V(lambda e: e.tensor_tensor(cw[:, 2], oh[:, 1], csum[:, 1, :].rearrange("p (b o) -> p b o", o=1).broadcast_to([S, CB, E]), ALU.mult), [a])
        a = V(lambda e: e.tensor_tensor(cw[:, 3], cw[:, 2], oh[:, 0], ALU.add), [a])
        a = V(lambda e: e.tensor_tensor(comb[:], cw[:, 3], csum[:, 3, :].rearrange("p (b o) -> p b o", o=1).broadcast_to([S, CB, E]), ALU.mult), [a])
        yield
        cs = V(lambda e: e.tensor_reduce(csum[:, 0, :], comb[:], AX_X, ALU.add), [a])
        a = V(lambda e: e.tensor_copy(cparts[:, :, 0, :], comb[:]), [a, G.get("cT_mm")])
        a = V(lambda e: e.tensor_tensor(cw[:, 4], comb[:], cparts[:, :, 0, :], ALU.subtract), [a])
        a = V(lambda e: e.tensor_copy(cparts[:, :, 1, :], cw[:, 4]), [a])
        a = V(lambda e: e.tensor_tensor(cparts[:, :, 2, :], cw[:, 4], cparts[:, :, 1, :], ALU.subtract), [a])
        for b in range(CB):
            G["x_b"] = G[("x_b", c)] = V(lambda e, b=b: e.scalar_tensor_tensor(x[:, c * CB + b, :], vbo[:], csum[:, 0, b:b + 1], x[:, c * CB + b, :], ALU.mult, ALU.add),
                                         [cs, ln[("norm", 1)], tb])
        yield
        m, bank = misc_bank()
        bank_b = bank[0:3 * E, 0:CT // 2].bitcast(BF16)
        for b in range(CB):
            tr = pe.put(lambda e, b=b: e.transpose(bank_b[:, b * S:(b + 1) * S], cparts[:, b].rearrange("p s e -> p (s e)"), ident_b),
                        [a, misc["free"][m]], sig("c_T"))
        G["cT_mm"] = tr
        G[("cT", c)] = misc["free"][m] = act.put(lambda e: e.copy(cT[:, c, :], bank_b), [tr], sig("c_T_out"))

    attention(1, bring_y, weigh)

    mem = ExitStack()
    raw = sb(mem, "w1_T_raw", [D, 2, 2 * HID1])
    vh = sb(mem, "w1_T_high", [D, E, 2 * HID1], F32R)
    vl = sb(mem, "w1_T_low", [D, E, 2 * HID1], F32R)
    vo = sb(mem, "wo_T", [128, 2, D])
    vb = sb(mem, "b1_cols1", [128, E, 4])
    sel = sb(mem, "expert_rows", [3 * E, E, 128], BF16)
    cb_sb = sb(mem, "comb_rows", [128, 3, CT])
    sg = sb(mem, "sigmoid", [128, 3, CT])
    ga = sb(mem, "gated", [128, 3, CT])
    gw = sb(mem, "weighted", [128, 3, CT])
    acc = sb(mem, "gated_sum", [128, 2, 2, CT])
    for dst, src in ((vb[:], t["f1_b1"]), (sel[:], t["sel"]), (vo[:], t["f1_wo"])):
        vin = load("ld_f1", dst, src)
    vready = {}

    def split_weights(e_):
        k = e_ % 2
        a = load(f"ld_v{k}", raw[:, k], t["f1_w1"][:, e_], [vready.get(e_ - 2)])
        a = dve.put(lambda e: e.tensor_copy(vh[:, e_], raw[:, k]), [a], sig("f_wh"))
        vready[e_] = dve.put(lambda e: e.tensor_tensor(vl[:, e_], raw[:, k], vh[:, e_].bitcast(F32), ALU.subtract), [a], sig("f_wl"))

    A_BANKS, B_BANKS, C_BANKS = (0, 1), (2, 3), (4, 5)
    outs = []
    units = [0]

    def up1(bank, c, e_, col, after):
        w = slice(col, col + 128)
        pe.put(lambda e: e.matmul(bank, vh[:, e_, w], xh[:, c, :], start=True, stop=False), after)
        pe.put(lambda e: e.matmul(bank, vh[:, e_, w], xl[:, c, :], start=False, stop=False))
        return pe.put(lambda e: e.matmul(bank, vl[:, e_, w], xh[:, c, :], start=False, stop=True), (), sig("f_up"))

    def experts1(c):
        for e_ in range(E):
            if c == 0 and e_ + 2 < E:
                split_weights(e_ + 2)
            u3 = (c * E + e_) % 3
            cbank = ps[:, C_BANKS[e_ % 2], :]
            mm = pe.put(lambda e, e_=e_, cbank=cbank: e.matmul(cbank, sel[:, e_, :], cT[:, c, :], start=True, stop=True),
                        [G[("cT", c)], vin, G.get(("C", e_ % 2))], sig("f_comb"))
            cbm = G[("C", e_ % 2)] = act.put(lambda e, u3=u3, cbank=cbank: e.copy(cb_sb[:, u3, :], cbank), [mm, G.get(("cb", u3))], sig("f_comb_out"))
            for hc in range(2):
                s3, s2_ = units[0] % 3, units[0] % 2
                units[0] += 1
                abank, bbank = ps[:, A_BANKS[s2_], :], ps[:, B_BANKS[s2_], :]
                mb = up1(bbank, c, e_, HID1 + hc * 128, [G[("x", c)], vready[e_], G.get(("B", s2_))])
                G[("B", s2_)] = sgm = act.put(lambda e, e_=e_, hc=hc, bbank=bbank, s3=s3: e.activation(sg[:, s3, :], bbank, ACT.Sigmoid, bias=vb[:, e_, 2 + hc:3 + hc]),
                                              [mb, G.get(("sg", s3))], sig("f_sig"))
                ma = up1(abank, c, e_, hc * 128, [G.get(("A", s2_))])
                gm = G[("A", s2_)] = G[("sg", s3)] = dve.put(
                    lambda e, e_=e_, hc=hc, abank=abank, s3=s3: e.scalar_tensor_tensor(ga[:, s3, :], abank, vb[:, e_, hc:hc + 1], sg[:, s3, :], ALU.add, ALU.mult),
                    [ma, sgm, G.get(("ga", s3))], sig("f_gated"))
                if e_ == 0:
                    wm = G[("ga", s3)] = G[("acc", hc)] = dve.put(lambda e, u3=u3, s3=s3, hc=hc: e.tensor_tensor(acc[:, c % 2, hc, :], ga[:, s3, :], cb_sb[:, u3, :], ALU.mult),
                                                                  [gm, cbm, G.get(("accfree", c % 2))], sig("f_weighted"))
                else:
                    wm = G[("ga", s3)] = dve.put(lambda e, u3=u3, s3=s3: e.tensor_tensor(gw[:, s3, :], ga[:, s3, :], cb_sb[:, u3, :], ALU.mult),
                                                 [gm, cbm, G.get(("gw", s3))], sig("f_weighted"))
                    G[("gw", s3)] = G[("acc", hc)] = pool.put(lambda e, s3=s3, hc=hc: e.tensor_tensor(acc[:, c % 2, hc, :], acc[:, c % 2, hc, :], gw[:, s3, :], ALU.add),
                                                              [wm, G[("acc", hc)]], sig("f_sum"))
                G[("cb", u3)] = wm
            if e_ == 1 and c > 0:
                down1(c - 1, G[("sum", c - 1)])
        G[("sum", c)] = [G[("acc", 0)], G[("acc", 1)]]

    def down1(c, summed):
        m, bank = misc_bank()
        for b in range(CB):
            for hc in range(2):
                mo = pe.put(lambda e, b=b, hc=hc: e.matmul(bank[:, b * D:(b + 1) * D], acc[:, c % 2, hc, b * S:(b + 1) * S], vo[:, hc, :], start=(hc == 0), stop=(hc == 1)),
                            summed + [misc["free"][m]], sig("f_out"))
        G[("accfree", c % 2)] = mo
        xs = x[:, c * CB:(c + 1) * CB, :]
        fin = misc["free"][m] = dve.put(lambda e: e.scalar_tensor_tensor(xs, bank.rearrange("p (b d) -> p b d", b=CB), tg_f[:, 1:2], xs, ALU.mult, ALU.add),
                                        [mo, G[("x_b", c)]], sig("f_x"))
        outs.append(load("out", out[:, c * CB:(c + 1) * CB, :], xs, [fin]))

    split_weights(0)
    split_weights(1)
    for c in range(NCH):
        experts1(c)
    down1(NCH - 1, G[("sum", NCH - 1)])
    sp.put(None, [outs[-1]])
    fence()

    with nc.Block() as block:
        block.tensor(pe.play)
        block.scalar(act.play)
        block.vector(dve.play)
        block.gpsimd(pool.play)
        block.sync(sp.play)
    mem.close()
    feed_mem.close()
    rt.close()
    top.close()


def kernel(**inputs):
    import numpy as np
    import concourse.bacc as bacc
    from concourse import mybir as mb
    from concourse.bass_utils import run_bass_kernel_spmd

    a = {k: np.asarray(v) for k, v in inputs.items()}
    c = np.ascontiguousarray
    bf = mb.dt.np(mb.dt.bfloat16) if hasattr(mb.dt, "np") else None
    import ml_dtypes
    bf = ml_dtypes.bfloat16
    f = np.float32
    eye = np.eye(128)
    sel = np.zeros((3, E, E, 128))
    for e in range(E):
        sel[:, e, e, :] = 1.0
    arrays = {
        "x": c(a["x"].transpose(1, 0, 2)),
        "ctxT": c(a["ctx_1024"].reshape(B * S2, D).T),
        "groupT": c(a["fside_BxSxS2_0"].transpose(2, 0, 1)),
        "mask0": c(a["mask_BxSxS2_ik1"].transpose(1, 0, 2)),
        "mask0T": c(a["mask_BxSxS2_ik1"].transpose(2, 0, 1)),
        "mask1": c(a["mask_1x1xSxS2_bk1"][0, 0]),
        "mask1T": c(a["mask_1x1xSxS2_bk1"][0, 0].T),
        "wq": c(np.stack([a["L0_xattn_wq_k"], a["L1_xattn_w_q"].T], 1)),
        "wk": c(np.stack([a["L0_xattn_wk_k"], a["L1_xattn_w_k"].T], 1)),
        "wv": c(np.stack([a["L0_xattn_wv_k"], a["L1_xattn_w_v"].T], 1)),
        "wo": c(np.stack([a["L0_xattn_wo_k"], a["L1_xattn_w_o"].T], 1)),
        "cols": c(np.stack([a["L0_xattn_wq_b"], a["L0_xattn_wk_b"], a["L1_xattn_b_q"], a["L1_xattn_b_k"]], 1)),
        "bv": c(np.stack([a["L0_xattn_wv_b"], a["L1_xattn_b_v"]])),
        "bo": c(np.stack([a["L0_xattn_wo_b"], a["L1_xattn_b_o"]])),
        "g": c(np.concatenate([a["g_xattn"], a["g_ffn"]])),
        "wg": c(np.stack([a["L0_ffn_Wg"], a["L1_ffn_Wg"].T], 1)),
        "w1": c(a["L0_ffn_W1"].transpose(1, 0, 2)),
        "b1": c(a["L0_ffn_b1"].reshape(E, HID0 // 128, 128).transpose(2, 0, 1)),
        "w2": c(a["L0_ffn_W2"].reshape(E, HID0 // 128, 128, D).transpose(2, 0, 1, 3)),
        "b2": c(a["L0_ffn_b2"]),
        "f1_w1": c(a["L1_ffn_W1"].transpose(2, 0, 1)),
        "f1_b1": c(a["L1_ffn_b1"].reshape(E, 4, 128).transpose(2, 0, 1)),
        "f1_wo": c(a["L1_ffn_Wo"].T.reshape(2, 128, D).transpose(1, 0, 2)),
        "f1_bo": c(a["L1_ffn_bo"]),
        "ident": eye.astype(f),
        "cbf": c(np.concatenate([eye, np.triu(np.ones((128, 128)), 1), np.ones((128, 128))], 1)).astype(bf),
        "iota8": c(np.tile(np.arange(E), (128, 1))).astype(f),
        "ones": np.ones((3, PAIRS, CK)).astype(bf),
        "zeros": np.zeros((SPARE, PAIRS, CT)).astype(bf),
        "zero_rows": np.zeros((128, 1024), f),
        "sel": sel.reshape(3 * E, E, 128).astype(bf),
    }
    nc = bacc.Bacc("TRN2", target_bir_lowering=False, num_devices=1)
    t = {k: nc.dram_tensor(f"in_{k}", v.shape, mb.dt.from_np(v.dtype), kind="ExternalInput").ap() for k, v in arrays.items()}
    out = nc.dram_tensor("out_x", (S, B, D), F32, kind="ExternalOutput").ap()
    scratch = {
        "q": nc.dram_tensor("scratch_q", (NCH, H, 3, DH, CT), BF16, kind="Internal").ap(),
        "k": nc.dram_tensor("scratch_k", (NCH, H, 6, DH, CK), BF16, kind="Internal").ap(),
        "shift": nc.dram_tensor("scratch_shift", (B, 3 * H, S), BF16, kind="Internal").ap(),
        "xe": nc.dram_tensor("scratch_xe", (SLOTS, D), F32, kind="Internal").ap(),
        "y": nc.dram_tensor("scratch_y", (SLOTS, D), F32, kind="Internal").ap(),
    }
    flamingo(nc, t, out, scratch)
    r = run_bass_kernel_spmd(nc, [{f"in_{k}": v for k, v in arrays.items()}], core_ids=[0])
    return c(r.results[0]["out_x"].transpose(1, 0, 2))
```

```python
from contextlib import ExitStack

import concourse.bass as bass
from concourse import mybir

B, S, S2, D = 32, 128, 120, 128
H = 16
DH = D // H
E = 8
HID0 = 512
HID1 = 256
TOPK = 2
TOKENS = B * S
CAP = -(-TOKENS * TOPK * 105 // (E * 100))
SLOTS = E * CAP

CB = 4
NCH = B // CB
CT = CB * S
CK = CB * S2
RING = 3
PAIRS = H // 2
HALF = 64
Q_SLOTS = (0, 1, 2, 0, 1, 0)
K_SLOTS = (0, 0, 0, 1, 1, 2)
Q_OUT = ((0, 0, 3, False), (3, 0, 2, False), (5, 0, 1, False))
K_OUT = ((0, 0, 3, True), (3, 1, 2, True), (5, 2, 1, True))
SLOT_ROWS = 6 * DH
SHIFT_ROW = SLOT_ROWS
SPARE = HALF - SLOT_ROWS
EPS_LN = 1e-5
EPS_GATE = 1e-9
SCALE = 1.0 / float(DH) ** 0.5
NEG_ADD = -998244352.0
NEG_SET = -float(2 ** 100)
SKIP = float(2 ** 20)

ALU = mybir.AluOpType
ACT = mybir.ActivationFunctionType
F32 = mybir.dt.float32
F32R = mybir.dt.float32r
BF16 = mybir.dt.bfloat16
I32 = mybir.dt.int32
U32 = mybir.dt.uint32
U8 = mybir.dt.uint8
AX_X = mybir.AxisListType.X


class Signal:

    def __init__(self, handle):
        self.handle, self.value = handle, 0


class Line:

    def __init__(self):
        self.items = []

    def put(self, emit, after=(), sig=None, by=1):
        self.items.append((emit, tuple(after), sig, by))
        if sig is None:
            return None
        sig.value += by
        return (sig, sig.value)

    def play(self, eng):
        waited = {}
        for emit, after, sig, by in self.items:
            for mark in after:
                if mark is not None and waited.get(id(mark[0]), 0) < mark[1]:
                    eng.wait_ge(mark[0].handle, mark[1])
                    waited[id(mark[0])] = mark[1]
            ins = emit(eng) if emit is not None else None
            if sig is not None:
                ins.then_inc(sig.handle, by)


def flamingo(nc, t, out, scratch):
    top = ExitStack()
    pe, act, dve, pool, sp = Line(), Line(), Line(), Line(), Line()
    signals = {}

    def sig(name):
        if name not in signals:
            signals[name] = Signal(top.enter_context(nc.semaphore(name)))
        return signals[name]

    def sb(stack, name, shape, dt=F32):
        return stack.enter_context(nc.sbuf_tensor(name, shape, dt))

    def load(name, dst, src, after=(), line=None):
        return (line or sp).put(lambda e: e.dma_start(dst, src), after, sig(name), 16)

    def fence(lines=(pe, act, dve, pool, sp)):
        marks = [(s, s.value) for s in signals.values() if s.value]
        for line in lines:
            line.put(None, marks)

    x = sb(top, "x_rows", [S, B, D])
    ctxT = sb(top, "ctx_T", [D, B * S2])
    wq = sb(top, "wq", [D, 2, D])
    wk = sb(top, "wk", [D, 2, D])
    wv = sb(top, "wv", [D, 2, D])
    wo = sb(top, "wo", [D, 2, D])
    cols = sb(top, "bias_cols", [D, 4])
    bv = sb(top, "bv_rows", [S, 2, D])
    bo = sb(top, "bo_rows", [S, 2, D])
    tg_x = sb(top, "tanh_g_xattn", [S, 2])
    tg_f = sb(top, "tanh_g_ffn", [S, 2])
    g_in = sb(top, "g_in", [S, 4])
    ident = sb(top, "ident", [128, 128])
    cbf = sb(top, "const_bf16", [128, 3 * 128], BF16)
    ident_b, tri_b, ones_b = cbf[:, 0:128], cbf[:, 128:256], cbf[:, 256:384]
    iota8 = sb(top, "iota8", [128, E])
    wg = sb(top, "wg", [D, 2, E])
    half_c = sb(top, "minus_half", [128, CB])
    xn = sb(top, "xn_rows", [S, 3, CB, D])
    xnT = sb(top, "xn_T", [D, 2, CT])
    stats = sb(top, "ln_stats", [S, 2, CB, 6])
    mv = sb(top, "ln_mean_var", [S, 2, CB, 2])
    rs = sb(top, "ln_rstd", [S, 2, 6, CB])
    slot_w = sb(top, "slot_weight", [S, TOPK, B])
    slot_put = sb(top, "slot_put", [S, TOPK, B], I32)
    slot_get = sb(top, "slot_get", [S, TOPK, B], I32)

    ps = top.enter_context(nc.psum_tensor("psum", [128, 8, 512], F32))

    v_rows = sb(top, "v_rows", [S2, 2, CB, D])
    full = sb(top, "full", [D, 2, CT])
    parts = sb(top, "parts", [D, 2, 3, CT], BF16)
    qop = sb(top, "q_operand", [128, RING, PAIRS, CT], BF16)
    kop = sb(top, "k_operand", [128, RING, PAIRS, 2, CK], BF16)
    vx = sb(top, "v_spread", [S2, 2, 4 * 128])
    onesx = sb(top, "ones_spread", [S2, 4, 32])

    for dst, src in ((x[:, 0:CB, :], t["x"][:, 0:CB, :]), (ctxT[:, 0:CK], t["ctxT"][:, 0:CK]), (wk[:], t["wk"]),
                     (cols[:], t["cols"]), (ident[:], t["ident"]), (wq[:], t["wq"])):
        first_in = load("ld_first", dst, src)
    for dst, src in ((g_in, t["g"].partition_broadcast(S)), (bo, t["bo"].partition_broadcast(S)), (wv, t["wv"]),
                     (bv, t["bv"].partition_broadcast(S)), (cbf, t["cbf"]), (wo, t["wo"]), (iota8, t["iota8"]), (wg, t["wg"])):
        weights_in = load("ld_w", dst[:], src)
    rows_in = {0: first_in}

    def load_rows(c0, c1):
        load(f"ld_rows{c0}_", x[:, c0 * CB:c1 * CB, :], t["x"][:, c0 * CB:c1 * CB, :])
        a = load(f"ld_rows{c0}_", ctxT[:, c0 * CK:c1 * CK], t["ctxT"][:, c0 * CK:c1 * CK])
        for c in range(c0, c1):
            rows_in[c] = a

    load_rows(1, 2)

    const_done = pool.put(lambda e: e.memset(half_c[:], -0.5), (), sig("const"))
    for j in (0, 2):
        cols_done = dve.put(lambda e, j=j: e.tensor_scalar(cols[:, j:j + 1], cols[:, j:j + 1], SCALE, None, ALU.mult),
                            [first_in], sig("cols"))
    tanh_done = {}

    def make_gates():
        act.put(lambda e: e.activation(tg_x[:, :], g_in[:, 0:2], ACT.Tanh), [weights_in], sig("tanh"))
        a = act.put(lambda e: e.activation(tg_f[:, :], g_in[:, 2:4], ACT.Tanh), (), sig("tanh"))
        for l in range(2):
            tanh_done["bo"] = dve.put(lambda e, l=l: e.tensor_scalar(bo[:, l, :], bo[:, l, :], tg_x[:, l:l + 1], None, ALU.mult),
                                      [a], sig("bo"))

    misc = {"n": 0, "free": [None, None]}
    MISC = (6, 7)

    def misc_bank():
        k = misc["n"] % 2
        misc["n"] += 1
        return k, ps[:, MISC[k], :]

    ln = {}

    def layernorm(who, slot, c, ready):
        st, m_v, r_s = stats[:, who], mv[:, who], rs[:, who]
        for b in range(CB):
            m = dve.put(lambda e, b=b: e.bn_stats(st[:, b, :], x[:, c * CB + b, :]), [ready, ln.get(("agg", who))], sig("ln_stats"))
        for b in range(CB):
            agg = dve.put(lambda e, b=b: e.bn_aggr(m_v[:, b, :], st[:, b, :]), [m, ln.get(("shift", who))], sig("ln_aggr"))
        ln[("agg", who)] = agg
        yield
        y, t_, r, m_r = (r_s[:, j, :] for j in range(4))
        eps = pool.put(lambda e: e.tensor_scalar(r_s[:, 4, :], m_v[:, :, 1], EPS_LN, None, ALU.add),
                       [agg, ln.get(("norm", who)), const_done], sig("ln_pow"))
        p = pool.put(lambda e: e.tensor_tensor(y, r_s[:, 4, :], half_c[:, :], ALU.pow), [eps], sig("ln_pow"))
        yield
        a = [p]
        for op in (lambda e: e.tensor_tensor(t_, y, y, ALU.mult),
                   lambda e: e.scalar_tensor_tensor(t_, r_s[:, 4, :], -0.5, t_, ALU.mult, ALU.mult),
                   lambda e: e.scalar_tensor_tensor(r, t_, 1.5, y, ALU.add, ALU.mult),
                   lambda e: e.scalar_tensor_tensor(m_r, m_v[:, :, 0], -1.0, r, ALU.mult, ALU.mult)):
            a = [dve.put(op, a, sig("ln_rstd"))]
        ln[("shift", who)] = a[0]
        yield
        yield
        for b in range(CB):
            norm = act.put(lambda e, b=b: e.activation(xn[:, slot, b, :], x[:, c * CB + b, :], ACT.Identity,
                                                       bias=m_r[:, b:b + 1], scale=r[:, b:b + 1]),
                           a + [ln.get(("rows_free", slot))], sig("ln_norm"))
        ln[("norm", who)] = norm
        yield
        yield
        m, bank = misc_bank()
        for b in range(CB):
            tr = pe.put(lambda e, b=b: e.transpose(bank[:, b * S:(b + 1) * S], xn[:, slot, b, :], ident[:, :]),
                        [norm, misc["free"][m], first_in], sig("ln_T"))
        ln[("rows_free", slot)] = tr
        ln[("T", who)] = misc["free"][m] = act.put(lambda e: e.copy(xnT[:, who, :], bank), [tr, ln.get(("T_free", who))], sig("ln_T_out"))
        yield

    def finish(task):
        for _ in task:
            pass

    q_dram, k_dram, s_dram = scratch["q"], scratch["k"], scratch["shift"]
    late = []
    free, live = {}, {}
    x_ready, x_biased = {}, {}
    q_ready, k_ready, v_ready = {}, {}, {}

    z, ones_in = {}, {}

    def clear_ring(r, line):
        z[r] = line.put(lambda e: e.memset(kop[:, r].rearrange("p a b c -> p (a b c)").bitcast(U32), 0), (), sig(f"zero{r}_"))
        for i in range(2):
            ones_in[r] = load(f"ones_row{r}_", kop[HALF * i + SHIFT_ROW:HALF * i + SHIFT_ROW + 3, r, :, i, :],
                              t["ones"][0:3], [z[r]])

    spare_in = {}

    def clear_spares():
        for r in range(RING):
            for i in range(2):
                spare_in[r] = load(f"spare_rows{r}_", qop[HALF * i + SLOT_ROWS:HALF * (i + 1), r, :, :], t["zeros"])

    clear_spares()
    clear_ring(0, pool)
    clear_ring(1, pool)
    pool.put(lambda e: e.memset(vx[:], 0.0), (), sig("spread0"))
    a = pool.put(lambda e: e.memset(onesx[:], 0.0), (), sig("spread0"))
    for g in range(4):
        spread = pool.put(lambda e, g=g: e.memset(onesx[:, g, 8 * g:8 * g + 8], 1.0), [a], sig("spread1"))

    def split(k, width, made, dram, outs, name, taken):
        f, p = full[:, k, 0:width], parts[:, k, :, 0:width]
        part_made = {}

        def write(last):
            for slot, part, count, same in outs:
                if (part if same else part + count - 1) == last:
                    src = p[:, part:part + 1, :].broadcast_to([D, count, width]) if same else p[:, part:part + count, :]
                    free[("parts", k)] = live[("split", k)] = load(
                        f"{name}_out", dram[:, slot:slot + count, :], src, [part_made[last], taken])

        part_made[0] = act.put(lambda e: e.copy(p[:, 0, :], f), [made, free.get(("parts", k))], sig("part0"))
        yield
        a = pool.put(lambda e: e.tensor_tensor(f, f, p[:, 0, :], ALU.subtract), [part_made[0]], sig("left"))
        write(0)
        yield
        part_made[1] = act.put(lambda e: e.copy(p[:, 1, :], f), [a], sig("part1"))
        yield
        free[("full", k)] = part_made[2] = pool.put(lambda e: e.tensor_tensor(p[:, 2, :], f, p[:, 1, :], ALU.subtract), [part_made[1]], sig("left"))
        write(1)
        yield
        write(2)

    def ring_free(c):
        yield
        while c >= RING and ("exp", (c - RING + 1) * CB - 1, 3) not in live:
            yield

    def project(l, which, src, src_ready, w, bias_col, scale, width):
        m, bank = misc_bank()
        mm = pe.put(lambda e: e.matmul(bank[:, 0:width], w[:, l, :], src, start=True, stop=True),
                    [src_ready, misc["free"][m], first_in], sig("project"))
        made = misc["free"][m] = act.put(
            lambda e: e.activation(full[:, which, 0:width], bank[:, 0:width], ACT.Identity,
                                   bias=cols[:, bias_col:bias_col + 1], scale=scale), [mm, free.get(("full", which)), cols_done], sig("projected"))
        return mm, made

    def prep_q(C):
        l, c = divmod(C, NCH)
        while C not in x_ready:
            yield
        yield from layernorm(0, 0, c, x_ready[C])
        if C == 0:
            make_gates()
        yield
        mm, made = project(l, 0, xnT[:, 0, :], ln[("T", 0)], wq, 2 * l, SCALE, CT)
        ln[("T_free", 0)] = mm

        def add_bias():
            for b in range(CB):
                x_biased[C] = pool.put(lambda e, b=b: e.tensor_tensor(x[:, c * CB + b, :], x[:, c * CB + b, :], bo[:, l, :], ALU.add),
                                       [ln[("norm", 0)], tanh_done["bo"]], sig("x_bias"))

        if c > 0:
            add_bias()
        yield
        yield from split(0, CT, made, q_dram[c], Q_OUT, "q", q_ready.get(C - NCH))
        w = live[("split", 0)]
        if c == 0:
            add_bias()
        yield from ring_free(C)
        r = C % RING
        for i in range(2):
            rows = slice(HALF * i + SHIFT_ROW, HALF * i + SHIFT_ROW + 3)
            load(f"q_in{r}_", qop[rows, r, :, :], t["zeros"][0:3], [free.get(("qop", r)), spare_in[r]])
        for i in range(2):
            q_ready[C] = load(f"q_in{r}_", qop[HALF * i:HALF * i + SLOT_ROWS, r, :, :],
                              q_dram[c].rearrange("(t i d) s n -> i (d s) t n", i=2, d=DH)[i], [w])

    def prep_k(C):
        l, c = divmod(C, NCH)
        while c not in rows_in:
            yield
        mm, made = project(l, 1, ctxT[:, c * CK:(c + 1) * CK], rows_in[c], wk, 2 * l + 1, 1.0, CK)
        yield
        yield from split(1, CK, made, k_dram[c], K_OUT, "k", k_ready.get(C - NCH))
        w = live[("split", 1)]
        yield from ring_free(C)
        r = C % RING
        for i in range(2):
            of_head = k_dram[c].rearrange("(t i d) s n -> i (d s) t n", i=2, d=DH)[i]
            k_ready[C] = load(f"k_in{r}_", kop[HALF * i:HALF * i + SLOT_ROWS, r, :, i, :], of_head,
                              [w, free.get(("qop", r)), ones_in[r]])

    def prep_v(C):
        l, c = divmod(C, NCH)
        m, bank = misc_bank()
        for b in range(CB):
            mm = pe.put(lambda e, b=b: e.matmul(bank[0:S2, b * D:(b + 1) * D], ctxT[:, (c * CB + b) * S2:(c * CB + b + 1) * S2],
                                                wv[:, l, :], start=True, stop=True),
                        [misc["free"][m], rows_in[c], weights_in], sig("v_project"))
        v_ready[C] = misc["free"][m] = dve.put(
            lambda e: e.tensor_tensor(v_rows[:, C % 2], bank[0:S2, :].rearrange("p (b d) -> p b d", b=CB),
                                      bv[0:S2, l:l + 1, :].broadcast_to([S2, CB, D]), ALU.add),
            [mm, free.get(("v", C % 2))], sig("v_rows"))

    def attention(l, bring, after_chunk, at_end):
        mem = ExitStack()
        buf = lambda name, shape, dt=F32: sb(mem, f"{name}{l}", shape, dt)
        neg = buf("neg_rows", [S, 2, CB, S2], BF16)
        negT = buf("neg_cols", [S2, 2, CB, S], BF16)
        shift = buf("shift", [S, 2, H])
        rest = buf("shift_rest", [S, 2, H])
        sparts = buf("shift_parts", [S, 2, 3, H], BF16)
        spT = buf("shift_parts_T", [3 * H, 2, S], BF16)
        expT = buf("exp_T", [S2, 2, H, S])
        rden = buf("rden", [D, S])
        oT = buf("o_T", [D, 2, S])
        if l == 0:
            m_in = buf("mask_in", [S, CB, S2], I32)
            mT_in = buf("maskT_in", [S2, CB, S], I32)
            gT = buf("group_T", [S2, 2, CB, S])
            expG = buf("exp_G", [S2, 2, H, S])
        else:
            m_in = buf("mask_in", [S, S2], U8)
            mT_in = buf("maskT_in", [S2, S], U8)

        neg_ready, g_ready = {}, {}

        def masks(c):
            k = c % 2
            if l == 1:
                if c == 0:
                    a = load("mask", m_in[:], t["mask1"])
                    a = load("mask", mT_in[:], t["mask1T"])
                    yield
                    pool.put(lambda e: e.tensor_scalar(neg[:, 0, 0, :], m_in[:], NEG_SET, None, ALU.mult), [a], sig("neg"))
                    neg_ready[0] = pool.put(lambda e: e.tensor_scalar(negT[:, 0, 0, :], mT_in[:], NEG_SET, None, ALU.mult), (), sig("neg"))
                neg_ready[c] = neg_ready[0]
                return
            sl = slice(c * CB, (c + 1) * CB)
            a = load("mask", m_in[:], t["mask0"][:, sl, :], [free.get("m_in")])
            a = load("mask", mT_in[:], t["mask0T"][:, sl, :], [free.get("m_in")])
            for _ in range(4):
                yield
            g_ready[c] = load(f"group{k}_", gT[:, k], t["groupT"][:, sl, :], [free.get(("g", k)), free.get(("g2", k))])
            pool.put(lambda e: e.tensor_scalar(neg[:, k], m_in[:], -NEG_ADD, NEG_ADD, ALU.mult, ALU.add),
                     [a, free.get(("neg", k))], sig("neg"))
            neg_ready[c] = free["m_in"] = pool.put(
                lambda e: e.tensor_scalar(negT[:, k], mT_in[:], -NEG_ADD, NEG_ADD, ALU.mult, ALU.add),
                [free.get(("negT", k))], sig("neg"))

        S_BANKS, T_BANKS, BANK_AV = (0, 1), (2, 3, 4), 5
        def scores(i, r):
            c, b = divmod(i, CB)
            k = 0 if l == 1 else c % 2
            bb = 0 if l == 1 else b
            sb_ = r % 2
            bank = ps[:, S_BANKS[sb_], 0:4 * S2].rearrange("p (h k) -> p h k", h=4)
            pe.put(lambda e: e.matmul(bank, ident_b, neg[:, k, bb:bb + 1, :].broadcast_to([S, 4, S2]), start=True, stop=False),
                   [free.get(("S", sb_)), neg_ready[c], q_ready[l * NCH + c], k_ready[l * NCH + c]])
            for u in range(2):
                pt = 2 * r + u
                mm = pe.put(lambda e, u=u, pt=pt: e.matmul(bank[:, 2 * u:2 * u + 2, :], qop[:, (l * NCH + c) % RING, pt, b * S:(b + 1) * S],
                                                           kop[:, (l * NCH + c) % RING, pt, :, b * S2:(b + 1) * S2], start=False, stop=(u == 1)),
                            (), sig("score") if u == 1 else None)
            mx = free[("S", sb_)] = dve.put(lambda e: e.tensor_reduce(shift[:, i % 2, 4 * r:4 * r + 4], bank, AX_X, ALU.max, negate=True),
                                     [mm, free.get(("shift", i % 2))], sig("row_max"))
            free[("neg", c % 2)] = mm
            if r == 3:
                live[("scored", i)] = mm
                k2 = i % 2
                sp_ = sparts[:, k2]
                order = lambda a: a.rearrange("p (t i) -> p i t", i=2)
                by_part = sp_.rearrange("p s h -> p (s h)").rearrange("p (i s t) -> p i s t", i=2, s=3)
                to = lambda j: by_part[:, :, j, :]
                a = act.put(lambda e: e.copy(to(0), order(shift[:, k2])), [mx, free.get(("sparts", k2))], sig("shift_0"))
                a = pool.put(lambda e: e.tensor_tensor(order(rest[:, k2]), order(shift[:, k2]), to(0), ALU.subtract), [a], sig("shift_part"))
                a = act.put(lambda e: e.copy(to(1), order(rest[:, k2])), [a], sig("shift_0"))
                a = pool.put(lambda e: e.tensor_tensor(to(2), order(rest[:, k2]), to(1), ALU.subtract), [a], sig("shift_part"))
                free[("shift", k2)] = live[("sparts", i)] = a

        def shift_rows(i):
            c, b = divmod(i, CB)
            k2 = i % 2
            m, bank = misc_bank()
            bank_b = bank[0:3 * H, 0:S // 2].bitcast(BF16)
            tr = free[("sparts", k2)] = pe.put(lambda e: e.transpose(bank_b, sparts[:, k2].rearrange("p s h -> p (s h)"), ident_b),
                                               [live[("sparts", i)], misc["free"][m]], sig("shift_T"))
            cp = misc["free"][m] = act.put(lambda e: e.copy(spT[:, k2, :], bank_b), [tr, free.get(("spT", k2))], sig("shift_T_out"))
            w = free[("spT", k2)] = load(f"shift_out{k2}_", s_dram[i], spT[:, k2, :], [cp], act)
            for par in range(2):
                src = s_dram[i][par * 3 * PAIRS:(par + 1) * 3 * PAIRS, :].rearrange("(s t) q -> s t q", s=3)
                live[("shift", i)] = load(f"shift_in{i % 4}_", qop[HALF * par + SHIFT_ROW:HALF * par + SHIFT_ROW + 3, (l * NCH + c) % RING, :, b * S:(b + 1) * S],
                                          src, [w, live[("scored", i)]])

        def weights(i, r):
            c, b = divmod(i, CB)
            k = 0 if l == 1 else c % 2
            bb = 0 if l == 1 else b
            tb = (4 * i + r) % 3
            bank = ps[0:S2, T_BANKS[tb], :]
            pe.put(lambda e: e.matmul(bank.rearrange("p (h q) -> p h q", h=4), ident_b[0:S2, 0:S2],
                                      negT[:, k, bb:bb + 1, :].broadcast_to([S2, 4, S]), start=True, stop=False),
                   [free.get(("T", tb)), live[("shift", i)]])
            for u in range(4):
                h = 4 * r + u
                mm = pe.put(lambda e, u=u, h=h: e.matmul(
                    bank[:, u * S:(u + 1) * S], kop[:, (l * NCH + c) % RING, h // 2, h % 2, b * S2:(b + 1) * S2],
                    qop[:, (l * NCH + c) % RING, h // 2, b * S:(b + 1) * S], start=False, stop=(u == 3)),
                    (), sig("logit_T") if u == 3 else None)
            free[("negT", c % 2)] = mm
            free[("qop", (l * NCH + c) % RING)] = mm
            k2 = i % 2
            live[("exp", l * B + i, r)] = free[("T", tb)] = act.put(
                lambda e: e.activation(expT[:, k2, 4 * r:4 * r + 4, :], bank.rearrange("p (h q) -> p h q", h=4), ACT.Exp),
                [mm, free.get(("expT", k2))], sig("exp"))

        def gate(i, p):
            if l == 1:
                return
            c, b = divmod(i, CB)
            k2 = i % 2
            for line, name, h0, h1 in ((dve, "gate_v", 8 * p, 8 * p + 6 - p), (pool, "gate_p", 8 * p + 6 - p, 8 * p + 8)):
                live[(name, i, p)] = line.put(lambda e, h0=h0, h1=h1: e.tensor_tensor(
                    expG[:, k2, h0:h1, :], expT[:, k2, h0:h1, :], gT[:, c % 2, b:b + 1, :].broadcast_to([S2, h1 - h0, S]), ALU.mult),
                    [live[("exp", l * B + i, 2 * p + 1)], g_ready[c], free.get(("expG", k2))], sig(name))
            if b == CB - 1 and p == 1:
                free[("g", c % 2)] = live[("gate_v", i, 1)]
                free[("g2", c % 2)] = live[("gate_p", i, 1)]

        def spread_v(i):
            c, b = divmod(i, CB)
            dst = vx[:, i % 2, :]
            dst = bass.AP(dst.tensor, dst.offset, [list(dst.ap[0]), [128, 4], [40, 4], [1, DH]])
            a = act.put(lambda e: e.copy(dst, v_rows[:, (l * NCH + c) % 2, b, :].rearrange("p (j g d) -> p j g d", j=4, g=4)),
                         [v_ready[l * NCH + c], spread, free.get(("vx", i % 2))], sig("spread_v"))
            live[("vx", i)] = a
            free[("v", (l * NCH + c) % 2)] = a

        def out_part(i, den):
            k2 = i % 2
            src = expT if den or l == 1 else expG
            for g in range(4):
                for j in range(4):
                    h = 4 * j + g
                    lhs = onesx[:, g, :] if den else vx[:, k2, h * 32:(h + 1) * 32]
                    dst = ps[32 * j:32 * j + 32, BANK_AV, (S if den else 0):(2 * S if den else S)]
                    after = [live[("exp", l * B + i, 3)], live[("vx", i)], free.get("AV")]
                    if not den and l == 0:
                        after += [live[(nm, i, p)] for nm in ("gate_v", "gate_p") for p in range(2)]
                    mm = pe.put(lambda e, lhs=lhs, dst=dst, h=h, g=g: e.matmul(
                        dst, lhs, src[:, k2, h, :], start=(g == 0 and not den), stop=(g == 3), skip_group_check=True),
                        after, sig("av") if (g == 3 and j == 3) else None)
            if den:
                free[("expT", k2)] = mm
                live[("den", i)] = mm
            else:
                free[("vx", k2)] = mm
                free[("expG", k2)] = mm

        def normalise(i):
            a = dve.put(lambda e: e.reciprocal(rden[:], ps[:, BANK_AV, S:2 * S]), [live[("den", i)], free.get("rden")], sig("rden"))
            live[("oT", i)] = free["AV"] = free["rden"] = dve.put(
                lambda e: e.tensor_tensor(oT[:, i % 2, :], ps[:, BANK_AV, 0:S], rden[:], ALU.mult),
                [a, free.get(("oT", i % 2))], sig("o_T"))

        def out_project(i):
            c, b = divmod(i, CB)
            m, bank = misc_bank()
            mm = free[("oT", i % 2)] = pe.put(lambda e: e.matmul(bank[:, 0:D], oT[:, i % 2, :], wo[:, l, :], start=True, stop=True),
                                              [live[("oT", i)], misc["free"][m]], sig("out_project"))
            misc["free"][m] = dve.put(lambda e: e.scalar_tensor_tensor(x[:, i, :], bank[:, 0:D], tg_x[:, l:l + 1], x[:, i, :],
                                                                       ALU.mult, ALU.add),
                                      [mm, x_biased[l * NCH + c]], sig("x_new"))
            if b == CB - 1:
                x_done[c] = misc["free"][m]

        x_done = {}
        LAG_T, LAG_AV = 3, 4
        AHEAD = 6
        first, end = l * NCH, (l + 1) * NCH
        masks_0 = masks(0)
        next(masks_0, None)
        if first not in k_ready:
            finish(prep_k(first))
        finish(bring(0))
        ahead = bring(1)
        for _ in prep_q(first):
            next(ahead, None)
        if first not in v_ready:
            prep_v(first)
        finish(masks_0)
        chains = [[(C, prep_k(C)) for C in range(first + 1, min(end + 2, 2 * NCH)) if C not in k_ready],
                  [(first + 1, ahead)] + [(C, bring(C - first)) for C in range(first + 2, end)],
                  [(C, prep_q(C)) for C in range(first + 1, end)]]
        preps, after = [], []

        for _ in range(AHEAD):
            next(chains[2][0][1])

        def step(c):
            for chain in chains:
                if chain and chain[0][0] - first <= c + 2 - (i < 1):
                    for _ in range(2 if chain[0][0] - first <= c + 1 else 1):
                        if chain and next(chain[0][1], "end") == "end":
                            chain.pop(0)
            for task in list(preps):
                if next(task, "end") == "end":
                    preps.remove(task)
            for _ in range(max(1, len(after))):
                if after and next(after[0], "end") == "end":
                    after.pop(0)
            if late and next(late[0], "end") == "end":
                late.pop(0)

        for i in range(B + LAG_AV + 1):
            c, b = divmod(i, CB)
            if b == 0:
                for chain in chains:
                    while chain and chain[0][0] - first <= c:
                        finish(chain.pop(0)[1])
                for task in preps:
                    finish(task)
                preps.clear()
            if b == 2 and c + 1 < NCH:
                preps.append(masks(c + 1))
            if 0 <= i - LAG_AV - 1 < B:
                normalise(i - LAG_AV - 1)
            for r in range(4):
                if 0 <= i - LAG_T < B:
                    weights(i - LAG_T, r)
                if i < B:
                    scores(i, r)
                if r == 1 and 0 <= i - 1 < B:
                    shift_rows(i - 1)
                if r == 2 and 0 <= i - LAG_AV - 1 < B:
                    out_project(i - LAG_AV - 1)
                if r == 2 and 0 <= i - LAG_T < B:
                    spread_v(i - LAG_T)
                    gate(i - LAG_T, 0)
                if r == 3 and 0 <= i - LAG_T < B:
                    gate(i - LAG_T, 1)
                if r == 2 and 0 <= i - LAG_AV < B:
                    out_part(i - LAG_AV, False)
                if r == 3 and 0 <= i - LAG_AV < B:
                    out_part(i - LAG_AV, True)
                if r == 0 and b == 3 and c + 1 < NCH:
                    prep_v(first + c + 1)
                step(c)
            j = i - LAG_AV - 1
            if j >= 0 and j % CB == CB - 1:
                after.append(after_chunk(j // CB, x_done[j // CB]))
        at_end()
        fence((sp,) if l == 0 else (sp, dve))
        mem.close()
        return after

    rt = ExitStack()
    lg = sb(rt, "r_logits", [S, CB, E])
    mx8 = sb(rt, "r_top", [S, CB, E])
    ix8 = sb(rt, "r_index", [S, CB, E], U32)
    ixf = sb(rt, "r_index_f", [S, TOPK, CB])
    oh = sb(rt, "r_onehot", [S, TOPK, CB, E])
    oh_b = sb(rt, "r_onehot_sum", [S, CB, E], BF16)
    run_b = sb(rt, "r_running", [S, E], BF16)
    run_f = sb(rt, "r_running_f", [S, E])
    tot_f = sb(rt, "r_chunk_total", [S, E])
    prod = sb(rt, "r_prod", [S, TOPK, CB, E])
    pos = sb(rt, "r_pos", [S, TOPK, CB])
    keep = sb(rt, "r_keep", [S, TOPK, CB])
    dest = sb(rt, "r_dest", [S, TOPK, CB])
    tmp = sb(rt, "r_tmp", [S, TOPK, CB])
    gate_e = sb(rt, "r_gate", [S, 3, CB])
    run0 = dve.put(lambda e: e.memset(run_b[:], 0.0), (), sig("r_run"))
    run0 = dve.put(lambda e: e.memset(run_f[:], 0.0), (), sig("r_run"))
    R = {}

    def zero_slots():
        flat = scratch["xe"].rearrange("n d -> (n d)")
        for at in range(0, SLOTS * D, 128 * 1024):
            k = min(1024, (SLOTS * D - at) // 128)
            R["zero"] = load("zero_slots", flat[at:at + k * 128].rearrange("(p n) -> p n", p=128), t["zero_rows"][:, 0:k])
            yield

    def choose(l):
        yield
        m, bank = misc_bank()
        for b in range(CB):
            mm = pe.put(lambda e, b=b: e.matmul(bank[:, b * E:(b + 1) * E], xnT[:, 1, b * S:(b + 1) * S], wg[:, l, :], start=True, stop=True),
                        [ln[("T", 1)], misc["free"][m]], sig("r_mm"))
        ln[("T_free", 1)] = mm
        a = misc["free"][m] = dve.put(lambda e: e.tensor_copy(lg[:], bank[:, 0:CB * E].rearrange("p (b e) -> p b e", b=CB)), [mm, R.get("lg")], sig("r_v"))
        yield
        for b in range(CB):
            a2 = dve.put(lambda e, b=b: e.max(mx8[:, b, :], lg[:, b, :]), [a, R.get("gate")], sig("r_v"))
        R["top"] = a2
        for b in range(CB):
            a = dve.put(lambda e, b=b: e.max_index(ix8[:, b, :], mx8[:, b, :], lg[:, b, :]), [a2], sig("r_v"))
        yield
        a = dve.put(lambda e: e.tensor_copy(ixf[:], ix8[:, :, 0:TOPK].rearrange("p b k -> p k b")), [a], sig("r_v"))
        for j in range(TOPK):
            R["hot"] = dve.put(lambda e, j=j: e.tensor_tensor(oh[:, j], iota8[:].rearrange("p (o e) -> p o e", o=1).broadcast_to([S, CB, E]),
                                                              ixf[:, j, :].rearrange("p (b o) -> p b o", o=1).broadcast_to([S, CB, E]), ALU.is_equal),
                               [a, weights_in], sig("r_v"))

    def route(c, x_done):
        slot = 1 + c % 2
        yield from layernorm(1, slot, c, x_done)
        yield from choose(0)
        V = lambda fn, after: dve.put(fn, after, sig("r_v"))
        a = V(lambda e: e.tensor_tensor(gate_e[:, 0, :], mx8[:, :, 1], mx8[:, :, 0], ALU.subtract), [R["top"]])
        ex = act.put(lambda e: e.activation(gate_e[:, 1, :], gate_e[:, 0, :], ACT.Exp), [a], sig("r_exp"))
        hot = V(lambda e: e.tensor_tensor(oh_b[:], oh[:, 0], oh[:, 1], ALU.add), [R["hot"]])
        yield
        yield
        m, bank = misc_bank()
        for b in range(CB):
            srcs = [(tri_b, oh_b[:, b, :])] + [(ones_b, oh_b[:, j, :]) for j in range(b)] + [(ones_b, run_b[:, :])]
            for s_, (lhs, rhs) in enumerate(srcs):
                mm = pe.put(lambda e, lhs=lhs, rhs=rhs, b=b, s_=s_, n_=len(srcs): e.matmul(
                    bank[:, b * E:(b + 1) * E], lhs, rhs, start=(s_ == 0), stop=(s_ == n_ - 1)),
                    [hot, run0, misc["free"][m]] + ([R["run"]] if "run" in R else []), sig("r_mm"))
        for j in range(TOPK):
            a = V(lambda e, j=j: e.tensor_tensor(prod[:, j], oh[:, j], bank[:, 0:CB * E].rearrange("p (b e) -> p b e", b=CB), ALU.mult), [mm, hot])
        misc["free"][m] = a
        yield
        yield
        a = V(lambda e: e.tensor_reduce(pos[:], prod[:], AX_X, ALU.add), [a])
        t1 = V(lambda e: e.tensor_reduce(tot_f[:], oh_b[:].rearrange("p b e -> p e b"), AX_X, ALU.add), [run0])
        g = V(lambda e: e.tensor_scalar(gate_e[:, 2, :], gate_e[:, 1, :], 1.0, None, ALU.add), [ex])
        V(lambda e: e.tensor_scalar(keep[:], pos[:], float(CAP), None, ALU.is_lt), [a])
        a = V(lambda e: e.scalar_tensor_tensor(dest[:], ixf[:], float(CAP), pos[:], ALU.mult, ALU.add), [a])
        t1 = V(lambda e: e.tensor_tensor(run_f[:], run_f[:], tot_f[:], ALU.add), [t1])
        g = V(lambda e: e.reciprocal(gate_e[:, 0, :], gate_e[:, 2, :]), [g])
        yield
        sl = slice(c * CB, (c + 1) * CB)
        V(lambda e: e.tensor_scalar(slot_get[:, :, sl], dest[:], float(SLOTS - 1), None, ALU.min), [a])
        a = V(lambda e: e.tensor_scalar(tmp[:], keep[:], -SKIP, SKIP, ALU.mult, ALU.add), [a])
        R["run"] = V(lambda e: e.tensor_copy(run_b[:], run_f[:]), [t1, mm])
        g = V(lambda e: e.tensor_tensor(gate_e[:, 1, :], gate_e[:, 1, :], gate_e[:, 0, :], ALU.mult), [g])
        put = V(lambda e: e.tensor_tensor(slot_put[:, :, sl], dest[:], tmp[:], ALU.add), [a])
        a = V(lambda e: e.tensor_scalar(tmp[:], keep[:], tg_f[:, 0:1], None, ALU.mult), [put])
        for j in range(TOPK):
            R["w"] = V(lambda e, j=j: e.tensor_tensor(slot_w[:, j, sl], gate_e[:, j, :], tmp[:, j, :], ALU.mult), [a, g])
        R["gate"] = R["lg"] = R["w"]
        yield
        late.append(send(c, slot, put))

    def send(c, slot, put):
        for b in range(CB):
            for j in range(TOPK):
                sc = pool.put(lambda e, b=b, j=j: e.indirect_dma_start(
                    scratch["xe"][:, :], bass.IndirectOffsetOnAxis(slot_put[:, j, c * CB + b:c * CB + b + 1], 0),
                    xn[:, slot, b, :], None, bounds_check=SLOTS - 1, oob_is_err=False),
                    [put, R["zero"]], sig(f"scatter{c % 2}"), 16)
                yield
        R["all"] = R.get("all", []) + [sc]
        ln[("rows_free", slot)] = sc

    def bring_x(c):
        if c == 2:
            load_rows(2, NCH)
            clear_ring(2, pool)
        x_ready[c] = rows_in[c]
        yield
        if c == 3:
            yield from zero_slots()

    routes = attention(0, bring_x, route, lambda: None)

    mem = ExitStack()
    w1 = sb(mem, "w1_raw", [D, E, HID0])
    w1h = sb(mem, "w1_high", [D, 2, HID0], F32R)
    w1l = sb(mem, "w1_low", [D, 2, HID0], F32R)
    w2 = sb(mem, "w2", [128, E, HID0 // 128, D])
    b1 = sb(mem, "b1_cols", [128, E, HID0 // 128])
    b2 = sb(mem, "b2_rows", [128, E, D])
    NC0 = HID0 // 128
    GW = 3 * 128
    groups = [(a, min(GW, CAP - a)) for a in range(0, CAP, GW)]
    xe = sb(mem, "xe_rows", [128, 3, 3, D])
    xeh = sb(mem, "xe_T_high", [D, 2, GW], F32R)
    xel = sb(mem, "xe_T_low", [D, 2, GW], F32R)
    hT = qop[:].rearrange("p a b c -> p (a b c)").bitcast(F32)[:, 0:2 * NC0 * GW].rearrange("p (k q n) -> p k q n", k=2, q=NC0)
    yb = sb(mem, "y_rows", [128, 3, 3, D])
    w_in = [None] * E
    consts = load("ld_w2", b1[:], t["b1"])
    consts = load("ld_w2", b2[:], t["b2"].partition_broadcast(128))
    for e_ in range(E):
        if e_ in (0, 1):
            hi = 1 if e_ == 0 else E
            load(f"ld_e{e_}", w1[:, e_:hi], t["w1"][:, e_:hi])
            load(f"ld_e{e_}", w2[:, e_:hi], t["w2"][:, e_:hi])
        w_in[e_] = (sig(f"ld_e{min(e_, 1)}"), 32)
    jobs = [(e_, a, w) for e_ in range(E) for a, w in groups]
    F = {}
    H_BANKS, T_BANKS, Y_BANKS = (0, 1, 2, 3), (4, 5), (6, 7)

    def fetch(n):
        e_, a, w = jobs[n]
        base = e_ * CAP + a
        full_, part_ = divmod(w, 128)
        after = [F.get(("xe", n % 3))] + R["all"]
        if full_:
            F[("in", n)] = load(f"xe_in{n % 3}", xe[:, n % 3, 0:full_, :], scratch["xe"][base:base + full_ * 128, :].rearrange("(s p) d -> p s d", p=128), after)
        if part_:
            F[("in", n)] = load(f"xe_in{n % 3}", xe[0:part_, n % 3, full_, :], scratch["xe"][base + full_ * 128:base + w, :], after)

    def turn(n):
        e_, a, w = jobs[n]
        bank = ps[:, T_BANKS[n % 2], :]
        for s_ in range(-(-w // 128)):
            r_ = min(128, w - 128 * s_)
            mm = pe.put(lambda e, s_=s_, r_=r_: e.transpose(bank[:, s_ * 128:s_ * 128 + r_], xe[0:r_, n % 3, s_, :], ident[0:r_, 0:r_]),
                        [F[("in", n)], F.get(("Tbank", n % 2))], sig("e_T"))
        F[("xe", n % 3)] = mm
        hi = act.put(lambda e: e.copy(xeh[:, n % 2, 0:w], bank[:, 0:w]), [mm, F.get(("xeTfree", n % 2))], sig("e_T_high"))
        F[("xeT", n)] = F[("Tbank", n % 2)] = dve.put(lambda e: e.tensor_tensor(xel[:, n % 2, 0:w], bank[:, 0:w], xeh[:, n % 2, 0:w].bitcast(F32), ALU.subtract),
                                                      [hi], sig("e_T_low"))

    def split_w1(e_):
        a = dve.put(lambda e: e.tensor_copy(w1h[:, e_ % 2], w1[:, e_]), [w_in[e_], F.get(("up", e_ - 2))], sig("e_wh"))
        F[("w1", e_)] = dve.put(lambda e: e.tensor_tensor(w1l[:, e_ % 2], w1[:, e_], w1h[:, e_ % 2].bitcast(F32), ALU.subtract), [a], sig("e_wl"))

    def up(n):
        e_, a, w = jobs[n]
        xh0, xl0 = xeh[:, n % 2, 0:w], xel[:, n % 2, 0:w]
        for q in range(NC0):
            bank = ps[:, H_BANKS[q], 0:w]
            wc = slice(q * 128, (q + 1) * 128)
            pe.put(lambda e, wc=wc, bank=bank: e.matmul(bank, w1h[:, e_ % 2, wc], xh0, start=True, stop=False),
                   [F[("xeT", n)], F[("w1", e_)], F.get(("H", q))])
            pe.put(lambda e, wc=wc, bank=bank: e.matmul(bank, w1h[:, e_ % 2, wc], xl0, start=False, stop=False))
            mm = pe.put(lambda e, wc=wc, bank=bank: e.matmul(bank, w1l[:, e_ % 2, wc], xh0, start=False, stop=True), (), sig("e_up"))
            F[("H", q)] = F[("h", n)] = act.put(lambda e, q=q, bank=bank: e.activation(hT[:, n % 2, q, 0:w], bank, ACT.Gelu_apprx_tanh, bias=b1[:, e_, q:q + 1]),
                                  [mm, consts, F.get(("hfree", n % 2))], sig("e_gelu"))
        F[("xeTfree", n % 2)] = F[("up", e_)] = mm

    def down(n):
        e_, a, w = jobs[n]
        bank = ps[:, Y_BANKS[n % 2], :]
        for s_ in range(-(-w // 128)):
            r_ = min(128, w - 128 * s_)
            for q in range(NC0):
                mm = pe.put(lambda e, s_=s_, r_=r_, q=q: e.matmul(bank[0:r_, s_ * D:(s_ + 1) * D], hT[:, n % 2, q, s_ * 128:s_ * 128 + r_], w2[:, e_, q, :],
                                                                  start=(q == 0), stop=(q == NC0 - 1)),
                            [F[("h", n)], F.get(("Y", n % 2))], sig("e_down") if q == NC0 - 1 else None)
        F[("hfree", n % 2)] = mm
        base = e_ * CAP + a
        full_, part_ = divmod(w, 128)
        y3 = bank[:, 0:3 * D].rearrange("p (s d) -> p s d", s=3)
        if full_:
            a1 = dve.put(lambda e: e.tensor_tensor(yb[:, n % 3, 0:full_, :], y3[:, 0:full_, :], b2[:, e_:e_ + 1, :].broadcast_to([128, full_, D]), ALU.add),
                         [mm, F.get(("y", n % 3))], sig("e_y"))
        if part_:
            a1 = dve.put(lambda e: e.tensor_tensor(yb[0:part_, n % 3, full_, :], y3[0:part_, full_, :], b2[0:part_, e_, :], ALU.add),
                         [mm, F.get(("y", n % 3))], sig("e_y"))
        F[("Y", n % 2)] = a1
        if full_:
            F[("y", n % 3)] = load(f"y_out{n % 3}", scratch["y"][base:base + full_ * 128, :].rearrange("(s p) d -> p s d", p=128), yb[:, n % 3, 0:full_, :], [a1])
        if part_:
            F[("y", n % 3)] = load(f"y_out{n % 3}", scratch["y"][base + full_ * 128:base + w, :], yb[0:part_, n % 3, full_, :], [a1])
        F[("ydone", n % 3)] = F[("y", n % 3)]

    NJ = len(jobs)
    chains = [routes, late]
    while any(chains):
        for chain in chains:
            if chain and next(chain[0], "end") == "end":
                chain.pop(0)
    prep_v(NCH)
    for k in range(2):
        F[("Y", k)] = misc["free"][k]
    split_w1(0)
    fetch(0)
    fetch(1)
    turn(0)
    for n in range(NJ):
        if n % len(groups) == 0 and n // len(groups) + 1 < E:
            split_w1(n // len(groups) + 1)
        if n + 2 < NJ:
            fetch(n + 2)
        if n + 1 < NJ:
            turn(n + 1)
        up(n)
        if n >= 1:
            down(n - 1)
    down(NJ - 1)
    ys = [F[("ydone", k)] for k in range(3)]
    fence((sp,))
    clear_spares()
    mem.close()
    feed_mem = ExitStack()
    got = sb(feed_mem, "got_rows", [128, 4, TOPK, D])
    xh = sb(feed_mem, "xn_T_high", [D, NCH, CT], F32R)
    xl = sb(feed_mem, "xn_T_low", [D, NCH, CT], F32R)
    vbo = sb(feed_mem, "bo_rows1", [S, D])
    comb = sb(feed_mem, "comb", [S, CB, E])
    cw = sb(feed_mem, "comb_work", [S, 4, CB, E])
    csum = sb(feed_mem, "comb_sum", [S, 4, CB])
    combT = sb(feed_mem, "comb_T", [CB * E, 2, S])
    vbo_in = load("ld_bo1", vbo[:], t["f1_bo"].partition_broadcast(S))
    tb = dve.put(lambda e: e.tensor_scalar(vbo[:], vbo[:], tg_f[:, 1:2], None, ALU.mult), [vbo_in], sig("f_bo"))

    def bring_y(c):
        for i in range(c * CB, (c + 1) * CB):
            for j in range(TOPK):
                F[("g", i)] = pool.put(lambda e, i=i, j=j: e.indirect_dma_start(
                    got[:, i % 4, j, :], None, scratch["y"][:, :], bass.IndirectOffsetOnAxis(slot_get[:, j, i:i + 1], 0),
                    bounds_check=SLOTS - 1, oob_is_err=True), ys + [F.get(("got", i % 4)), R["w"]], sig(f"gather{i % 4}"), 16)
                yield
            if i > c * CB:
                add_y(i - 1)
        add_y(c * CB + CB - 1)
        x_ready[NCH + c] = F[("got", (CB - 1) % 4)]

    def add_y(i):
        a = dve.put(lambda e: e.scalar_tensor_tensor(x[:, i, :], got[:, i % 4, 0, :], slot_w[:, 0, i:i + 1], x[:, i, :], ALU.mult, ALU.add), [F[("g", i)]], sig("combine"))
        F[("got", i % 4)] = dve.put(lambda e: e.scalar_tensor_tensor(x[:, i, :], got[:, i % 4, 1, :], slot_w[:, 1, i:i + 1], x[:, i, :], ALU.mult, ALU.add), [a], sig("combine"))

    G = {}

    def weigh(c, x_done):
        yield from layernorm(1, 1 + c % 2, c, x_done)
        hi = act.put(lambda e: e.copy(xh[:, c, :], xnT[:, 1, :]), [ln[("T", 1)]], sig("f_xh"))
        yield from choose(1)
        V = lambda fn, after: dve.put(fn, after, sig("c_v"))
        a = G[("x", c)] = V(lambda e: e.tensor_tensor(xl[:, c, :], xnT[:, 1, :], xh[:, c, :].bitcast(F32), ALU.subtract), [hi])
        ln[("T_free", 1)] = a
        V(lambda e: e.tensor_tensor(cw[:, 0], lg[:], mx8[:, :, 0:1].broadcast_to([S, CB, E]), ALU.subtract), [R["top"], R["hot"]])
        a = R["lg"] = R["gate"] = V(lambda e: e.tensor_tensor(csum[:, 0, :], mx8[:, :, 1], mx8[:, :, 0], ALU.subtract), [G.get("x_b")])
        yield
        yield
        act.put(lambda e: e.activation(cw[:, 1], cw[:, 0], ACT.Exp), [a], sig("c_exp"))
        ex = act.put(lambda e: e.activation(csum[:, 1, :], csum[:, 0, :], ACT.Exp), [a], sig("c_exp"))
        yield
        a = V(lambda e: e.tensor_reduce(csum[:, 2, :], cw[:, 1], AX_X, ALU.add), [ex])
        a = V(lambda e: e.scalar_tensor_tensor(csum[:, 2, :], csum[:, 2, :], EPS_GATE, csum[:, 1, :], ALU.mult, ALU.add), [a])
        a = V(lambda e: e.tensor_scalar(csum[:, 2, :], csum[:, 2, :], 1.0, None, ALU.add), [a])
        a = V(lambda e: e.reciprocal(csum[:, 3, :], csum[:, 2, :]), [a])
        a = V(lambda e: e.tensor_tensor(cw[:, 2], oh[:, 1], csum[:, 1, :].rearrange("p (b o) -> p b o", o=1).broadcast_to([S, CB, E]), ALU.mult), [a])
        a = V(lambda e: e.tensor_tensor(cw[:, 3], cw[:, 2], oh[:, 0], ALU.add), [a])
        a = V(lambda e: e.tensor_tensor(comb[:], cw[:, 3], csum[:, 3, :].rearrange("p (b o) -> p b o", o=1).broadcast_to([S, CB, E]), ALU.mult), [a, G.get("comb_T")])
        yield
        cs = V(lambda e: e.tensor_reduce(csum[:, 0, :], comb[:], AX_X, ALU.add), [a])
        for b in range(CB):
            G["x_b"] = G[("x_b", c)] = V(lambda e, b=b: e.scalar_tensor_tensor(x[:, c * CB + b, :], vbo[:], csum[:, 0, b:b + 1], x[:, c * CB + b, :], ALU.mult, ALU.add),
                                         [cs, ln[("norm", 1)], tb])
        yield
        yield
        m, bank = misc_bank()
        tr = G["comb_T"] = pe.put(lambda e: e.transpose(bank[0:CB * E, 0:S], comb[:].rearrange("p b e -> p (b e)"), ident[:, :]),
                                  [a, misc["free"][m]], sig("c_T"))
        cp = misc["free"][m] = act.put(lambda e: e.copy(combT[:, c % 2, :], bank[0:CB * E, 0:S]), [tr, G.get(("combT", c % 2))], sig("c_T_out"))
        G[("combT", c % 2)] = G[("comb", c)] = load(f"comb_out{c % 2}_", scratch["comb"][c].rearrange("e (b s) -> b e s", b=CB),
                                                    combT[:, c % 2, :], [cp])

    raw, vready = full, {}

    def fetch_weights(e_):
        k = e_ % 2
        vready[e_] = load(f"ld_v{k}", raw[:, k, :], t["f1_w1"][:, e_], [vready.get(e_ - 2), free[("full", k)]])

    def fetch_two():
        fetch_weights(0)
        fetch_weights(1)

    weighs = attention(1, bring_y, weigh, fetch_two)

    mem = ExitStack()
    vh = sb(mem, "w1_T_high", [D, 2, 2 * HID1], F32R)
    vl = sb(mem, "w1_T_low", [D, 2, 2 * HID1], F32R)
    vo = sb(mem, "wo_T", [128, 2, D])
    vb = sb(mem, "b1_cols1", [128, E, 4])
    flat = qop[:].rearrange("p a b c -> p (a b c)").bitcast(F32)
    cb_sb, sg, ga, gw = (flat[:, j * 3 * CT:(j + 1) * 3 * CT].rearrange("p (s n) -> p s n", s=3) for j in range(4))
    flat = kop[:].rearrange("p a b c d -> p (a b c d)").bitcast(F32)
    acc = flat[:, 0:NCH * 2 * CT].rearrange("p (c k n) -> p c k n", c=NCH, k=2)
    for dst, src in ((vb[:], t["f1_b1"]), (vo[:], t["f1_wo"])):
        vin = load("ld_f1", dst, src)

    def split_weights(e_):
        k = e_ % 2
        a = act.put(lambda e: e.copy(vh[:, k], raw[:, k, :]), [vready[e_], G.get(("up", e_ - 2))], sig("f_wh"))
        vready[e_] = dve.put(lambda e: e.tensor_tensor(vl[:, k], raw[:, k, :], vh[:, k].bitcast(F32), ALU.subtract), [a], sig("f_wl"))

    A_BANKS, B_BANKS = (0, 1, 2), (3, 4, 5)
    outs = []

    def up1(bank, c, e_, col, after):
        w = slice(col, col + 128)
        k = e_ % 2
        pe.put(lambda e: e.matmul(bank, vh[:, k, w], xh[:, c, :], start=True, stop=False), after)
        pe.put(lambda e: e.matmul(bank, vh[:, k, w], xl[:, c, :], start=False, stop=False))
        return pe.put(lambda e: e.matmul(bank, vl[:, k, w], xh[:, c, :], start=False, stop=True), (), sig("f_up"))

    def fetch_comb(u):
        e_, c = divmod(u, NCH)
        G[("rows", u)] = load(f"comb_in{u % 3}_", cb_sb[:, u % 3, :], scratch["comb"][c, e_].partition_broadcast(128),
                              [G[("comb", c)], G.get(("cb", u % 3))])

    def expert1(e_, c):
        u3 = (e_ * NCH + c) % 3
        cbm = G[("rows", e_ * NCH + c)]
        for hc in range(2):
            s3 = (2 * (e_ * NCH + c) + hc) % 3
            abank, bbank = ps[:, A_BANKS[s3], :], ps[:, B_BANKS[s3], :]
            mb = up1(bbank, c, e_, HID1 + hc * 128, [G[("x", c)], vready[e_], G.get(("B", s3))])
            G[("B", s3)] = sgm = act.put(lambda e, hc=hc, bbank=bbank, s3=s3: e.activation(sg[:, s3, :], bbank, ACT.Sigmoid, bias=vb[:, e_, 2 + hc:3 + hc]),
                                          [mb, vin, G.get(("sg", s3))], sig("f_sig"))
            ma = G[("up", e_)] = up1(abank, c, e_, hc * 128, [G.get(("A", s3))])
            gm = G[("A", s3)] = G[("sg", s3)] = dve.put(
                lambda e, hc=hc, abank=abank, s3=s3: e.scalar_tensor_tensor(ga[:, s3, :], abank, vb[:, e_, hc:hc + 1], sg[:, s3, :], ALU.add, ALU.mult),
                [ma, sgm, vin, G.get(("ga", s3))], sig("f_gated"))
            flush()
            pending.append((e_, c, hc, s3, u3, gm, cbm))

    pending = []

    def flush():
        if not pending:
            return
        e_, c, hc, s3, u3, gm, cbm = pending.pop()
        line, name = (pool, "f_sum") if e_ == 0 else (dve, "f_weighted")
        to = acc[:, c, hc, :] if e_ == 0 else gw[:, s3, :]
        wm = G[("ga", s3)] = G[("cb", u3)] = G[("acc", c, hc)] = line.put(
            lambda e: e.tensor_tensor(to, ga[:, s3, :], cb_sb[:, u3, :], ALU.mult), [gm, cbm, G.get(("gw", s3)), G.get(("acc", c, hc))], sig(name))
        if e_ > 0:
            G[("gw", s3)] = G[("acc", c, hc)] = pool.put(lambda e: e.tensor_tensor(acc[:, c, hc, :], acc[:, c, hc, :], gw[:, s3, :], ALU.add),
                                                         [wm], sig("f_sum"))

    def down1(c):
        m, bank = misc_bank()
        for b in range(CB):
            for hc in range(2):
                mo = pe.put(lambda e, b=b, hc=hc: e.matmul(bank[:, b * D:(b + 1) * D], acc[:, c, hc, b * S:(b + 1) * S], vo[:, hc, :], start=(hc == 0), stop=(hc == 1)),
                            [G[("acc", c, 0)], G[("acc", c, 1)], vin, misc["free"][m]], sig("f_out"))
        xs = x[:, c * CB:(c + 1) * CB, :]
        fin = misc["free"][m] = dve.put(lambda e: e.scalar_tensor_tensor(xs, bank.rearrange("p (b d) -> p b d", b=CB), tg_f[:, 1:2], xs, ALU.mult, ALU.add),
                                        [mo, G[("x_b", c)]], sig("f_x"))
        outs.append(load("out", out[:, c * CB:(c + 1) * CB, :], xs, [fin]))

    split_weights(0)
    split_weights(1)
    for e_ in range(E):
        for c in range(NCH):
            for _ in range(3):
                if weighs and next(weighs[0], "end") == "end":
                    weighs.pop(0)
            while ("comb", c) not in G:
                if next(weighs[0], "end") == "end":
                    weighs.pop(0)
            u = e_ * NCH + c
            for v in (u, u + 1):
                if ("rows", v) not in G and v < E * NCH and ("comb", v % NCH) in G:
                    fetch_comb(v)
            expert1(e_, c)
            if c == 0 and 1 <= e_ < E - 1:
                fetch_weights(e_ + 1)
            if c == 4 and 1 <= e_ < E - 1:
                split_weights(e_ + 1)
            if e_ == E - 1 and c > 1:
                down1(c - 2)
    flush()
    down1(NCH - 2)
    down1(NCH - 1)
    sp.put(None, [outs[-1]])
    fence()

    with nc.Block() as block:
        block.tensor(pe.play)
        block.scalar(act.play)
        block.vector(dve.play)
        block.gpsimd(pool.play)
        block.sync(sp.play)
    mem.close()
    feed_mem.close()
    rt.close()
    top.close()


def kernel(**inputs):
    import numpy as np
    import concourse.bacc as bacc
    from concourse import mybir as mb
    from concourse.bass_utils import run_bass_kernel_spmd

    a = {k: np.asarray(v) for k, v in inputs.items()}
    c = np.ascontiguousarray
    import ml_dtypes
    bf = ml_dtypes.bfloat16
    f = np.float32
    eye = np.eye(128)
    arrays = {
        "x": c(a["x"].transpose(1, 0, 2)),
        "ctxT": c(a["ctx_1024"].reshape(B * S2, D).T),
        "groupT": c(a["fside_BxSxS2_0"].transpose(2, 0, 1)),
        "mask0": c(a["mask_BxSxS2_ik1"].transpose(1, 0, 2)),
        "mask0T": c(a["mask_BxSxS2_ik1"].transpose(2, 0, 1)),
        "mask1": c(a["mask_1x1xSxS2_bk1"][0, 0]),
        "mask1T": c(a["mask_1x1xSxS2_bk1"][0, 0].T),
        "wq": c(np.stack([a["L0_xattn_wq_k"], a["L1_xattn_w_q"].T], 1)),
        "wk": c(np.stack([a["L0_xattn_wk_k"], a["L1_xattn_w_k"].T], 1)),
        "wv": c(np.stack([a["L0_xattn_wv_k"], a["L1_xattn_w_v"].T], 1)),
        "wo": c(np.stack([a["L0_xattn_wo_k"], a["L1_xattn_w_o"].T], 1)),
        "cols": c(np.stack([a["L0_xattn_wq_b"], a["L0_xattn_wk_b"], a["L1_xattn_b_q"], a["L1_xattn_b_k"]], 1)),
        "bv": c(np.stack([a["L0_xattn_wv_b"], a["L1_xattn_b_v"]])),
        "bo": c(np.stack([a["L0_xattn_wo_b"], a["L1_xattn_b_o"]])),
        "g": c(np.concatenate([a["g_xattn"], a["g_ffn"]])),
        "wg": c(np.stack([a["L0_ffn_Wg"], a["L1_ffn_Wg"].T], 1)),
        "w1": c(a["L0_ffn_W1"].transpose(1, 0, 2)),
        "b1": c(a["L0_ffn_b1"].reshape(E, HID0 // 128, 128).transpose(2, 0, 1)),
        "w2": c(a["L0_ffn_W2"].reshape(E, HID0 // 128, 128, D).transpose(2, 0, 1, 3)),
        "b2": c(a["L0_ffn_b2"]),
        "f1_w1": c(a["L1_ffn_W1"].transpose(2, 0, 1)),
        "f1_b1": c(a["L1_ffn_b1"].reshape(E, 4, 128).transpose(2, 0, 1)),
        "f1_wo": c(a["L1_ffn_Wo"].T.reshape(2, 128, D).transpose(1, 0, 2)),
        "f1_bo": c(a["L1_ffn_bo"]),
        "ident": eye.astype(f),
        "cbf": c(np.concatenate([eye, np.triu(np.ones((128, 128)), 1), np.ones((128, 128))], 1)).astype(bf),
        "iota8": c(np.tile(np.arange(E), (128, 1))).astype(f),
        "ones": np.ones((3, PAIRS, CK)).astype(bf),
        "zeros": np.zeros((SPARE, PAIRS, CT)).astype(bf),
        "zero_rows": np.zeros((128, 1024), f),
    }
    nc = bacc.Bacc("TRN2", target_bir_lowering=False, num_devices=1)
    t = {k: nc.dram_tensor(f"in_{k}", v.shape, mb.dt.from_np(v.dtype), kind="ExternalInput").ap() for k, v in arrays.items()}
    out = nc.dram_tensor("out_x", (S, B, D), F32, kind="ExternalOutput").ap()
    scratch = {
        "q": nc.dram_tensor("scratch_q", (NCH, D, 6, CT), BF16, kind="Internal").ap(),
        "k": nc.dram_tensor("scratch_k", (NCH, D, 6, CK), BF16, kind="Internal").ap(),
        "shift": nc.dram_tensor("scratch_shift", (B, 3 * H, S), BF16, kind="Internal").ap(),
        "xe": nc.dram_tensor("scratch_xe", (SLOTS, D), F32, kind="Internal").ap(),
        "comb": nc.dram_tensor("scratch_comb", (NCH, E, CT), F32, kind="Internal").ap(),
        "y": nc.dram_tensor("scratch_y", (SLOTS, D), F32, kind="Internal").ap(),
    }
    flamingo(nc, t, out, scratch)
    r = run_bass_kernel_spmd(nc, [{f"in_{k}": v for k, v in arrays.items()}], core_ids=[0])
    return c(r.results[0]["out_x"].transpose(1, 0, 2))
```
